# Optimizing a Trainium2 kernel written in Bass

```python
import numpy as np
import jax
import jax.numpy as jnp

def _softmax(x, axis=-1):
    return jax.nn.softmax(x, axis=axis)

def _gelu(x):
    return jax.nn.gelu(x, approximate=True)

def _silu(x):
    return jax.nn.silu(x)

def _sigmoid(x):
    return jax.nn.sigmoid(x)

def _layernorm(x, axis=-1, eps=1e-05):
    m = jnp.mean(x, axis=axis, keepdims=True)
    v = jnp.var(x, axis=axis, keepdims=True)
    return (x - m) / jnp.sqrt(v + eps)

def _scatter_add(tgt, idx, src, axis=0):
    return tgt.at[idx].add(src)

def _segment_sum(src, seg, n):
    return jax.ops.segment_sum(src, seg, n)
kernel_name = 'mk_xattn_ffn_d2_seqx_r8_79aa1a'

def setup_inputs(seed: int=0):
    np.random.seed(seed)
    _w = jnp.asarray

    def _rec_inputs():
        import jax
        import jax.numpy as jnp
        _rk = jax.random.key(seed)
        x = -0.0002928 + 1 * jax.random.normal(jax.random.fold_in(_rk, 1), (32, 128, 128), jnp.float32)
        _lenS = 128 - jax.random.randint(jax.random.fold_in(_rk, 7), (32,), 0, max(1, 128 // 4) + 1, jnp.int32)
        _lenS2 = 128 - jax.random.randint(jax.random.fold_in(_rk, 8), (32,), 0, max(1, 128 // 4) + 1, jnp.int32)
        _ctx_1024P = jax.random.normal(jax.random.fold_in(_rk, 11), (32, 16, 128), jnp.float32)
        _ctx_1024c = jax.random.dirichlet(jax.random.fold_in(_rk, 511), 0.3 * jnp.ones((16,), jnp.float32), (32, 128))
        _ctx_1024t = jnp.einsum('bsk,bkd->bsd', _ctx_1024c, _ctx_1024P)
        _ctx_1024t = _ctx_1024t * jax.lax.rsqrt(jnp.mean(jnp.square(_ctx_1024t)) + 1e-12) * 0.953939
        ctx_1024 = -1.39393e-06 + 0.999914 * (_ctx_1024t + 0.3 * jax.random.normal(jax.random.fold_in(_rk, 611), (32, 128, 128), jnp.float32))
        _validS = jnp.arange(128)[None, :] < _lenS[:, None]
        _validS2 = jnp.arange(128)[None, :] < _lenS2[:, None]
        _causal = jnp.tril(jnp.ones((128, 128), dtype=bool))
        mask_Bx1xSxS2_ik0 = jnp.where(jnp.broadcast_to(_validS2[:, None, None, :], (32, 1, 128, 128)), 0, 1).astype(jnp.int32)
        return (x, ctx_1024, mask_Bx1xSxS2_ik0)
    x, ctx_1024, mask_Bx1xSxS2_ik0 = _rec_inputs()

    def _L0_xattn_setup():
        import jax, jax.numpy as jnp
        import numpy as np
        D_MODEL = 128
        NUM_HEADS = 16
        HEAD_DIM = D_MODEL // NUM_HEADS
        SCALE = HEAD_DIM ** (-0.5)
        BIAS_LEN = 128
        ROPE_BASE = 10000.0
        LN_EPS = 1e-05

        def _layernorm(x, gamma, beta):
            mu = jnp.mean(x, axis=-1, keepdims=True)
            var = jnp.mean(jnp.square(x - mu), axis=-1, keepdims=True)
            return (x - mu) * jax.lax.rsqrt(var + LN_EPS) * gamma + beta

        def _rope(x, cos, sin):
            half = HEAD_DIM // 2
            c = cos[None, None, :, :]
            s = sin[None, None, :, :]
            x_even, x_odd = (x[..., :half], x[..., half:])
            return jnp.concatenate([x_even * c - x_odd * s, x_even * s + x_odd * c], axis=-1)

        def _temporal_bias(L_q, L_kv):
            pos = jnp.arange(BIAS_LEN, dtype=jnp.float32)
            dist = jnp.abs(pos[None, :] - pos[:, None])
            bias = jnp.exp(-dist * 0.1) - dist * 0.05
            if L_q <= BIAS_LEN and L_kv <= BIAS_LEN:
                return bias[:L_q, :L_kv]
            return jax.image.resize(bias, (L_q, L_kv), method='bilinear')
        key = jax.random.key(seed)
        ks = jax.random.split(key, 8)
        B, Lq, Lkv = (8, 64, 64)
        return {'decoder_hidden': jax.random.normal(ks[0], (B, Lq, D_MODEL), jnp.float32), 'encoder_output': jax.random.normal(ks[1], (B, Lkv, D_MODEL), jnp.float32), 'Wqkv': jax.random.normal(ks[2], (3 * D_MODEL, D_MODEL), jnp.float32) * 0.02, 'Wout': jax.random.normal(ks[3], (D_MODEL, D_MODEL), jnp.float32) * 0.02, 'b_out': jnp.zeros((D_MODEL,), jnp.float32), 'Wgate': jax.random.normal(ks[4], (D_MODEL, D_MODEL), jnp.float32) * 0.02, 'b_gate': jnp.zeros((D_MODEL,), jnp.float32), 'gamma': jnp.ones((D_MODEL,), jnp.float32), 'beta': jnp.zeros((D_MODEL,), jnp.float32)}
    _L0_xattn_all = _L0_xattn_setup()
    _L0_xattn_in = {k: v for k, v in _L0_xattn_all.items() if k in ('Wqkv', 'Wout', 'b_out', 'Wgate', 'b_gate', 'gamma', 'beta')}
    del _L0_xattn_all

    def _L0_ffn_setup():
        import jax, jax.numpy as jnp
        import numpy as np
        DIM = 128
        DEPTH = 2
        HEADS = 8
        DIM_HEAD = 64
        WINDOW = 64
        INNER = HEADS * DIM_HEAD
        HID = int(DIM * 4 * 2 / 3)
        B, N = (2, 1024)
        QK_SCALE = 8.0

        def shift_token(t):
            t1, t2 = jnp.split(t, 2, axis=-1)
            t2 = jnp.pad(t2, ((0, 0), (1, 0), (0, 0)))[:, :-1]
            return jnp.concatenate([t1, t2], axis=-1)

        def l2norm(t):
            return t / jnp.clip(jnp.linalg.norm(t, axis=-1, keepdims=True), 1e-12)

        def rotate_half(x):
            x1, x2 = jnp.split(x, 2, axis=-1)
            return jnp.concatenate([-x2, x1], axis=-1)

        def rotary_xpos(q, k):
            n = q.shape[-2]
            half_idx = jnp.arange(0, DIM_HEAD, 2, dtype=jnp.float32)
            inv_freq = 1.0 / 10000.0 ** (half_idx / DIM_HEAD)
            t = jnp.arange(n, dtype=jnp.float32)
            freqs = t[:, None] * inv_freq[None, :]
            freqs = jnp.concatenate([freqs, freqs], axis=-1)
            base = (half_idx + 0.4 * DIM_HEAD) / (1.4 * DIM_HEAD)
            power = (t - n // 2) / float(WINDOW // 2)
            scale = base[None, :] ** power[:, None]
            scale = jnp.concatenate([scale, scale], axis=-1)
            cos, sin = (jnp.cos(freqs), jnp.sin(freqs))
            q = q * cos * scale + rotate_half(q) * sin * scale
            k = k * cos / scale + rotate_half(k) * sin / scale
            return (q, k)

        def local_attention(q, k, v):
            b, h, n, d = q.shape
            w = n // WINDOW
            bq = q.reshape(b, h, w, WINDOW, d) * QK_SCALE
            bk = k.reshape(b, h, w, WINDOW, d)
            bv = v.reshape(b, h, w, WINDOW, d)

            def look_around(t):
                p = jnp.pad(t, ((0, 0), (0, 0), (1, 0), (0, 0), (0, 0)))
                return jnp.concatenate([p[:, :, :w], p[:, :, 1:]], axis=3)
            bk, bv = (look_around(bk), look_around(bv))
            bt = jnp.arange(n).reshape(w, WINDOW)
            btp = jnp.pad(bt, ((1, 0), (0, 0)), constant_values=-1)
            btk = jnp.concatenate([btp[:w], btp[1:]], axis=1)
            sim = jnp.einsum('bhwid,bhwjd->bhwij', bq, bk)
            i = bt[:, :, None]
            j = btk[:, None, :]
            mask = (i < j) | (i > j + WINDOW) | (j == -1)
            sim = jnp.where(mask, -jnp.finfo(sim.dtype).max, sim)
            attn = jax.nn.softmax(sim, axis=-1)
            out = jnp.einsum('bhwij,bhwjd->bhwid', attn, bv)
            return out.reshape(b, h, n, d)

        def _layer(x, wqkv, qs, ksc, wo, lg, lb, w1, b1, w2, b2):
            b, n, _ = x.shape
            h = shift_token(x)
            qkv = h @ wqkv
            q, k, v = jnp.split(qkv, 3, axis=-1)
            to_heads = lambda t: t.reshape(b, n, HEADS, DIM_HEAD).transpose(0, 2, 1, 3)
            q, k, v = (to_heads(q), to_heads(k), to_heads(v))
            q = l2norm(q) * qs
            k = l2norm(k) * ksc
            q, k = rotary_xpos(q, k)
            o = local_attention(q, k, v)
            o = o.transpose(0, 2, 1, 3).reshape(b, n, INNER)
            x = x + o @ wo
            h = shift_token(x)
            mu = h.mean(-1, keepdims=True)
            var = h.var(-1, keepdims=True)
            h = (h - mu) / jnp.sqrt(var + 1e-05) * lg + lb
            h = h @ w1 + b1
            a, g = jnp.split(h, 2, axis=-1)
            h = a * jax.nn.gelu(g, approximate=False)
            x = x + h @ w2 + b2
            return x
        key = jax.random.key(seed)
        ks = jax.random.split(key, 6)
        return {'x': jax.random.normal(ks[0], (B, N, DIM), jnp.float32), 'wqkv': jax.random.normal(ks[1], (DEPTH, DIM, 3 * INNER), jnp.float32) * 0.02, 'q_scale': jnp.ones((DEPTH, DIM_HEAD), jnp.float32), 'k_scale': jnp.ones((DEPTH, DIM_HEAD), jnp.float32), 'wo': jax.random.normal(ks[2], (DEPTH, INNER, DIM), jnp.float32) * 0.02, 'ln_g': jnp.ones((DEPTH, DIM), jnp.float32), 'ln_b': jnp.zeros((DEPTH, DIM), jnp.float32), 'w1': jax.random.normal(ks[3], (DEPTH, DIM, 2 * HID), jnp.float32) * 0.02, 'b1': jnp.zeros((DEPTH, 2 * HID), jnp.float32), 'w2': jax.random.normal(ks[4], (DEPTH, HID, DIM), jnp.float32) * 0.02, 'b2': jnp.zeros((DEPTH, DIM), jnp.float32)}
    _L0_ffn_all = _L0_ffn_setup()
    _L0_ffn_in = {k: v for k, v in _L0_ffn_all.items() if k in ('wqkv', 'q_scale', 'k_scale', 'wo', 'ln_g', 'ln_b', 'w1', 'b1', 'w2', 'b2')}
    del _L0_ffn_all

    def _L1_xattn_setup():
        import jax, jax.numpy as jnp
        import numpy as np
        import math
        B, S, D, H = (2, 256, 128, 16)
        DK = D // H

        def _split_heads(x):
            b, s, _ = x.shape
            return x.reshape(b, s, H, DK).transpose(0, 2, 1, 3)
        key = jax.random.key(seed)
        ks = jax.random.split(key, 12)

        def xavier(k, shape):
            fan_in, fan_out = (shape[1], shape[0])
            limit = math.sqrt(6.0 / (fan_in + fan_out))
            return jax.random.uniform(k, shape, jnp.float32, -limit, limit)
        inp = {'query': jax.random.normal(ks[0], (B, S, D), jnp.float32), 'key': jax.random.normal(ks[1], (B, S, D), jnp.float32), 'value': jax.random.normal(ks[2], (B, S, D), jnp.float32), 'mask': jnp.broadcast_to(jnp.tril(jnp.ones((S, S), jnp.int32)), (B, 1, S, S)), 'Wq': xavier(ks[3], (D, D)), 'bq': jnp.zeros((D,), jnp.float32), 'Wk': xavier(ks[4], (D, D)), 'bk': jnp.zeros((D,), jnp.float32), 'Wv': xavier(ks[5], (D, D)), 'bv': jnp.zeros((D,), jnp.float32), 'Wo': xavier(ks[6], (D, D)), 'bo': jnp.zeros((D,), jnp.float32)}
        return inp
    _L1_xattn_all = _L1_xattn_setup()
    _L1_xattn_in = {k: v for k, v in _L1_xattn_all.items() if k in ('Wq', 'bq', 'Wk', 'bk', 'Wv', 'bv', 'Wo', 'bo')}
    del _L1_xattn_all

    def _L1_ffn_setup():
        import jax, jax.numpy as jnp
        import numpy as np
        D, FF, E, K = (128, 128, 8, 2)
        B, S = (4, 128)

        def _gelu(x):
            return jax.nn.gelu(x, approximate=False)
        key = jax.random.key(seed)
        ks = jax.random.split(key, 12)
        s = 0.02
        return {'x': jax.random.normal(ks[0], (B, S, D), jnp.float32), 'gate_w': jax.random.normal(ks[1], (D, E), jnp.float32) * s, 'gate_b': jnp.zeros((E,), jnp.float32), 'sw1': jax.random.normal(ks[2], (D, FF), jnp.float32) * s, 'sb1': jnp.zeros((FF,), jnp.float32), 'sw2': jax.random.normal(ks[3], (FF, D), jnp.float32) * s, 'sb2': jnp.zeros((D,), jnp.float32), 'w1': jax.random.normal(ks[4], (E, D, FF), jnp.float32) * s, 'b1': jnp.zeros((E, FF), jnp.float32), 'w2': jax.random.normal(ks[5], (E, FF, D), jnp.float32) * s, 'b2': jnp.zeros((E, D), jnp.float32)}
    _L1_ffn_all = _L1_ffn_setup()
    _L1_ffn_in = {k: v for k, v in _L1_ffn_all.items() if k in ('gate_w', 'gate_b', 'sw1', 'sb1', 'sw2', 'sb2', 'w1', 'b1', 'w2', 'b2')}
    del _L1_ffn_all
    return {'x': x, 'ctx_1024': ctx_1024, 'mask_Bx1xSxS2_ik0': mask_Bx1xSxS2_ik0, 'L0_xattn_Wqkv': _L0_xattn_in['Wqkv'], 'L0_xattn_Wout': _L0_xattn_in['Wout'], 'L0_xattn_b_out': _L0_xattn_in['b_out'], 'L0_xattn_Wgate': _L0_xattn_in['Wgate'], 'L0_xattn_b_gate': _L0_xattn_in['b_gate'], 'L0_xattn_gamma': _L0_xattn_in['gamma'], 'L0_xattn_beta': _L0_xattn_in['beta'], 'L0_ffn_wqkv': _L0_ffn_in['wqkv'], 'L0_ffn_q_scale': _L0_ffn_in['q_scale'], 'L0_ffn_k_scale': _L0_ffn_in['k_scale'], 'L0_ffn_wo': _L0_ffn_in['wo'], 'L0_ffn_ln_g': _L0_ffn_in['ln_g'], 'L0_ffn_ln_b': _L0_ffn_in['ln_b'], 'L0_ffn_w1': _L0_ffn_in['w1'], 'L0_ffn_b1': _L0_ffn_in['b1'], 'L0_ffn_w2': _L0_ffn_in['w2'], 'L0_ffn_b2': _L0_ffn_in['b2'], 'L1_xattn_Wq': _L1_xattn_in['Wq'], 'L1_xattn_bq': _L1_xattn_in['bq'], 'L1_xattn_Wk': _L1_xattn_in['Wk'], 'L1_xattn_bk': _L1_xattn_in['bk'], 'L1_xattn_Wv': _L1_xattn_in['Wv'], 'L1_xattn_bv': _L1_xattn_in['bv'], 'L1_xattn_Wo': _L1_xattn_in['Wo'], 'L1_xattn_bo': _L1_xattn_in['bo'], 'L1_ffn_gate_w': _L1_ffn_in['gate_w'], 'L1_ffn_gate_b': _L1_ffn_in['gate_b'], 'L1_ffn_sw1': _L1_ffn_in['sw1'], 'L1_ffn_sb1': _L1_ffn_in['sb1'], 'L1_ffn_sw2': _L1_ffn_in['sw2'], 'L1_ffn_sb2': _L1_ffn_in['sb2'], 'L1_ffn_w1': _L1_ffn_in['w1'], 'L1_ffn_b1': _L1_ffn_in['b1'], 'L1_ffn_w2': _L1_ffn_in['w2'], 'L1_ffn_b2': _L1_ffn_in['b2']}

def reference(x, ctx_1024, mask_Bx1xSxS2_ik0, L0_xattn_Wqkv, L0_xattn_Wout, L0_xattn_b_out, L0_xattn_Wgate, L0_xattn_b_gate, L0_xattn_gamma, L0_xattn_beta, L0_ffn_wqkv, L0_ffn_q_scale, L0_ffn_k_scale, L0_ffn_wo, L0_ffn_ln_g, L0_ffn_ln_b, L0_ffn_w1, L0_ffn_b1, L0_ffn_w2, L0_ffn_b2, L1_xattn_Wq, L1_xattn_bq, L1_xattn_Wk, L1_xattn_bk, L1_xattn_Wv, L1_xattn_bv, L1_xattn_Wo, L1_xattn_bo, L1_ffn_gate_w, L1_ffn_gate_b, L1_ffn_sw1, L1_ffn_sb1, L1_ffn_sw2, L1_ffn_sb2, L1_ffn_w1, L1_ffn_b1, L1_ffn_w2, L1_ffn_b2):
    import jax
    import jax.numpy as jnp

    def _L0_xattn_ref(decoder_hidden, encoder_output, Wqkv, Wout, b_out, Wgate, b_gate, gamma, beta):
        import jax, jax.numpy as jnp
        import numpy as np
        D_MODEL = 128
        NUM_HEADS = 16
        HEAD_DIM = D_MODEL // NUM_HEADS
        SCALE = HEAD_DIM ** (-0.5)
        BIAS_LEN = 128
        ROPE_BASE = 10000.0
        LN_EPS = 1e-05

        def _layernorm(x, gamma, beta):
            mu = jnp.mean(x, axis=-1, keepdims=True)
            var = jnp.mean(jnp.square(x - mu), axis=-1, keepdims=True)
            return (x - mu) * jax.lax.rsqrt(var + LN_EPS) * gamma + beta

        def _rope(x, cos, sin):
            half = HEAD_DIM // 2
            c = cos[None, None, :, :]
            s = sin[None, None, :, :]
            x_even, x_odd = (x[..., :half], x[..., half:])
            return jnp.concatenate([x_even * c - x_odd * s, x_even * s + x_odd * c], axis=-1)

        def _temporal_bias(L_q, L_kv):
            pos = jnp.arange(BIAS_LEN, dtype=jnp.float32)
            dist = jnp.abs(pos[None, :] - pos[:, None])
            bias = jnp.exp(-dist * 0.1) - dist * 0.05
            if L_q <= BIAS_LEN and L_kv <= BIAS_LEN:
                return bias[:L_q, :L_kv]
            return jax.image.resize(bias, (L_q, L_kv), method='bilinear')
        B, L_q, _ = decoder_hidden.shape
        L_kv = encoder_output.shape[1]
        residual = decoder_hidden
        q_in = _layernorm(decoder_hidden, gamma, beta)
        kv_in = _layernorm(encoder_output, gamma, beta)
        q = q_in @ Wqkv[:D_MODEL].T
        k = kv_in @ Wqkv[D_MODEL:2 * D_MODEL].T
        v = kv_in @ Wqkv[2 * D_MODEL:].T
        q = q.reshape(B, L_q, NUM_HEADS, HEAD_DIM).transpose(0, 2, 1, 3)
        k = k.reshape(B, L_kv, NUM_HEADS, HEAD_DIM).transpose(0, 2, 1, 3)
        v = v.reshape(B, L_kv, NUM_HEADS, HEAD_DIM).transpose(0, 2, 1, 3)
        L = max(L_q, L_kv)
        inv_freq = 1.0 / ROPE_BASE ** (jnp.arange(0, HEAD_DIM, 2, dtype=jnp.float32) / HEAD_DIM)
        freqs = jnp.arange(L, dtype=jnp.float32)[:, None] * inv_freq[None, :]
        cos, sin = (jnp.cos(freqs), jnp.sin(freqs))
        q = _rope(q, cos[:L_q], sin[:L_q])
        k = _rope(k, cos[:L_kv], sin[:L_kv])
        scores = jnp.einsum('bhqd,bhkd->bhqk', q, k) * SCALE
        scores = scores + _temporal_bias(L_q, L_kv)[None, None, :, :]
        attn = jax.nn.softmax(scores, axis=-1)
        attended = jnp.einsum('bhqk,bhkd->bhqd', attn, v)
        attended = attended.transpose(0, 2, 1, 3).reshape(B, L_q, D_MODEL)
        attended = attended @ Wout.T + b_out
        gate = jax.nn.sigmoid(attended @ Wgate.T + b_gate)
        output = gate * attended + (1.0 - gate) * residual
        return output

    def _L0_ffn_ref(x, wqkv, q_scale, k_scale, wo, ln_g, ln_b, w1, b1, w2, b2):
        import jax, jax.numpy as jnp
        import numpy as np
        DIM = 128
        DEPTH = 2
        HEADS = 8
        DIM_HEAD = 64
        WINDOW = 64
        INNER = HEADS * DIM_HEAD
        HID = int(DIM * 4 * 2 / 3)
        B, N = (2, 1024)
        QK_SCALE = 8.0

        def shift_token(t):
            t1, t2 = jnp.split(t, 2, axis=-1)
            t2 = jnp.pad(t2, ((0, 0), (1, 0), (0, 0)))[:, :-1]
            return jnp.concatenate([t1, t2], axis=-1)

        def l2norm(t):
            return t / jnp.clip(jnp.linalg.norm(t, axis=-1, keepdims=True), 1e-12)

        def rotate_half(x):
            x1, x2 = jnp.split(x, 2, axis=-1)
            return jnp.concatenate([-x2, x1], axis=-1)

        def rotary_xpos(q, k):
            n = q.shape[-2]
            half_idx = jnp.arange(0, DIM_HEAD, 2, dtype=jnp.float32)
            inv_freq = 1.0 / 10000.0 ** (half_idx / DIM_HEAD)
            t = jnp.arange(n, dtype=jnp.float32)
            freqs = t[:, None] * inv_freq[None, :]
            freqs = jnp.concatenate([freqs, freqs], axis=-1)
            base = (half_idx + 0.4 * DIM_HEAD) / (1.4 * DIM_HEAD)
            power = (t - n // 2) / float(WINDOW // 2)
            scale = base[None, :] ** power[:, None]
            scale = jnp.concatenate([scale, scale], axis=-1)
            cos, sin = (jnp.cos(freqs), jnp.sin(freqs))
            q = q * cos * scale + rotate_half(q) * sin * scale
            k = k * cos / scale + rotate_half(k) * sin / scale
            return (q, k)

        def local_attention(q, k, v):
            b, h, n, d = q.shape
            w = n // WINDOW
            bq = q.reshape(b, h, w, WINDOW, d) * QK_SCALE
            bk = k.reshape(b, h, w, WINDOW, d)
            bv = v.reshape(b, h, w, WINDOW, d)

            def look_around(t):
                p = jnp.pad(t, ((0, 0), (0, 0), (1, 0), (0, 0), (0, 0)))
                return jnp.concatenate([p[:, :, :w], p[:, :, 1:]], axis=3)
            bk, bv = (look_around(bk), look_around(bv))
            bt = jnp.arange(n).reshape(w, WINDOW)
            btp = jnp.pad(bt, ((1, 0), (0, 0)), constant_values=-1)
            btk = jnp.concatenate([btp[:w], btp[1:]], axis=1)
            sim = jnp.einsum('bhwid,bhwjd->bhwij', bq, bk)
            i = bt[:, :, None]
            j = btk[:, None, :]
            mask = (i < j) | (i > j + WINDOW) | (j == -1)
            sim = jnp.where(mask, -jnp.finfo(sim.dtype).max, sim)
            attn = jax.nn.softmax(sim, axis=-1)
            out = jnp.einsum('bhwij,bhwjd->bhwid', attn, bv)
            return out.reshape(b, h, n, d)

        def _layer(x, wqkv, qs, ksc, wo, lg, lb, w1, b1, w2, b2):
            b, n, _ = x.shape
            h = shift_token(x)
            qkv = h @ wqkv
            q, k, v = jnp.split(qkv, 3, axis=-1)
            to_heads = lambda t: t.reshape(b, n, HEADS, DIM_HEAD).transpose(0, 2, 1, 3)
            q, k, v = (to_heads(q), to_heads(k), to_heads(v))
            q = l2norm(q) * qs
            k = l2norm(k) * ksc
            q, k = rotary_xpos(q, k)
            o = local_attention(q, k, v)
            o = o.transpose(0, 2, 1, 3).reshape(b, n, INNER)
            x = x + o @ wo
            h = shift_token(x)
            mu = h.mean(-1, keepdims=True)
            var = h.var(-1, keepdims=True)
            h = (h - mu) / jnp.sqrt(var + 1e-05) * lg + lb
            h = h @ w1 + b1
            a, g = jnp.split(h, 2, axis=-1)
            h = a * jax.nn.gelu(g, approximate=False)
            x = x + h @ w2 + b2
            return x
        for l in range(DEPTH):
            x = _layer(x, wqkv[l], q_scale[l], k_scale[l], wo[l], ln_g[l], ln_b[l], w1[l], b1[l], w2[l], b2[l])
        return x

    def _L1_xattn_ref(query, key, value, mask, Wq, bq, Wk, bk, Wv, bv, Wo, bo):
        import jax, jax.numpy as jnp
        import numpy as np
        import math
        B, S, D, H = (2, 256, 128, 16)
        DK = D // H

        def _split_heads(x):
            b, s, _ = x.shape
            return x.reshape(b, s, H, DK).transpose(0, 2, 1, 3)
        Q = _split_heads(query @ Wq.T + bq)
        K = _split_heads(key @ Wk.T + bk)
        V = _split_heads(value @ Wv.T + bv)
        scores = jnp.einsum('bhqd,bhkd->bhqk', Q, K) / math.sqrt(DK)
        scores = jnp.where(mask == 0, jnp.float32(-1000000000.0), scores)
        attn = jax.nn.softmax(scores, axis=-1)
        out = jnp.einsum('bhqk,bhkd->bhqd', attn, V)
        out = out.transpose(0, 2, 1, 3).reshape(query.shape[0], query.shape[1], D)
        return out @ Wo.T + bo

    def _L1_ffn_ref(x, gate_w, gate_b, sw1, sb1, sw2, sb2, w1, b1, w2, b2):
        import jax, jax.numpy as jnp
        import numpy as np
        D, FF, E, K = (128, 128, 8, 2)
        B, S = (4, 128)

        def _gelu(x):
            return jax.nn.gelu(x, approximate=False)
        Bb, Ss, Dm = x.shape
        t = x.reshape(-1, Dm)
        T = t.shape[0]
        shared = _gelu(t @ sw1 + sb1) @ sw2 + sb2
        probs = jax.nn.softmax(t @ gate_w + gate_b, axis=-1)
        topk_p, topk_i = jax.lax.top_k(probs, K)
        combine = jnp.zeros((T, E), t.dtype).at[jnp.arange(T)[:, None], topk_i].set(topk_p)
        h = _gelu(jnp.einsum('td,edf->etf', t, w1) + b1[:, None, :])
        y = jnp.einsum('etf,efd->etd', h, w2) + b2[:, None, :]
        routed = jnp.einsum('te,etd->td', combine, y)
        return (routed + shared).reshape(Bb, Ss, Dm)
    x = x + _L0_xattn_ref(_layernorm(x, axis=-1), ctx_1024, L0_xattn_Wqkv, L0_xattn_Wout, L0_xattn_b_out, L0_xattn_Wgate, L0_xattn_b_gate, L0_xattn_gamma, L0_xattn_beta)
    x = x + _L0_ffn_ref(_layernorm(x, axis=-1), L0_ffn_wqkv, L0_ffn_q_scale, L0_ffn_k_scale, L0_ffn_wo, L0_ffn_ln_g, L0_ffn_ln_b, L0_ffn_w1, L0_ffn_b1, L0_ffn_w2, L0_ffn_b2)
    x = x + _L1_xattn_ref(_layernorm(x, axis=-1), ctx_1024, ctx_1024, mask_Bx1xSxS2_ik0, L1_xattn_Wq, L1_xattn_bq, L1_xattn_Wk, L1_xattn_bk, L1_xattn_Wv, L1_xattn_bv, L1_xattn_Wo, L1_xattn_bo)
    x = x + _L1_ffn_ref(_layernorm(x, axis=-1), L1_ffn_gate_w, L1_ffn_gate_b, L1_ffn_sw1, L1_ffn_sb1, L1_ffn_sw2, L1_ffn_sb2, L1_ffn_w1, L1_ffn_b1, L1_ffn_w2, L1_ffn_b2)
    return x

_drawn_inputs = setup_inputs


def setup_inputs(seed=0):
    import zlib

    import numpy as np

    out = dict(_drawn_inputs(seed))
    spreads = {'L0_xattn_b_out': (0.0, 0.1),
     'L0_xattn_b_gate': (0.0, 0.462),
     'L0_xattn_gamma': (1.0, 0.6),
     'L0_xattn_beta': (0.0, 0.8),
     'L0_ffn_q_scale': (1.0, 0.6),
     'L0_ffn_k_scale': (1.0, 0.6),
     'L0_ffn_ln_g': (1.0, 0.6),
     'L0_ffn_ln_b': (0.0, 0.8),
     'L0_ffn_b1': (0.0, 0.8),
     'L0_ffn_b2': (0.0, 0.8),
     'L1_xattn_bq': (0.0, 2.0),
     'L1_xattn_bk': (0.0, 2.0),
     'L1_xattn_bv': (0.0, 0.8),
     'L1_xattn_bo': (0.0, 2.0),
     'L1_ffn_gate_b': (0.0, 2.0),
     'L1_ffn_sb1': (0.0, 2.0),
     'L1_ffn_sb2': (0.0, 2.0),
     'L1_ffn_b1': (0.0, 2.0),
     'L1_ffn_b2': (0.0, 2.0)}
    factors = {'L0_xattn_Wqkv': 5.902,
     'L0_xattn_Wout': 5.85,
     'L0_xattn_Wgate': 8.0,
     'L0_ffn_wqkv': 3.723,
     'L0_ffn_wo': 3.698,
     'L0_ffn_w1': 7.878,
     'L0_ffn_w2': 7.765,
     'L1_ffn_gate_w': 6.888,
     'L1_ffn_sw1': 5.576,
     'L1_ffn_sw2': 5.114,
     'L1_ffn_w1': 8.0,
     'L1_ffn_w2': 8.0,
     'L1_xattn_Wq': 7.005,
     'L1_xattn_Wk': 5.941,
     'L1_xattn_Wv': 2.827,
     'L1_xattn_Wo': 2.776}
    for name, (base, spread) in spreads.items():
        noise = np.random.default_rng([zlib.crc32(name.encode()), seed]).standard_normal(out[name].shape)
        drawn = base * np.exp(spread * noise) if base else spread * noise
        out[name] = jnp.asarray(drawn.astype(out[name].dtype))
    for name, factor in factors.items():
        out[name] = (out[name] * factor).astype(out[name].dtype)
    return out
```

```python
from contextlib import ExitStack

import concourse.bass as bass
import numpy as np
from concourse import mybir

F32 = mybir.dt.float32
BF16 = mybir.dt.bfloat16
I32 = mybir.dt.int32
U32 = mybir.dt.uint32
ALU = mybir.AluOpType
ACT = mybir.ActivationFunctionType
AX = mybir.AxisListType

P = 128
NSEQ = 32
PAIRS = NSEQ // 2
GROUP = 4
STEPS = NSEQ // GROUP // 2
NH, ND = 16, 8
WH, WD = 8, 64
SLOT = 64
LAYERS = 2
HID = 341
CHUNKS = [(0, 128), (128, 128), (256, HID - 256)]
EXPERTS = 8
EPS = 1e-5
MASKED = -1e9

CF = {}
_at = 0
for _name, _n in (("ident", P), ("rope_c", 2 * P), ("rope_s", 2 * P), ("xpos_c", 2 * WD), ("xpos_s", 2 * WD),
                  ("iota", EXPERTS)):
    CF[_name] = slice(_at, _at + _n)
    _at += _n
CF_COLS = _at
CB = {}
_at = 0
for _name, _n in (("ident", P), ("bias", 3 * P), ("band", P), ("band_t", P), ("pick_n", NH * P), ("pick_w", WH * P)):
    CB[_name] = slice(_at, _at + _n)
    _at += _n
CB_COLS = _at


def settle(eng, passed):
    eng.sem_inc(passed, 1)


class Chain:

    def __init__(self, eng, sem, step, per_step):
        self.eng, self.sem, self.base, self.per_step, self.n = eng, sem, step * per_step, per_step, 0

    def tag(self, ins):
        ins.then_inc(self.sem, 1)
        self.n += 1

    def wait(self):
        self.eng.wait_ge(self.sem, self.base + self.n)

    def end(self):
        assert self.n == self.per_step, (self.n, self.per_step)


def slot_head(slot):
    return 8 * (slot // 8) + 2 * (slot % 4) + slot % 8 // 4


def narrow_stage(nc, g, first):
    tag = "n1_" if first else "n2_"
    with ExitStack() as ctx:
        def sb(name, shape, dt):
            return ctx.enter_context(nc.sbuf_tensor(tag + name, shape, dt))

        def ps(name, shape, dt):
            return ctx.enter_context(nc.psum_tensor(tag + name, shape, dt))

        def sem(name):
            return ctx.enter_context(nc.semaphore(tag + name))

        x_all, z_all, ctx_all, cf, cb, ones_row = g["x"], g["z"], g["ctx"], g["cf"], g["cb"], g["ones_row"]
        ident, identb = cf[:, CF["ident"]], cb[:, CB["ident"]]
        bias3 = cb[:, CB["bias"]].rearrange("p (t k) -> p t k", t=3)
        pick = cb[0:2 * NH, CB["pick_n"]].rearrange("p (h k) -> p h k", h=NH)
        w = g["w_n1"] if first else g["w_n2"]
        wqkv, wout = w[:, 0:3 * P], w[:, 3 * P:4 * P]

        stats = sb("stats", [P, 2, 2, 6], F32)
        mv = sb("mv", [P, 2, 2, 2], F32)
        var_eps = sb("var_eps", [P, 4], F32)
        rstd = sb("rstd", [P, 4], F32)
        minus_half = g["minus_half"]
        xn = [sb(f"xn{u}", [P, P], F32) for u in range(2)]
        z_in = [sb(f"z_in{u}", [P, 2, P], F32) for u in range(2)]
        xT = [sb(f"xT{u}", [P, 2, P], F32) for u in range(2)]
        rot = [sb(f"rot{u}", [P, 2 * P], F32) for u in range(2)]
        rot_b = [sb(f"rot_b{u}", [P, 2 * P], F32) for u in range(2)]
        rest = [sb(f"rest{u}", [P, 2 * P], F32) for u in range(2)]
        rest2 = [sb(f"rest2{u}", [P, 2 * P], F32) for u in range(2)]
        stack = [sb(f"stack{u}", [P, 2, NH, SLOT], BF16) for u in range(2)]
        qT = [sb(f"qT{u}", [P, NH // 2, P], BF16) for u in range(2)]
        kT = [sb(f"kT{u}", [P, NH // 2, P], BF16) for u in range(2)]
        vaug = [sb(f"vaug{u}", [P, NH, 32], F32) for u in range(2)]
        negmax = [sb(f"negmax{u}", [P, NH], F32) for u in range(2)]
        negrest = [sb(f"negrest{u}", [P, NH], F32) for u in range(2)]
        shift = [sb(f"shift{u}", [P, 2, NH], BF16) for u in range(2)]
        shiftT = [sb(f"shiftT{u}", [2 * NH, P], BF16) for u in range(2)]
        prob = [sb(f"prob{u}", [P, NH, P], F32) for u in range(2)]
        oT = [sb(f"oT{u}", [P, 4, P], F32) for u in range(2)]
        rsum = [sb(f"rsum{u}", [P, NH], F32) for u in range(2)]
        att = [sb(f"att{u}", [P, P], F32) for u in range(2)]
        attT = [sb(f"attT{u}", [P, P], F32) for u in range(2)]
        aoT = [sb(f"aoT{u}", [P, P], F32) for u in range(2)]
        gate = [sb(f"gate{u}", [P, P], F32) for u in range(2)]
        mix = [sb(f"mix{u}", [P, 3, P], F32) for u in range(2)]
        neg_mask = [sb(f"neg_mask{u}", [P, P], BF16) for u in range(2)]
        neg_maskT = [sb(f"neg_maskT{u}", [P, P], BF16) for u in range(2)]
        row_max = [sb(f"row_max{u}", [P, 1], F32) for u in range(2)]
        q_scale = [sb(f"q_scale{u}", [P, 1], F32) for u in range(2)]

        misc = [ps(f"misc{u}", [P, 512], F32) for u in range(2)]
        tile = [ps(f"tile{u}", [P, 1024], F32) for u in range(2)]
        obank = [ps(f"obank{u}", [P, 512], F32) for u in range(2)]

        stats_ready = sem("stats_ready")
        rstd_ready = sem("rstd_ready")
        z_ready = sem("z_ready")
        ctx_ready = sem("ctx_ready")
        zT_ready = sem("zT_ready")
        xT_ready = sem("xT_ready")
        qkv_ready = sem("qkv_ready")
        v_ready = sem("v_ready")
        rot_ready = sem("rot_ready")
        split_ready = sem("split_ready")
        stackT_ready = sem("stackT_ready")
        qT_ready = sem("qT_ready")
        kT_ready = sem("kT_ready")
        mask_ready = sem("mask_ready")
        scores_ready = sem("scores_ready")
        max_done = sem("max_done")
        shift_ready = sem("shift_ready")
        shiftT_psum = sem("shiftT_psum")
        shiftT_ready = sem("shiftT_ready")
        shifted_ready = sem("shifted_ready")
        exp_done = sem("exp_done")
        pv_ready = sem("pv_ready")
        oT_ready = sem("oT_ready")
        o_ready = sem("o_ready")
        att_ready = sem("att_ready")
        attT_psum = sem("attT_psum")
        attT_ready = sem("attT_ready")
        ao_ready = sem("ao_ready")
        aoT_ready = sem("aoT_ready")
        gate_psum = sem("gate_psum")
        gate_ready = sem("gate_ready")
        dve_chain = sem("dve_chain")
        pool_chain = sem("pool_chain")

        def heads(ap, n=4):
            return ap.unsqueeze(1).broadcast_to([P, n, P])

        block = ctx.enter_context(nc.Block())

        @block.vector
        def _(dve):
            with dve.Fori(0, PAIRS) as it:
                ch = Chain(dve, dve_chain, it, 19 if first else 14)
                for u in range(2):
                    if not first:
                        xb = x_all[:, 2 * it + u, :]
                        ch.tag(dve.tensor_tensor(xb, xb, z_all[:, 2 * it + u, :], ALU.add))
                if not first:
                    ch.wait()
                    settle(dve, g["passed"])
                for u in range(2):
                    last = dve.bn_stats(stats[:, u, 0, :], x_all[:, 2 * it + u, :])
                    if first:
                        last = dve.bn_stats(stats[:, u, 1, :], ctx_all[:, 2 * it + u, :])
                ch.tag(last)
                ch.wait()
                settle(dve, g["passed"])
                for u in range(2):
                    last = dve.bn_aggr(mv[:, u, 0, :], stats[:, u, 0, :])
                    if first:
                        last = dve.bn_aggr(mv[:, u, 1, :], stats[:, u, 1, :])
                last.then_inc(stats_ready, 1)
                if not first:
                    for u in range(2):
                        ch.tag(dve.tensor_scalar(neg_mask[u][:, :], g["mask"][:, 2 * it + u, :], 0.0, MASKED,
                                                 ALU.is_equal, ALU.mult))
                    ch.wait()
                    for u in range(2):
                        ch.tag(dve.tensor_reduce(row_max[u][:, :], neg_mask[u][:, :], AX.X, ALU.max))
                    ch.wait()
                    for u in range(2):
                        dve.tensor_scalar(q_scale[u][:, :], row_max[u][:, :], 0.0, float(ND) ** -0.5,
                                          ALU.is_equal, ALU.mult).then_inc(mask_ready, 1)
                dve.wait_ge(rstd_ready, it * (2 if first else 1) + 1)
                if first:
                    for u in range(2):
                        ch.tag(dve.tensor_scalar(xn[u][:, :], x_all[:, 2 * it + u, :], mv[:, u, 0, 0:1],
                                                 rstd[:, 2 * u:2 * u + 1], ALU.subtract, ALU.mult))
                    for u in range(2):
                        dve.tensor_scalar(z_in[u][:, 1, :], ctx_all[:, 2 * it + u, :], mv[:, u, 1, 0:1],
                                          rstd[:, 2 * u + 1:2 * u + 2], ALU.subtract,
                                          ALU.mult).then_inc(ctx_ready, 1)
                    ch.wait()
                    settle(dve, g["passed"])
                    for u in range(2):
                        last = dve.bn_stats(stats[:, u, 0, :], xn[u][:, :])
                    ch.tag(last)
                    ch.wait()
                    settle(dve, g["passed"])
                    for u in range(2):
                        last = dve.bn_aggr(mv[:, u, 0, :], stats[:, u, 0, :])
                    last.then_inc(stats_ready, 1)
                    dve.wait_ge(rstd_ready, it * 2 + 2)
                    for u in range(2):
                        dve.tensor_scalar(z_in[u][:, 0, :], xn[u][:, :], mv[:, u, 0, 0:1],
                                          rstd[:, 2 * u:2 * u + 1], ALU.subtract, ALU.mult).then_inc(z_ready, 1)
                else:
                    for u in range(2):
                        dve.tensor_scalar(z_in[u][:, 0, :], x_all[:, 2 * it + u, :], mv[:, u, 0, 0:1],
                                          rstd[:, 2 * u:2 * u + 1], ALU.subtract, ALU.mult).then_inc(z_ready, 1)
                for u in range(2):
                    dve.wait_ge(qkv_ready, it * 2 + u + 1)
                    qk = misc[u][:, 0:2 * P]
                    if first:
                        ch.tag(dve.tensor_tensor(rot[u][:, :], qk, cf[:, CF["rope_c"]], ALU.mult))
                        ch.tag(dve.tensor_tensor(
                            rot_b[u][:, :].rearrange("p (h t r) -> p h t r", t=2, r=4),
                            qk.rearrange("p (h t r) -> p h t r", t=2, r=4)[:, :, ::-1, :],
                            cf[:, CF["rope_s"]].rearrange("p (h t r) -> p h t r", t=2, r=4), ALU.mult))
                        ch.wait()
                        dve.tensor_tensor(rot[u][:, :], rot[u][:, :], rot_b[u][:, :],
                                          ALU.add).then_inc(rot_ready, 1)
                    else:
                        dve.wait_ge(mask_ready, it * 2 + 2)
                        dve.tensor_scalar(rot[u][:, 0:P], qk[:, 0:P], q_scale[u][:, 0:1], None, ALU.mult)
                        dve.tensor_copy(rot[u][:, P:2 * P], qk[:, P:2 * P]).then_inc(rot_ready, 1)
                for u in range(2):
                    dve.wait_ge(stackT_ready, it * 2 + u + 1)
                    dve.tensor_copy(qT[u][:, :, :].rearrange("p h q -> p (h q)"),
                                    tile[u][:, 0:512].bitcast(BF16)).then_inc(qT_ready, 1)
                for c in range(2):
                    for u in range(2):
                        dve.wait_ge(scores_ready, it * 4 + 2 * c + u + 1)
                        dve.tensor_reduce(negmax[u][:, 8 * c:8 * c + 8],
                                          tile[u][:, :].rearrange("p (h k) -> p h k", h=8), AX.X, ALU.max,
                                          negate=True).then_inc(max_done, 1)
                dve.wait_ge(max_done, it * 4 + 4)
                for u in range(2):
                    ch.tag(dve.tensor_copy(shift[u][:, 0, :], negmax[u][:, :]))
                ch.wait()
                for u in range(2):
                    ch.tag(dve.tensor_tensor(negrest[u][:, :], negmax[u][:, :], shift[u][:, 0, :], ALU.subtract))
                ch.wait()
                for u in range(2):
                    dve.tensor_copy(shift[u][:, 1, :], negrest[u][:, :]).then_inc(shift_ready, 1)
                for u in range(2):
                    dve.wait_ge(shiftT_psum, it * 2 + u + 1)
                    dve.tensor_copy(shiftT[u][:, :],
                                    misc[u][0:2 * NH, 384:448].bitcast(BF16)).then_inc(shiftT_ready, 1)
                for u in range(2):
                    dve.wait_ge(o_ready, it * 2 + u + 1)
                    o = obank[u][:, :].rearrange("p (h r) -> p h r", r=32)
                    ch.tag(dve.reciprocal(rsum[u][:, :], o[:, :, ND]))
                    ch.wait()
                    dve.tensor_tensor(att[u][:, :].rearrange("p (h r) -> p h r", r=ND), o[:, :, 0:ND],
                                      rsum[u][:, :].unsqueeze(2).broadcast_to([P, NH, ND]),
                                      ALU.mult).then_inc(att_ready, 1)
                for u in range(2):
                    xb = x_all[:, 2 * it + u, :]
                    if first:
                        dve.wait_ge(gate_ready, it * 2 + u + 1)
                        ch.tag(dve.tensor_tensor(mix[u][:, 0, :], misc[u][:, 256:384], xn[u][:, :], ALU.subtract))
                        ch.wait()
                        ch.tag(dve.scalar_tensor_tensor(out=mix[u][:, 1, :], in0=gate[u][:, :], scalar=1.0,
                                                        in1=mix[u][:, 0, :], op0=ALU.add, op1=ALU.mult))
                        ch.wait()
                        dve.scalar_tensor_tensor(out=mix[u][:, 2, :], in0=mix[u][:, 1, :], scalar=0.5,
                                                 in1=xn[u][:, :], op0=ALU.mult, op1=ALU.add).then_inc(g["mixed"], 1)
                        dve.wait_ge(g["mixed"], it * 2 + u + 1)
                        last = dve.tensor_tensor(xb, xb, mix[u][:, 2, :], ALU.add)
                    else:
                        dve.wait_ge(ao_ready, it * 2 + u + 1)
                        last = dve.tensor_tensor(xb, xb, misc[u][:, P:2 * P], ALU.add)
                ch.tag(last)
                ch.end()

        @block.gpsimd
        def _(pool):
            pairs = lambda buf: buf[:, 0:4].rearrange("p (u s) -> p u s", u=2)
            for u in range(2):
                pool.memset(stack[u][:, :, :, :], 0.0)
                pool.memset(vaug[u][:, :, :], 0.0).then_inc(pool_chain, 1)
            pool.wait_ge(pool_chain, 2)
            for u in range(2):
                pool.memset(vaug[u][:, :, ND:ND + 1], 1.0).then_inc(pool_chain, 1)
            pool.wait_ge(pool_chain, 4)
            with pool.Fori(0, PAIRS) as it:
                ch = Chain(pool, pool_chain, it, 10 if first else 9)
                ch.base = ch.base + 4
                for n in range(2 if first else 1):
                    pool.wait_ge(stats_ready, it * (2 if first else 1) + n + 1)
                    settle(pool, g["passed"])
                    of = slice(0, 2 if first else 1)
                    ch.tag(pool.tensor_scalar(pairs(var_eps)[:, :, of], mv[:, :, of, 1], EPS, 1.0,
                                              ALU.add, ALU.mult))
                    ch.wait()
                    pool.tensor_tensor(pairs(rstd)[:, :, of], pairs(var_eps)[:, :, of], pairs(minus_half)[:, :, of],
                                       ALU.pow).then_inc(rstd_ready, 1)
                for u in range(2):
                    pool.wait_ge(rot_ready, it * 2 + u + 1)
                    settle(pool, g["passed"])

                    def cast(out, src):
                        return pool.tensor_scalar(out, src, 1.0, 0.0, ALU.mult, ALU.add)

                    def slots(which, a, b, step=1):
                        v = stack[u][:, which, :, 0:6 * ND].rearrange("p h (s r) -> p h s r", r=ND)
                        return v[:, :, a:b:step, :]

                    def part(buf, which, n):
                        v = buf[u][:, which * P:(which + 1) * P].rearrange("p (h r) -> p h r", r=ND)
                        return v.unsqueeze(2).broadcast_to([P, NH, n, ND])

                    both = lambda s: stack[u][:, :, :, s * ND:(s + 1) * ND]
                    whole = lambda buf: buf[u][:, :].rearrange("p (a h r) -> p a h r", a=2, r=ND)
                    cast(slots(0, 0, 3), part(rot, 0, 3))
                    cast(slots(1, 0, 4, 3), part(rot, 1, 2))
                    ch.tag(cast(slots(1, 5, 6), part(rot, 1, 1)))
                    ch.wait()
                    ch.tag(pool.tensor_tensor(whole(rest), whole(rot), both(0), ALU.subtract))
                    ch.wait()
                    settle(pool, g["passed"])
                    cast(slots(0, 3, 5), part(rest, 0, 2))
                    ch.tag(cast(slots(1, 1, 5, 3), part(rest, 1, 2)))
                    ch.wait()
                    ch.tag(pool.tensor_tensor(whole(rest2), whole(rest), both(4), ALU.subtract))
                    ch.wait()
                    settle(pool, g["passed"])
                    cast(slots(0, 5, 6), part(rest2, 0, 1))
                    cast(slots(1, 2, 3), part(rest2, 1, 1)).then_inc(split_ready, 1)
                ch.end()

        @block.scalar
        def _(act):
            with act.Fori(0, PAIRS) as it:
                if not first:
                    for u in range(2):
                        act.activation(z_in[u][:, 1, :], ctx_all[:, 2 * it + u, :], ACT.Copy).then_inc(ctx_ready, 1)
                for u in range(2):
                    act.wait_ge(zT_ready, it * 2 + u + 1)
                    zT = misc[u][:, 0:2 * P]
                    out = xT[u][:, :, :].rearrange("p s t -> p (s t)")
                    if first:
                        act.activation(out, zT, ACT.Identity, scale=g["cols"][:, 0:1],
                                       bias=g["cols"][:, 1:2]).then_inc(xT_ready, 1)
                    else:
                        act.activation(neg_maskT[u][:, :], misc[u][:, 448:512].bitcast(BF16), ACT.Copy)
                        act.activation(out, zT, ACT.Copy).then_inc(xT_ready, 1)
                for u in range(2):
                    act.wait_ge(qkv_ready, it * 2 + u + 1)
                    act.activation(vaug[u][:, :, 0:ND], obank[u][:, 0:P].rearrange("p (h r) -> p h r", r=ND),
                                   ACT.Copy).then_inc(v_ready, 1)
                for u in range(2):
                    act.wait_ge(stackT_ready, it * 2 + u + 1)
                    act.activation(kT[u][:, :, :].rearrange("p h k -> p (h k)"), tile[u][:, 512:1024].bitcast(BF16),
                                   ACT.Copy).then_inc(kT_ready, 1)
                for c in range(2):
                    for u in range(2):
                        act.wait_ge(shifted_ready, it * 4 + 2 * c + u + 1)
                        act.activation(prob[u][:, 8 * c:8 * c + 8, :].rearrange("p h q -> p (h q)"), tile[u][:, :],
                                       ACT.Exp).then_inc(exp_done, 1)
                for u in range(2):
                    act.wait_ge(pv_ready, it * 2 + u + 1)
                    act.activation(oT[u][:, :, :].rearrange("p g q -> p (g q)"), obank[u][:, :],
                                   ACT.Copy).then_inc(oT_ready, 1)
                for u in range(2):
                    act.wait_ge(attT_psum, it * 2 + u + 1)
                    act.activation(attT[u][:, :], misc[u][:, 0:P], ACT.Copy).then_inc(attT_ready, 1)
                if first:
                    for u in range(2):
                        act.wait_ge(ao_ready, it * 2 + u + 1)
                        act.activation(aoT[u][:, :], misc[u][:, P:2 * P], ACT.Identity,
                                       bias=g["cols"][:, 2:3]).then_inc(aoT_ready, 1)
                    for u in range(2):
                        act.wait_ge(gate_psum, it * 2 + u + 1)
                        act.activation(gate[u][:, :], misc[u][:, 384:512], ACT.Tanh,
                                       scale=0.5).then_inc(gate_ready, 1)

        @block.tensor
        def _(pe):
            def stack_pair(u, h):
                rows = slice(SLOT * (h % 2), SLOT * (h % 2) + SLOT)
                return qT[u][rows, h // 2, :], kT[u][rows, h // 2, :]

            with pe.Fori(0, PAIRS) as it:
                for u in range(2):
                    pe.wait_ge(z_ready, it * 2 + u + 1)
                    pe.wait_ge(ctx_ready, it * 2 + u + 1)
                    if not first:
                        pe.wait_ge(mask_ready, it * 2 + u + 1)
                        pe.transpose(misc[u][:, 448:512].bitcast(BF16), neg_mask[u][:, :], identb)
                    pe.transpose(misc[u][:, 0:P], z_in[u][:, 0, :], ident)
                    pe.transpose(misc[u][:, P:2 * P], z_in[u][:, 1, :], ident).then_inc(zT_ready, 1)
                for u in range(2):
                    pe.wait_ge(xT_ready, it * 2 + u + 1)
                    for into, which, at in ((misc[u][:, 0:P], 0, 0), (misc[u][:, P:2 * P], 1, P),
                                            (obank[u][:, 0:P], 1, 2 * P)):
                        if not first:
                            pe.matmul(into, ones_row[0:1, :], g["row_n2"][0:1, at:at + P], start=True, stop=False)
                        last = pe.matmul(into, xT[u][:, which, :], wqkv[:, at:at + P], start=first, stop=True)
                    last.then_inc(qkv_ready, 1)
                for u in range(2):
                    pe.wait_ge(split_ready, it * 2 + u + 1)
                    for which in range(2):
                        into = tile[u][:, 512 * which:512 * which + 512].bitcast(BF16)
                        for pair in range(NH // 2):
                            last = pe.transpose(into[:, pair * P:(pair + 1) * P],
                                                stack[u][:, which, 2 * pair:2 * pair + 2, :]
                                                .rearrange("p h s -> p (h s)"), identb)
                    last.then_inc(stackT_ready, 1)
                for c in range(2):
                    for u in range(2):
                        if c == 0:
                            pe.wait_ge(qT_ready, it * 2 + u + 1)
                            pe.wait_ge(kT_ready, it * 2 + u + 1)
                        else:
                            pe.wait_ge(max_done, it * 4 + u + 1)
                        for half in range(2):
                            if not first:
                                pe.matmul(tile[u][:, 512 * half:512 * half + 512], identb, heads(neg_mask[u][:, :]),
                                          start=True, stop=False, skip_group_check=True)
                        for j in range(8):
                            slot = 4 * (j % 2) + j // 2
                            q, k = stack_pair(u, slot_head(8 * c + slot))
                            last = pe.matmul(tile[u][:, P * slot:P * (slot + 1)], q, k, start=first, stop=True,
                                             skip_group_check=True)
                        last.then_inc(scores_ready, 1)
                for u in range(2):
                    pe.wait_ge(shift_ready, it * 2 + u + 1)
                    pe.transpose(misc[u][0:2 * NH, 384:448].bitcast(BF16),
                                 shift[u][:, :, :].rearrange("p t h -> p (t h)"), identb).then_inc(shiftT_psum, 1)

                def shifted_scores(u, c):
                    for half in range(2):
                        bank = tile[u][:, 512 * half:512 * half + 512]
                        if first:
                            for t in range(3):
                                pe.matmul(bank, identb, heads(bias3[:, t, :]), start=(t == 0), stop=False,
                                          skip_group_check=True)
                        else:
                            pe.matmul(bank, identb, heads(neg_maskT[u][:, :]), start=True, stop=False,
                                      skip_group_check=True)
                    for j in range(8):
                        slot = 4 * (j % 2) + j // 2
                        q, k = stack_pair(u, slot_head(8 * c + slot))
                        pe.matmul(tile[u][:, P * slot:P * (slot + 1)], k, q, start=False, stop=False,
                                  skip_group_check=True)
                    for slot in range(8):
                        last = pe.matmul(tile[u][:, P * slot:P * (slot + 1)], pick[:, 8 * c + slot, :],
                                         shiftT[u][:, :], start=False, stop=True, skip_group_check=True)
                    last.then_inc(shifted_ready, 1)

                def values(u, c):
                    for h in range(8 * c, 8 * c + 8):
                        row = 32 * (h % 4)
                        slot = 8 * c + 4 * (h % 2) + h % 8 // 2
                        last = pe.matmul(obank[u][row:row + 32, P * (h // 4):P * (h // 4) + P], vaug[u][:, h, :],
                                         prob[u][:, slot, :], start=True, stop=True)
                    return last

                for u in range(2):
                    pe.wait_ge(shiftT_ready, it * 2 + u + 1)
                    shifted_scores(u, 0)
                for u in range(2):
                    pe.wait_ge(exp_done, it * 4 + u + 1)
                    shifted_scores(u, 1)
                    pe.wait_ge(v_ready, it * 2 + u + 1)
                    values(u, 0)
                for u in range(2):
                    pe.wait_ge(exp_done, it * 4 + 2 + u + 1)
                    values(u, 1).then_inc(pv_ready, 1)
                for u in range(2):
                    pe.wait_ge(oT_ready, it * 2 + u + 1)
                    for n in range(4):
                        last = pe.transpose(obank[u][:, n * P:(n + 1) * P], oT[u][:, n, :], ident)
                    last.then_inc(o_ready, 1)
                for u in range(2):
                    pe.wait_ge(att_ready, it * 2 + u + 1)
                    pe.transpose(misc[u][:, 0:P], att[u][:, :], ident).then_inc(attT_psum, 1)
                for u in range(2):
                    pe.wait_ge(attT_ready, it * 2 + u + 1)
                    if first:
                        pe.matmul(misc[u][:, 2 * P:3 * P], ones_row[0:1, :], g["row_n1"][0:1, 0:P],
                                  start=True, stop=False)
                        pe.matmul(misc[u][:, 2 * P:3 * P], attT[u][:, :], wout, start=False, stop=True)
                        pe.matmul(misc[u][:, P:2 * P], wout, attT[u][:, :], start=True,
                                  stop=True).then_inc(ao_ready, 1)
                    else:
                        pe.matmul(misc[u][:, P:2 * P], ones_row[0:1, :], g["row_n2"][0:1, 3 * P:4 * P],
                                  start=True, stop=False)
                        pe.matmul(misc[u][:, P:2 * P], attT[u][:, :], wout, start=False,
                                  stop=True).then_inc(ao_ready, 1)
                if first:
                    for u in range(2):
                        pe.wait_ge(aoT_ready, it * 2 + u + 1)
                        pe.matmul(misc[u][:, 384:512], ones_row[0:1, :], g["row_n1"][0:1, P:2 * P],
                                  start=True, stop=False)
                        pe.matmul(misc[u][:, 384:512], aoT[u][:, :], w[:, 4 * P:5 * P], start=False,
                                  stop=True).then_inc(gate_psum, 1)



def norm_stage(nc, g):
    N = 2 * GROUP
    with ExitStack() as ctx:
        stats = ctx.enter_context(nc.sbuf_tensor("nz_stats", [P, N, 6], F32))
        mv = ctx.enter_context(nc.sbuf_tensor("nz_mv", [P, N, 2], F32))
        var_eps = ctx.enter_context(nc.sbuf_tensor("nz_var_eps", [P, N], F32))
        rstd = ctx.enter_context(nc.sbuf_tensor("nz_rstd", [P, N], F32))
        stats_ready = ctx.enter_context(nc.semaphore("nz_stats_ready"))
        rstd_ready = ctx.enter_context(nc.semaphore("nz_rstd_ready"))
        dve_chain = ctx.enter_context(nc.semaphore("nz_dve_chain"))
        pool_chain = ctx.enter_context(nc.semaphore("nz_pool_chain"))
        block = ctx.enter_context(nc.Block())

        @block.vector
        def _(dve):
            with dve.Fori(0, NSEQ // N) as it:
                ch = Chain(dve, dve_chain, it, 1)
                for n in range(N):
                    last = dve.bn_stats(stats[:, n, :], g["x"][:, N * it + n, :])
                ch.tag(last)
                ch.wait()
                settle(dve, g["passed"])
                for n in range(N):
                    last = dve.bn_aggr(mv[:, n, :], stats[:, n, :])
                last.then_inc(stats_ready, 1)
                dve.wait_ge(rstd_ready, it + 1)
                for n in range(N):
                    dve.tensor_scalar(g["z"][:, N * it + n, :], g["x"][:, N * it + n, :], mv[:, n, 0:1],
                                      rstd[:, n:n + 1], ALU.subtract, ALU.mult)
                ch.end()

        @block.gpsimd
        def _(pool):
            with pool.Fori(0, NSEQ // N) as it:
                ch = Chain(pool, pool_chain, it, 1)
                pool.wait_ge(stats_ready, it + 1)
                settle(pool, g["passed"])
                ch.tag(pool.tensor_scalar(var_eps[:, :], mv[:, :, 1], EPS, 1.0, ALU.add, ALU.mult))
                ch.wait()
                pool.tensor_tensor(rstd[:, :], var_eps[:, :], g["minus_half"][:, 0:N], ALU.pow).then_inc(rstd_ready, 1)
                ch.end()


WIDE_SEMS = ["wqkv_loaded", "wo_loaded", "gain_loaded", "tables_ready", "dve_chain", "pool_chain", "zc_ready",
             "raw_ready", "square_ready", "norm2_ready", "half_turn_ready", "inv_norm_ready", "rot_ready",
             "scores_ready", "shift_ready", "shiftT_psum", "shiftT_ready", "pv_ready", "rsum_ready", "att_ready",
             "out_ready", "edges_ready", "zT_ready", "hT_ready", "qk_ready", "v_psum", "v_ready", "qkT_psum",
             "qkT_ready", "shifted_ready", "exp_done", "attT_psum", "attT_ready"]


def wide_stage(nc, g, layer, s):
    with ExitStack() as ctx:
        def sb(name, shape, dt):
            return ctx.enter_context(nc.sbuf_tensor("w_" + name, shape, dt))

        def ps(name, shape, dt):
            return ctx.enter_context(nc.psum_tensor("w_" + name, shape, dt))

        z_all, cf, cb = g["z"], g["cf"], g["cb"]
        ident, identb = cf[:, CF["ident"]], cb[:, CB["ident"]]
        pick = cb[0:2 * WH, CB["pick_w"]].rearrange("p (h k) -> p h k", h=WH)
        band, band_t = cb[:, CB["band"]], cb[:, CB["band_t"]]
        IN = WH * WD
        wqkv = sb("wqkv", [P, 3 * IN], F32)
        wo = sb("wo", [P, 4, P], F32)
        qk_gain = sb("qk_gain", [P, 2, WD], F32)
        rot_c = sb("rot_c", [P, 2, WD], F32)
        rot_s = sb("rot_s", [P, 2, WD], F32)
        zc = [sb(f"zc{u}", [P, P], F32) for u in range(2)]
        hT = [sb(f"hT{u}", [P, P], F32) for u in range(2)]
        square = [sb(f"square{u}", [P, 2 * IN], F32) for u in range(2)]
        raw = [sb(f"raw{u}", [P, 2 * IN], F32) for u in range(2)]
        rot = [sb(f"rot{u}", [P, 2 * IN], F32) for u in range(2)]
        half_turn = [sb(f"half_turn{u}", [P, 2 * IN], F32) for u in range(2)]
        norm2 = [sb(f"norm2{u}", [P, 2 * WH], F32) for u in range(2)]
        clipped = [sb(f"clipped{u}", [P, 2 * WH], F32) for u in range(2)]
        inv_norm = [sb(f"inv_norm{u}", [P, 2 * WH], F32) for u in range(2)]
        qkT = [sb(f"qkT{u}", [P, WH, P], F32) for u in range(2)]
        values1 = [sb(f"values{u}", [P, WH, WD + 1], F32) for u in range(2)]
        negmax = [sb(f"negmax{u}", [P, WH], F32) for u in range(2)]
        negrest = [sb(f"negrest{u}", [P, WH], F32) for u in range(2)]
        shift = [sb(f"shift{u}", [P, 2, WH], BF16) for u in range(2)]
        shiftT = [sb(f"shiftT{u}", [2 * WH, P], BF16) for u in range(2)]
        prob = [sb(f"prob{u}", [P, WH, P], F32) for u in range(2)]
        rsum = [sb(f"rsum{u}", [P, WH], F32) for u in range(2)]
        att = [sb(f"att{u}", [P, IN], F32) for u in range(2)]
        attT = [sb(f"attT{u}", [P, 4, P], F32) for u in range(2)]

        misc = [ps(f"misc{u}", [P, 512], F32) for u in range(2)]
        tile = [ps(f"tile{u}", [P, 1024], F32) for u in range(2)]
        obank = [ps(f"obank{c}", [P, 512], F32) for c in range(2)]

        block = ctx.enter_context(nc.Block())
        n0 = layer * PAIRS

        @block.sync
        def _(sp):
            one = bass.ds(layer, 1)
            sp.dma_start(wqkv[:, :], g["d_wqkv"][one, :, :].rearrange("a p n -> p (a n)")).then_inc(
                s["wqkv_loaded"], 16)
            sp.dma_start(wo[:, :, :], g["d_wo"][one, :, :].rearrange("a (c p) n -> p (a c) n", p=P)).then_inc(
                s["wo_loaded"], 16)
            for k, name in enumerate(("d_qs", "d_ks")):
                sp.dma_start(qk_gain[:, k, :], g[name][one, :].broadcast_to([P, WD])).then_inc(s["gain_loaded"], 16)

        @block.vector
        def _(dve):
            for u in range(2):
                dve.memset(hT[u][WD:P, 0:1], 0.0).then_inc(s["edges_ready"], 1)
            dve.wait_ge(s["gain_loaded"], 32 * layer + 32)
            gain = qk_gain[:, :, :].rearrange("p a (t r) -> p a t r", t=2)
            dve.tensor_tensor(rot_c[:, :, :], qk_gain[:, :, :],
                              cf[:, CF["xpos_c"]].rearrange("p (a r) -> p a r", a=2), ALU.mult)
            dve.tensor_tensor(rot_s[:, :, :].rearrange("p a (t r) -> p a t r", t=2), gain[:, :, ::-1, :],
                              cf[:, CF["xpos_s"]].rearrange("p (a t r) -> p a t r", a=2, t=2),
                              ALU.mult).then_inc(s["tables_ready"], 1)
            with dve.Fori(0, PAIRS) as it:
                n = n0 + it
                ch = Chain(dve, s["dve_chain"], n, 12)
                for u in range(2):
                    dve.tensor_copy(zc[u][:, :], z_all[:, 2 * it + u, :]).then_inc(s["zc_ready"], 1)
                dve.wait_ge(s["tables_ready"], layer + 1)
                for u in range(2):
                    dve.wait_ge(s["raw_ready"], n * 2 + u + 1)
                    for a in range(2):
                        by_head = lambda buf: buf[u][:, a * IN:(a + 1) * IN].rearrange("p (h r) -> p h r", h=WH)
                        last = dve.tensor_tensor(by_head(rot), by_head(raw),
                                                 rot_c[:, a, :].unsqueeze(1).broadcast_to([P, WH, WD]), ALU.mult)
                    ch.tag(last)
                    dve.wait_ge(s["square_ready"], n * 2 + u + 1)
                    dve.tensor_reduce(norm2[u][:, :], square[u][:, :].rearrange("p (h r) -> p h r", r=WD), AX.X,
                                      ALU.add).then_inc(s["norm2_ready"], 1)
                for u in range(2):
                    dve.wait_ge(s["half_turn_ready"], n * 2 + u + 1)
                    ch.wait()
                    ch.tag(dve.tensor_tensor(rot[u][:, :], rot[u][:, :], half_turn[u][:, :], ALU.add))
                    ch.wait()
                    dve.wait_ge(s["inv_norm_ready"], n * 2 + u + 1)
                    by_head = rot[u][:, :].rearrange("p (h r) -> p h r", r=WD)
                    dve.tensor_tensor(by_head, by_head, inv_norm[u][:, :].unsqueeze(2).broadcast_to([P, 2 * WH, WD]),
                                      ALU.mult).then_inc(s["rot_ready"], 1)
                for u in range(2):
                    dve.wait_ge(s["scores_ready"], n * 2 + u + 1)
                    ch.tag(dve.tensor_reduce(negmax[u][:, :], tile[u][:, :].rearrange("p (h k) -> p h k", h=WH), AX.X,
                                             ALU.max, negate=True))
                    ch.wait()
                    ch.tag(dve.tensor_copy(shift[u][:, 0, :], negmax[u][:, :]))
                    ch.wait()
                    ch.tag(dve.tensor_tensor(negrest[u][:, :], negmax[u][:, :], shift[u][:, 0, :], ALU.subtract))
                    ch.wait()
                    dve.tensor_copy(shift[u][:, 1, :], negrest[u][:, :]).then_inc(s["shift_ready"], 1)
                for u in range(2):
                    dve.wait_ge(s["shiftT_psum"], n * 2 + u + 1)
                    dve.tensor_copy(shiftT[u][:, :], misc[u][0:2 * WH, 0:64].bitcast(BF16)).then_inc(
                        s["shiftT_ready"], 1)
                for u in range(2):
                    for c in range(2):
                        dve.wait_ge(s["pv_ready"], n * 4 + 2 * u + c + 1)
                        o = obank[c][:, 0:4 * (WD + 1)].rearrange("p (h r) -> p h r", r=WD + 1)
                        dve.reciprocal(rsum[u][:, 4 * c:4 * c + 4], o[:, :, WD]).then_inc(s["rsum_ready"], 1)
                        dve.wait_ge(s["rsum_ready"], n * 4 + 2 * u + c + 1)
                        dve.tensor_tensor(att[u][:, 4 * c * WD:4 * (c + 1) * WD].rearrange("p (h r) -> p h r", r=WD),
                                          o[:, :, 0:WD],
                                          rsum[u][:, 4 * c:4 * c + 4].unsqueeze(2).broadcast_to([P, 4, WD]),
                                          ALU.mult).then_inc(s["att_ready"], 1)
                for u in range(2):
                    dve.wait_ge(s["out_ready"], n * 2 + u + 1)
                    zb = z_all[:, 2 * it + u, :]
                    last = dve.tensor_tensor(zb, zb, misc[u][:, 0:P], ALU.add)
                    ch.tag(last)
                ch.end()

        @block.gpsimd
        def _(pool):
            for u in range(2):
                pool.memset(values1[u][:, :, WD:WD + 1], 1.0).then_inc(s["edges_ready"], 1)
            pool.wait_ge(s["tables_ready"], layer + 1)
            settle(pool, g["passed"])
            with pool.Fori(0, PAIRS) as it:
                n = n0 + it
                ch = Chain(pool, s["pool_chain"], n, 2)
                for u in range(2):
                    pool.wait_ge(s["raw_ready"], n * 2 + u + 1)
                    for a in range(2):
                        for t in range(2):
                            half = lambda buf, t: buf[u][:, a * IN:(a + 1) * IN].rearrange(
                                "p (h t r) -> p h t r", h=WH, t=2)[:, :, t, :]
                            table = rot_s[:, a, t * WD // 2:(t + 1) * WD // 2].unsqueeze(1).broadcast_to(
                                [P, WH, WD // 2])
                            last = pool.tensor_tensor(half(half_turn, t), half(raw, 1 - t), table, ALU.mult)
                    last.then_inc(s["half_turn_ready"], 1)
                    pool.wait_ge(s["norm2_ready"], n * 2 + u + 1)
                    settle(pool, g["passed"])
                    ch.tag(pool.tensor_scalar(clipped[u][:, :], norm2[u][:, :], 1e-24, 1.0, ALU.max, ALU.mult))
                    ch.wait()
                    pool.tensor_tensor(inv_norm[u][:, :], clipped[u][:, :], g["minus_half"][:, 0:2 * WH],
                                       ALU.pow).then_inc(s["inv_norm_ready"], 1)
                ch.end()

        @block.scalar
        def _(act):
            act.wait_ge(s["edges_ready"], 4 * layer + 4)
            settle(act, g["passed"])
            with act.Fori(0, PAIRS) as it:
                n = n0 + it
                for u in range(2):
                    act.wait_ge(s["zT_ready"], n * 2 + u + 1)
                    act.activation(hT[u][0:WD, :], misc[u][0:WD, 0:P], ACT.Copy)
                    act.activation(hT[u][WD:P, 1:P], misc[u][WD:P, 0:P - 1], ACT.Copy).then_inc(s["hT_ready"], 1)
                for u in range(2):
                    act.wait_ge(s["qk_ready"], n * 2 + u + 1)
                    act.activation(raw[u][:, :], tile[u][:, :], ACT.Copy).then_inc(s["raw_ready"], 1)
                    act.activation(square[u][:, :], tile[u][:, :], ACT.Square).then_inc(s["square_ready"], 1)
                    act.wait_ge(s["v_psum"], n * 2 + u + 1)
                    act.activation(values1[u][:, :, 0:WD], misc[u][:, :].rearrange("p (h r) -> p h r", r=WD),
                                   ACT.Copy).then_inc(s["v_ready"], 1)
                for u in range(2):
                    act.wait_ge(s["qkT_psum"], n * 2 + u + 1)
                    act.activation(qkT[u][:, :, :].rearrange("p h k -> p (h k)"), tile[u][:, :],
                                   ACT.Copy).then_inc(s["qkT_ready"], 1)
                for u in range(2):
                    act.wait_ge(s["shifted_ready"], n * 2 + u + 1)
                    act.activation(prob[u][:, :, :].rearrange("p h q -> p (h q)"), tile[u][:, :],
                                   ACT.Exp).then_inc(s["exp_done"], 1)
                for u in range(2):
                    act.wait_ge(s["attT_psum"], n * 2 + u + 1)
                    act.activation(attT[u][:, :, :].rearrange("p c q -> p (c q)"), misc[u][:, :],
                                   ACT.Copy).then_inc(s["attT_ready"], 1)

        @block.tensor
        def _(pe):
            pe.wait_ge(s["wqkv_loaded"], 16 * layer + 16)
            pe.wait_ge(s["wo_loaded"], 16 * layer + 16)
            settle(pe, g["passed"])
            with pe.Fori(0, PAIRS) as it:
                n = n0 + it
                for u in range(2):
                    pe.wait_ge(s["zc_ready"], n * 2 + u + 1)
                    pe.transpose(misc[u][:, 0:P], zc[u][:, :], ident).then_inc(s["zT_ready"], 1)
                for u in range(2):
                    pe.wait_ge(s["hT_ready"], n * 2 + u + 1)
                    for half in range(2):
                        last = pe.matmul(tile[u][:, 512 * half:512 * half + 512], hT[u][:, :],
                                         wqkv[:, IN * half:IN * (half + 1)], start=True, stop=True)
                    last.then_inc(s["qk_ready"], 1)
                    pe.matmul(misc[u][:, :], hT[u][:, :], wqkv[:, 2 * IN:3 * IN], start=True,
                              stop=True).then_inc(s["v_psum"], 1)
                for u in range(2):
                    pe.wait_ge(s["rot_ready"], n * 2 + u + 1)
                    for j in range(WH):
                        last = pe.transpose(tile[u][:, j * P:(j + 1) * P], rot[u][:, j * P:(j + 1) * P], ident)
                    last.then_inc(s["qkT_psum"], 1)

                def pair(u, h):
                    rows = slice(WD * (h % 2), WD * (h % 2) + WD)
                    return qkT[u][rows, h // 2, :], qkT[u][rows, WH // 2 + h // 2, :]

                def shared(ap):
                    return ap.unsqueeze(1).broadcast_to([P, 4, P])

                for u in range(2):
                    pe.wait_ge(s["qkT_ready"], n * 2 + u + 1)
                    for half in range(2):
                        bank = tile[u][:, 512 * half:512 * half + 512]
                        pe.matmul(bank, identb, shared(band), start=True, stop=False, skip_group_check=True)
                    for j in range(8):
                        slot = 4 * (j % 2) + j // 2
                        q, k = pair(u, slot_head(slot))
                        last = pe.matmul(tile[u][:, P * slot:P * (slot + 1)], q, k, start=False, stop=True,
                                         skip_group_check=True)
                    last.then_inc(s["scores_ready"], 1)
                for u in range(2):
                    pe.wait_ge(s["shift_ready"], n * 2 + u + 1)
                    pe.wait_ge(s["v_ready"], n * 2 + u + 1)
                    pe.transpose(misc[u][0:2 * WH, 0:64].bitcast(BF16),
                                 shift[u][:, :, :].rearrange("p t h -> p (t h)"), identb).then_inc(
                        s["shiftT_psum"], 1)
                for u in range(2):
                    pe.wait_ge(s["shiftT_ready"], n * 2 + u + 1)
                    for half in range(2):
                        bank = tile[u][:, 512 * half:512 * half + 512]
                        pe.matmul(bank, identb, shared(band_t), start=True, stop=False, skip_group_check=True)
                    for j in range(8):
                        slot = 4 * (j % 2) + j // 2
                        q, k = pair(u, slot_head(slot))
                        pe.matmul(tile[u][:, P * slot:P * (slot + 1)], k, q, start=False, stop=False,
                                  skip_group_check=True)
                    for slot in range(8):
                        last = pe.matmul(tile[u][:, P * slot:P * (slot + 1)], pick[:, slot, :], shiftT[u][:, :],
                                         start=False, stop=True, skip_group_check=True)
                    last.then_inc(s["shifted_ready"], 1)
                for u in range(2):
                    pe.wait_ge(s["exp_done"], n * 2 + u + 1)
                    for c in range(2):
                        if u:
                            pe.wait_ge(s["att_ready"], n * 4 + c + 1)
                        for j in range(4):
                            h = 4 * c + j
                            last = pe.matmul(obank[c][:, j * (WD + 1):(j + 1) * (WD + 1)],
                                             prob[u][:, 4 * (h % 2) + h // 2, :],
                                             values1[u][:, h, :], start=True, stop=True)
                        last.then_inc(s["pv_ready"], 1)
                for u in range(2):
                    pe.wait_ge(s["att_ready"], n * 4 + 2 * u + 2)
                    for c in range(4):
                        last = pe.transpose(misc[u][:, c * P:(c + 1) * P], att[u][:, c * P:(c + 1) * P], ident)
                    last.then_inc(s["attT_psum"], 1)
                for u in range(2):
                    pe.wait_ge(s["attT_ready"], n * 2 + u + 1)
                    for c in range(4):
                        last = pe.matmul(misc[u][:, 0:P], attT[u][:, c, :], wo[:, c, :], start=(c == 0),
                                         stop=(c == 3))
                    last.then_inc(s["out_ready"], 1)


GLU_SEMS = ["before_ready", "w1_loaded", "w2_loaded", "b1_loaded", "b2_loaded", "ln_loaded", "first_row_zero",
            "dve_chain", "pool_chain", "stats_ready", "rstd_ready", "hn_ready", "lin_ready", "gel_ready",
            "gated_ready", "y_ready", "turn_ready", "hT_ready", "gate_ready"]


def glu_stage(nc, g, layer, s):
    with ExitStack() as ctx:
        def sb(name, shape, dt):
            return ctx.enter_context(nc.sbuf_tensor("m_" + name, shape, dt))

        def ps(name, shape, dt):
            return ctx.enter_context(nc.psum_tensor("m_" + name, shape, dt))

        z_all, cf, ones_row = g["z"], g["cf"], g["ones_row"]
        ident = cf[:, CF["ident"]]
        N = GROUP * P
        w1 = sb("w1", [P, 2 * HID], F32)
        w2 = sb("w2", [P, 3, P], F32)
        b1 = sb("b1", [P, 2, 3], F32)
        b2 = sb("b2", [1, P], F32)
        ln = sb("ln", [P, 2], F32)
        before = sb("before", [P, NSEQ, WD], F32)
        stats = [sb(f"stats{u}", [P, GROUP, 2, 6], F32) for u in range(2)]
        mv = [sb(f"mv{u}", [P, GROUP, 2], F32) for u in range(2)]
        var_eps = [sb(f"var_eps{u}", [P, GROUP], F32) for u in range(2)]
        rstd = [sb(f"rstd{u}", [P, GROUP], F32) for u in range(2)]
        hn = [sb(f"hn{u}", [P, GROUP, P], F32) for u in range(2)]
        hT = [sb(f"hT{u}", [P, N], F32) for u in range(2)]
        gel = [sb(f"gel{u}", [P, N], F32) for u in range(2)]
        gated = [[sb(f"gated{u}{c}", [P, N], F32) for c in range(3)] for u in range(2)]
        turn = [ps(f"turn{u}", [P, N], F32) for u in range(2)]
        gate = [ps(f"gate{i}", [P, N], F32) for i in range(2)]
        lin = [ps(f"lin{i}", [P, N], F32) for i in range(2)]
        y = [ps(f"y{u}", [P, GROUP, P], F32) for u in range(2)]
        block = ctx.enter_context(nc.Block())
        n0 = layer * STEPS

        @block.sync
        def _(sp):
            one = bass.ds(layer, 1)
            for k in range(4):
                seqs = slice(NSEQ // 4 * k, NSEQ // 4 * (k + 1))
                sp.dma_start(before[1:P, seqs, :], z_all[0:P - 1, seqs, WD:P]).then_inc(s["before_ready"], 16)
            sp.dma_start(w1[:, :], g["d_w1"][one, :, :].rearrange("a p n -> p (a n)")).then_inc(s["w1_loaded"], 16)
            for c, (at, n) in enumerate(CHUNKS):
                sp.dma_start(w2[0:n, c, :], g["d_w2"][one, at:at + n, :].rearrange("a p n -> p (a n)")).then_inc(
                    s["w2_loaded"], 16)
                for a in range(2):
                    sp.dma_start(b1[0:n, a, c:c + 1],
                                 g["d_b1"][one, a * HID + at:a * HID + at + n].rearrange("a p -> p a")).then_inc(
                        s["b1_loaded"], 16)
            sp.dma_start(b2[0:1, :], g["d_b2"][one, :]).then_inc(s["b2_loaded"], 16)
            sp.dma_start(ln[:, 0:1], g["d_ln_g"][one, :].rearrange("a p -> p a")).then_inc(s["ln_loaded"], 16)
            sp.dma_start(ln[:, 1:2], g["d_ln_b"][one, :].rearrange("a p -> p a")).then_inc(s["ln_loaded"], 16)

        @block.vector
        def _(dve):
            dve.wait_ge(s["before_ready"], 64 * layer + 64)
            dve.wait_ge(s["first_row_zero"], layer + 1)
            dve.wait_ge(s["b1_loaded"], 96 * layer + 96)
            settle(dve, g["passed"])
            with dve.Fori(0, STEPS) as it:
                n = n0 + it
                ch = Chain(dve, s["dve_chain"], n, 4)
                for u in range(2):
                    for j in range(GROUP):
                        b = 2 * GROUP * it + (GROUP * u + j)
                        dve.bn_stats(stats[u][:, j, 0, :], z_all[:, b, 0:WD])
                        last = dve.bn_stats(stats[u][:, j, 1, :], before[:, b, :])
                    ch.tag(last)
                    ch.wait()
                    settle(dve, g["passed"])
                    for j in range(GROUP):
                        last = dve.bn_aggr(mv[u][:, j, :], stats[u][:, j, :, :].rearrange("p a b -> p (a b)"))
                    last.then_inc(s["stats_ready"], 1)
                for u in range(2):
                    dve.wait_ge(s["rstd_ready"], n * 2 + u + 1)
                    for j in range(GROUP):
                        b = 2 * GROUP * it + (GROUP * u + j)
                        dve.tensor_scalar(hn[u][:, j, 0:WD], z_all[:, b, 0:WD], mv[u][:, j, 0:1], rstd[u][:, j:j + 1],
                                          ALU.subtract, ALU.mult)
                        last = dve.tensor_scalar(hn[u][:, j, WD:P], before[:, b, :], mv[u][:, j, 0:1],
                                                 rstd[u][:, j:j + 1], ALU.subtract, ALU.mult)
                    last.then_inc(s["hn_ready"], 1)
                for u in range(2):
                    for c, (at, rows) in enumerate(CHUNKS):
                        i = 3 * u + c
                        dve.wait_ge(s["lin_ready"], n * 6 + i + 1)
                        dve.wait_ge(s["gel_ready"], n * 6 + i + 1)
                        dve.scalar_tensor_tensor(out=gated[u][c][0:rows, :], in0=lin[i % 2][0:rows, :],
                                                 scalar=b1[0:rows, 0, c:c + 1], in1=gel[i % 2][0:rows, :],
                                                 op0=ALU.add, op1=ALU.mult).then_inc(s["gated_ready"], 1)
                for u in range(2):
                    dve.wait_ge(s["y_ready"], n * 2 + u + 1)
                    zs = z_all[:, bass.ds(2 * GROUP * it + GROUP * u, GROUP), :]
                    ch.tag(dve.tensor_tensor(zs, zs, y[u][:, :, :], ALU.add))
                ch.end()

        @block.gpsimd
        def _(pool):
            pool.memset(before[0:1, :, :], 0.0).then_inc(s["first_row_zero"], 1)
            with pool.Fori(0, STEPS) as it:
                n = n0 + it
                ch = Chain(pool, s["pool_chain"], n, 2)
                for u in range(2):
                    pool.wait_ge(s["stats_ready"], n * 2 + u + 1)
                    settle(pool, g["passed"])
                    ch.tag(pool.tensor_scalar(var_eps[u][:, :], mv[u][:, :, 1], EPS, 1.0, ALU.add, ALU.mult))
                    ch.wait()
                    pool.tensor_tensor(rstd[u][:, :], var_eps[u][:, :], g["minus_half"][:, 0:GROUP],
                                       ALU.pow).then_inc(s["rstd_ready"], 1)
                ch.end()

        @block.scalar
        def _(act):
            act.wait_ge(s["ln_loaded"], 32 * layer + 32)
            act.wait_ge(s["b1_loaded"], 96 * layer + 96)
            settle(act, g["passed"])
            with act.Fori(0, STEPS) as it:
                n = n0 + it
                for u in range(2):
                    act.wait_ge(s["turn_ready"], n * 2 + u + 1)
                    act.activation(hT[u][:, :], turn[u][:, :], ACT.Identity, scale=ln[:, 0:1],
                                   bias=ln[:, 1:2]).then_inc(s["hT_ready"], 1)
                for i in range(6):
                    c, rows = i % 3, CHUNKS[i % 3][1]
                    act.wait_ge(s["gate_ready"], n * 6 + i + 1)
                    if i >= 2:
                        act.wait_ge(s["gated_ready"], n * 6 + i - 1)
                    act.activation(gel[i % 2][0:rows, :], gate[i % 2][0:rows, :], ACT.Gelu,
                                   bias=b1[0:rows, 1, c:c + 1]).then_inc(s["gel_ready"], 1)

        @block.tensor
        def _(pe):
            pe.wait_ge(s["w1_loaded"], 16 * layer + 16)
            pe.wait_ge(s["w2_loaded"], 48 * layer + 48)
            pe.wait_ge(s["b2_loaded"], 16 * layer + 16)
            settle(pe, g["passed"])
            with pe.Fori(0, STEPS) as it:
                n = n0 + it
                for u in range(2):
                    pe.wait_ge(s["hn_ready"], n * 2 + u + 1)
                    for j in range(GROUP):
                        last = pe.transpose(turn[u][:, j * P:(j + 1) * P], hn[u][:, j, :], ident)
                    last.then_inc(s["turn_ready"], 1)
                for u in range(2):
                    pe.wait_ge(s["hT_ready"], n * 2 + u + 1)
                    for c, (at, rows) in enumerate(CHUNKS):
                        i = 3 * u + c
                        if i >= 2:
                            pe.wait_ge(s["gel_ready"], n * 6 + i - 1)
                        pe.matmul(gate[i % 2][0:rows, :], w1[:, HID + at:HID + at + rows], hT[u][:, :], start=True,
                                  stop=True).then_inc(s["gate_ready"], 1)
                        if i >= 2:
                            pe.wait_ge(s["gated_ready"], n * 6 + i - 1)
                        pe.matmul(lin[i % 2][0:rows, :], w1[:, at:at + rows], hT[u][:, :], start=True,
                                  stop=True).then_inc(s["lin_ready"], 1)
                for u in range(2):
                    pe.wait_ge(s["gated_ready"], n * 6 + 3 * u + 3)
                    for j in range(GROUP):
                        pe.matmul(y[u][:, j, :], ones_row[0:1, :], b2[0:1, :], start=True, stop=False)
                        for c, (at, rows) in enumerate(CHUNKS):
                            last = pe.matmul(y[u][:, j, :], gated[u][c][0:rows, j * P:(j + 1) * P], w2[0:rows, c, :],
                                             start=False, stop=(c == 2))
                    last.then_inc(s["y_ready"], 1)


def expert_stage(nc, g, out):
    with ExitStack() as ctx:
        def sb(name, shape, dt):
            return ctx.enter_context(nc.sbuf_tensor("x_" + name, shape, dt))

        def ps(name, shape, dt):
            return ctx.enter_context(nc.psum_tensor("x_" + name, shape, dt))

        def sem(name):
            return ctx.enter_context(nc.semaphore("x_" + name))

        x_all, cf, ones_row = g["x"], g["cf"], g["ones_row"]
        ident, iota = cf[:, CF["ident"]], cf[:, CF["iota"]]
        N = GROUP * P
        E, ALL = EXPERTS, EXPERTS + 1
        w1, w2, b1, b2 = g["e_w1"], g["e_w2"], g["e_b1"], g["e_b2"]
        stats = [sb(f"stats{u}", [P, GROUP, 6], F32) for u in range(2)]
        mv = [sb(f"mv{u}", [P, GROUP, 2], F32) for u in range(2)]
        var_eps = [sb(f"var_eps{u}", [P, GROUP], F32) for u in range(2)]
        rstd = [sb(f"rstd{u}", [P, GROUP], F32) for u in range(2)]
        zn = [sb(f"zn{u}", [P, GROUP, P], F32) for u in range(2)]
        zT = [sb(f"zT{u}", [P, N], F32) for u in range(2)]
        top = [sb(f"top{u}", [P, GROUP], F32) for u in range(2)]
        less = [sb(f"less{u}", [P, GROUP, E], F32) for u in range(2)]
        raised = [sb(f"raised{u}", [P, GROUP, E], F32) for u in range(2)]
        total = [sb(f"total{u}", [P, GROUP], F32) for u in range(2)]
        inv_total = [sb(f"inv_total{u}", [P, GROUP], F32) for u in range(2)]
        prob = [sb(f"prob{u}", [P, GROUP, E], F32) for u in range(2)]
        sorted8 = [sb(f"sorted{u}", [P, GROUP, 8], F32) for u in range(2)]
        order = [sb(f"order{u}", [P, GROUP, 8], U32) for u in range(2)]
        orderf = [sb(f"orderf{u}", [P, GROUP, 8], F32) for u in range(2)]
        pick = [[sb(f"pick{u}{k}", [P, GROUP, E], F32) for k in range(2)] for u in range(2)]
        weight = [sb(f"weight{u}", [P, GROUP, ALL], F32) for u in range(2)]
        weightT = [sb(f"weightT{u}", [ALL, N], F32) for u in range(2)]
        hg = [sb(f"hg{i}", [P, N], F32) for i in range(3)]
        acc = [sb(f"acc{u}", [P, GROUP, P], F32) for u in range(2)]
        turn = [ps(f"turn{u}", [P, 512], F32) for u in range(2)]
        hid = [ps(f"hid{i}", [P, N], F32) for i in range(3)]
        y = [ps(f"y{i}", [P, GROUP, P], F32) for i in range(3)]

        stats_ready, rstd_ready = sem("stats_ready"), sem("rstd_ready")
        zn_ready, turn_ready, zT_ready = sem("zn_ready"), sem("turn_ready"), sem("zT_ready")
        logits_ready, less_ready, raised_ready = sem("logits_ready"), sem("less_ready"), sem("raised_ready")
        weight_ready, weightT_psum, weightT_ready = sem("weight_ready"), sem("weightT_psum"), sem("weightT_ready")
        hid_ready, hg_ready, y_ready, y_used = sem("hid_ready"), sem("hg_ready"), sem("y_ready"), sem("y_used")
        acc_free = [sem(f"acc_free{u}") for u in range(2)]
        dve_chain, pool_chain, shared_one = sem("dve_chain"), sem("pool_chain"), sem("shared_one")
        block = ctx.enter_context(nc.Block())

        @block.vector
        def _(dve):
            dve.sem_inc(y_used, 3)
            dve.wait_ge(shared_one, 2)
            with dve.Fori(0, STEPS) as it:
                ch = Chain(dve, dve_chain, it, 18)
                for u in range(2):
                    for j in range(GROUP):
                        last = dve.bn_stats(stats[u][:, j, :], x_all[:, 2 * GROUP * it + (GROUP * u + j), :])
                    ch.tag(last)
                    ch.wait()
                    settle(dve, g["passed"])
                    for j in range(GROUP):
                        last = dve.bn_aggr(mv[u][:, j, :], stats[u][:, j, :])
                    last.then_inc(stats_ready, 1)
                for u in range(2):
                    dve.wait_ge(rstd_ready, it * 2 + u + 1)
                    for j in range(GROUP):
                        last = dve.tensor_scalar(zn[u][:, j, :], x_all[:, 2 * GROUP * it + (GROUP * u + j), :],
                                                 mv[u][:, j, 0:1], rstd[u][:, j:j + 1], ALU.subtract, ALU.mult)
                    last.then_inc(zn_ready, 1)
                for u in range(2):
                    dve.wait_ge(logits_ready, it * 2 + u + 1)
                    logits = turn[u][:, 0:GROUP * E].rearrange("p (j e) -> p j e", e=E)
                    ch.tag(dve.tensor_reduce(top[u][:, :], logits, AX.X, ALU.max))
                    ch.wait()
                    dve.tensor_tensor(less[u][:, :, :], logits, top[u][:, :].unsqueeze(2).broadcast_to([P, GROUP, E]),
                                      ALU.subtract).then_inc(less_ready, 1)
                for u in range(2):
                    dve.wait_ge(raised_ready, it * 2 + u + 1)
                    ch.tag(dve.tensor_reduce(total[u][:, :], raised[u][:, :, :], AX.X, ALU.add))
                    ch.wait()
                    ch.tag(dve.reciprocal(inv_total[u][:, :], total[u][:, :]))
                    ch.wait()
                    ch.tag(dve.tensor_tensor(prob[u][:, :, :], raised[u][:, :, :],
                                             inv_total[u][:, :].unsqueeze(2).broadcast_to([P, GROUP, E]), ALU.mult))
                    ch.wait()
                    settle(dve, g["passed"])
                    for j in range(GROUP):
                        last = dve.max(sorted8[u][:, j, :], prob[u][:, j, :])
                    ch.tag(last)
                    ch.wait()
                    settle(dve, g["passed"])
                    for j in range(GROUP):
                        last = dve.max_index(order[u][:, j, :], sorted8[u][:, j, :], prob[u][:, j, :])
                    ch.tag(last)
                    ch.wait()
                    ch.tag(dve.tensor_copy(orderf[u][:, :, :], order[u][:, :, :]))
                    ch.wait()
                    for k in range(2):
                        for j in range(GROUP):
                            last = dve.scalar_tensor_tensor(out=pick[u][k][:, j, :], in0=iota,
                                                            scalar=orderf[u][:, j, k:k + 1], in1=prob[u][:, j, :],
                                                            op0=ALU.is_equal, op1=ALU.mult)
                    ch.tag(last)
                    ch.wait()
                    dve.tensor_tensor(weight[u][:, :, 0:E], pick[u][0][:, :, :], pick[u][1][:, :, :],
                                      ALU.add).then_inc(weight_ready, 1)
                dve.wait_ge(weight_ready, it * 2 + 2)
                for u in range(2):
                    dve.wait_ge(acc_free[u], 16 * it + 16)
                    for e in range(ALL):
                        k = ALL * u + e
                        dve.wait_ge(y_ready, it * 2 * ALL + k + 1)
                        if e:
                            dve.wait_ge(y_used, it * 2 * ALL + k + 3)
                        if e < E:
                            for j in range(GROUP):
                                before = x_all[:, 2 * GROUP * it + GROUP * u + j, :] if e == 0 else acc[u][:, j, :]
                                last = dve.scalar_tensor_tensor(out=acc[u][:, j, :], in0=y[k % 3][:, j, :],
                                                                scalar=weight[u][:, j, e:e + 1], in1=before,
                                                                op0=ALU.mult, op1=ALU.add)
                        else:
                            last = dve.tensor_tensor(acc[u][:, :, :], y[k % 3][:, :, :], acc[u][:, :, :], ALU.add)
                        last.then_inc(y_used, 1)
                ch.end()

        @block.gpsimd
        def _(pool):
            for u in range(2):
                pool.memset(weight[u][:, :, E:ALL], 1.0).then_inc(shared_one, 1)
            with pool.Fori(0, STEPS) as it:
                ch = Chain(pool, pool_chain, it, 2)
                for u in range(2):
                    pool.wait_ge(stats_ready, it * 2 + u + 1)
                    settle(pool, g["passed"])
                    ch.tag(pool.tensor_scalar(var_eps[u][:, :], mv[u][:, :, 1], EPS, 1.0, ALU.add, ALU.mult))
                    ch.wait()
                    pool.tensor_tensor(rstd[u][:, :], var_eps[u][:, :], g["minus_half"][:, 0:GROUP],
                                       ALU.pow).then_inc(rstd_ready, 1)
                ch.end()

        @block.sync
        def _(sp):
            for u in range(2):
                sp.sem_inc(acc_free[u], 16)
            with sp.Fori(0, STEPS) as it:
                for u in range(2):
                    sp.wait_ge(y_used, it * 2 * ALL + ALL * (u + 1) + 3)
                    sp.dma_start(out[bass.ds(2 * GROUP * it + GROUP * u, GROUP), :, :].rearrange("b t d -> t b d"),
                                 acc[u][:, :, :]).then_inc(acc_free[u], 16)
            for u in range(2):
                sp.wait_ge(acc_free[u], 16 * STEPS + 16)

        @block.scalar
        def _(act):
            with act.Fori(0, STEPS) as it:
                for u in range(2):
                    act.wait_ge(turn_ready, it * 2 + u + 1)
                    act.activation(zT[u][:, :], turn[u][:, :], ACT.Copy).then_inc(zT_ready, 1)
                for u in range(2):
                    act.wait_ge(less_ready, it * 2 + u + 1)
                    act.activation(raised[u][:, :, :], less[u][:, :, :], ACT.Exp).then_inc(raised_ready, 1)
                for u in range(2):
                    for e in range(ALL):
                        k = ALL * u + e
                        act.wait_ge(hid_ready, it * 2 * ALL + k + 1)
                        act.activation(hg[k % 3][:, :], hid[k % 3][:, :], ACT.Gelu,
                                       bias=b1[:, e:e + 1]).then_inc(hg_ready, 1)
                        if e == E - 3:
                            act.wait_ge(weightT_psum, it * 2 + u + 1)
                            act.activation(weightT[u][:, :], turn[u][0:ALL, :], ACT.Copy).then_inc(weightT_ready, 1)

        @block.tensor
        def _(pe):
            with pe.Fori(0, STEPS) as it:
                for u in range(2):
                    pe.wait_ge(zn_ready, it * 2 + u + 1)
                    for j in range(GROUP):
                        last = pe.transpose(turn[u][:, j * P:(j + 1) * P], zn[u][:, j, :], ident)
                    last.then_inc(turn_ready, 1)
                for u in range(2):
                    pe.wait_ge(zT_ready, it * 2 + u + 1)
                    for j in range(GROUP):
                        logits = turn[u][:, E * j:E * (j + 1)]
                        pe.matmul(logits, ones_row[0:1, :], g["e_gate_b"][0:1, :], start=True, stop=False)
                        last = pe.matmul(logits, zT[u][:, j * P:(j + 1) * P], g["e_gate_w"][:, :], start=False,
                                         stop=True)
                    last.then_inc(logits_ready, 1)

                def hidden(k):
                    pe.matmul(hid[k % 3][:, :], w1[:, k % ALL, :], zT[k // ALL][:, :], start=True,
                              stop=True).then_inc(hid_ready, 1)

                def project(k):
                    u, e = k // ALL, k % ALL
                    pe.wait_ge(hg_ready, it * 2 * ALL + k + 1)
                    pe.wait_ge(y_used, it * 2 * ALL + k + 1)
                    if e == E:
                        pe.wait_ge(weightT_ready, it * 2 + u + 1)
                    for j in range(GROUP):
                        if e == E:
                            pe.matmul(y[k % 3][:, j, :], weightT[u][:, j * P:(j + 1) * P], b2[:, :], start=True,
                                      stop=False)
                        last = pe.matmul(y[k % 3][:, j, :], hg[k % 3][:, j * P:(j + 1) * P], w2[:, e, :],
                                         start=(e < E), stop=True)
                    last.then_inc(y_ready, 1)

                for k in range(2 * ALL):
                    hidden(k)
                    if k >= 1:
                        project(k - 1)
                    if k % ALL == 4:
                        u = k // ALL
                        pe.wait_ge(weight_ready, it * 2 + u + 1)
                        for j in range(GROUP):
                            last = pe.transpose(turn[u][0:ALL, j * P:(j + 1) * P], weight[u][:, j, :], ident)
                        last.then_inc(weightT_psum, 1)
                project(2 * ALL - 1)


def program(nc, d, out):
    with ExitStack() as ctx:
        def sb(name, shape, dt=F32):
            return ctx.enter_context(nc.sbuf_tensor(name, shape, dt))

        def sem(name):
            return ctx.enter_context(nc.semaphore(name))

        g = {
            "x": sb("x_all", [P, NSEQ, P]), "z": sb("z_all", [P, NSEQ, P]), "ctx": sb("ctx_all", [P, NSEQ, P]),
            "cf": sb("consts_f32", [P, CF_COLS]), "cb": sb("consts_bf16", [P, CB_COLS], BF16),
            "ones_row": sb("ones_row", [1, P]), "minus_half": sb("minus_half", [P, 16]),
            "w_n1": sb("w_n1", [P, 5 * P]), "w_n2": sb("w_n2", [P, 4 * P]),
            "row_n1": sb("row_n1", [1, 2 * P]), "row_n2": sb("row_n2", [1, 4 * P]), "cols": sb("cols", [P, 3]),
            "e_w1": sb("e_w1", [P, EXPERTS + 1, P]), "e_w2": sb("e_w2", [P, EXPERTS + 1, P]),
            "e_b1": sb("e_b1", [P, EXPERTS + 1]), "e_b2": sb("e_b2", [EXPERTS + 1, P]),
            "e_gate_w": sb("e_gate_w", [P, EXPERTS]), "e_gate_b": sb("e_gate_b", [1, EXPERTS]),
            "mixed": sem("mixed"), "passed": sem("passed"),
            "d_wqkv": d["L0_ffn_wqkv"], "d_wo": d["L0_ffn_wo"], "d_qs": d["L0_ffn_q_scale"],
            "d_ks": d["L0_ffn_k_scale"], "d_w1": d["L0_ffn_w1"], "d_w2": d["L0_ffn_w2"], "d_b1": d["L0_ffn_b1"],
            "d_b2": d["L0_ffn_b2"], "d_ln_g": d["L0_ffn_ln_g"], "d_ln_b": d["L0_ffn_ln_b"],
        }
        loaded, set_up = sem("loaded"), sem("set_up")
        wide = {n: sem(n) for n in WIDE_SEMS}
        glu = {n: sem("m_" + n) for n in GLU_SEMS}

        with nc.Block() as block:
            @block.sync
            def _(sp):
                n = 0

                def load(dst, src):
                    nonlocal n
                    sp.dma_start(dst, src).then_inc(loaded, 16)
                    n += 16

                col = lambda name: d[name].rearrange("(p a) -> p a", a=1)
                row = lambda name: d[name].rearrange("(a p) -> a p", a=1)
                for k in range(4):
                    seqs = slice(NSEQ // 4 * k, NSEQ // 4 * (k + 1))
                    load(g["x"][:, seqs, :], d["x"][seqs, :, :].rearrange("b t d -> t b d"))
                    load(g["ctx"][:, seqs, :], d["ctx_1024"][seqs, :, :].rearrange("b t d -> t b d"))
                load(g["cf"][:, :], d["consts_f32"])
                load(g["cb"][:, :], d["consts_bf16"].bitcast(BF16))
                load(g["w_n1"][:, 0:3 * P], d["L0_xattn_WqkvT"])
                load(g["w_n1"][:, 3 * P:4 * P], d["L0_xattn_WoutT"])
                load(g["w_n1"][:, 4 * P:5 * P], d["L0_xattn_WgateT"])
                load(g["row_n1"][0:1, 0:P], row("L0_xattn_b_out"))
                load(g["row_n1"][0:1, P:2 * P], row("L0_xattn_b_gate"))
                for k, name in enumerate(("L0_xattn_gamma", "L0_xattn_beta", "L0_xattn_b_out")):
                    load(g["cols"][:, k:k + 1], col(name))
                for k, name in enumerate("qkvo"):
                    load(g["w_n2"][:, k * P:(k + 1) * P], d[f"L1_xattn_W{name}T"])
                    load(g["row_n2"][0:1, k * P:(k + 1) * P], row(f"L1_xattn_b{name}"))
                load(g["e_w1"][:, 0:EXPERTS, :], d["L1_ffn_w1"].rearrange("e d f -> d e f"))
                load(g["e_w1"][:, EXPERTS, :], d["L1_ffn_sw1"])
                load(g["e_w2"][:, 0:EXPERTS, :], d["L1_ffn_w2"].rearrange("e d f -> d e f"))
                load(g["e_w2"][:, EXPERTS, :], d["L1_ffn_sw2"])
                load(g["e_b1"][:, 0:EXPERTS], d["L1_ffn_b1T"])
                load(g["e_b1"][:, EXPERTS:EXPERTS + 1], col("L1_ffn_sb1"))
                load(g["e_b2"][0:EXPERTS, :], d["L1_ffn_b2"])
                load(g["e_b2"][EXPERTS:EXPERTS + 1, :], row("L1_ffn_sb2"))
                load(g["e_gate_w"][:, :], d["L1_ffn_gate_w"])
                load(g["e_gate_b"][0:1, :], row("L1_ffn_gate_b"))
                sp.wait_ge(loaded, n)

            @block.gpsimd
            def _(pool):
                pool.memset(g["ones_row"][:, :], 1.0).then_inc(set_up, 1)
                pool.memset(g["minus_half"][:, :], -0.5).then_inc(set_up, 1)
                pool.wait_ge(set_up, 2)

        narrow_stage(nc, g, True)
        norm_stage(nc, g)
        with nc.Fori(0, LAYERS) as layer:
            wide_stage(nc, g, layer, wide)
            glu_stage(nc, g, layer, glu)
        with nc.sbuf_tensor("mask_all", [P, NSEQ, P], I32) as mask_all, nc.semaphore("mask_loaded") as mask_loaded:
            g["mask"] = mask_all
            with nc.Block() as block:
                @block.sync
                def _(sp):
                    for k in range(4):
                        seqs = slice(NSEQ // 4 * k, NSEQ // 4 * (k + 1))
                        sp.dma_start(mask_all[:, seqs, :], d["mask"][seqs, 0, :, :].rearrange("b q k -> q b k")
                                     ).then_inc(mask_loaded, 16)
                    sp.wait_ge(mask_loaded, 64)
            narrow_stage(nc, g, False)
        expert_stage(nc, g, out)


def constants():
    f = np.float32
    cf = np.zeros((P, CF_COLS), f)
    cb = np.zeros((P, CB_COLS), f)
    cf[:, CF["ident"]] = np.eye(P)
    cb[:, CB["ident"]] = np.eye(P)
    t = np.arange(P, dtype=f)
    half = ND // 2
    freqs = t[:, None] * (f(1) / f(10000) ** (np.arange(0, ND, 2, dtype=f) / f(ND)))[None, :]
    c, s = np.cos(freqs).astype(f), np.sin(freqs).astype(f)
    c, s = np.tile(np.concatenate([c, c], 1), (1, NH)), np.tile(np.concatenate([-s, s], 1), (1, NH))
    cf[:, CF["rope_c"]] = np.concatenate([c * f(ND ** -0.5), c], 1)
    cf[:, CF["rope_s"]] = np.concatenate([s * f(ND ** -0.5), s], 1)
    idx = np.arange(0, WD, 2, dtype=f)
    freqs = t[:, None] * (f(1) / f(10000) ** (idx / f(WD)))[None, :]
    base = (idx + f(0.4 * WD)) / f(1.4 * WD)
    scale = base[None, :] ** ((t - P // 2) / f(32))[:, None]
    c, s = np.cos(freqs).astype(f), np.sin(freqs).astype(f)
    both = lambda a, b: np.concatenate([a, b], 1)
    cf[:, CF["xpos_c"]] = both(both(c * scale, c * scale) * f(8), both(c / scale, c / scale))
    cf[:, CF["xpos_s"]] = both(both(-s * scale, s * scale) * f(8), both(-s / scale, s / scale))
    cf[:, CF["iota"]] = np.arange(EXPERTS)
    dist = np.abs(t[None, :] - t[:, None])
    rest = (np.exp(-dist * f(0.1)) - dist * f(0.05)).astype(f)
    for n in range(3):
        term = (rest.view(np.uint32) & np.uint32(0xFFFF0000)).view(f)
        cb[:, CB["bias"].start + n * P:CB["bias"].start + (n + 1) * P] = term
        rest = rest - term
    i, j = np.arange(P)[:, None], np.arange(P)[None, :]
    band = np.where((i < j) | (i > j + 64), f(-2.0 ** 100), f(0))
    cb[:, CB["band"]] = band
    cb[:, CB["band_t"]] = band.T
    for name, heads in (("pick_n", NH), ("pick_w", WH)):
        pick = np.zeros((P, heads, P), f)
        for h in range(heads):
            pick[[h, heads + h], h, :] = 1
        cb[:, CB[name]] = pick.reshape(P, heads * P)
    return cf, (cb.view(np.uint32) >> 16).astype(np.uint16)


def kernel(**inputs):
    from concourse import bacc
    from concourse.bass_utils import run_bass_kernel_spmd

    arrays = {}
    for name, a in inputs.items():
        a = np.asarray(a)
        if name == "L0_xattn_Wqkv" or name in ("L0_xattn_Wout", "L0_xattn_Wgate") or \
                name.startswith("L1_xattn_W") or name == "L1_ffn_b1":
            name, a = name + "T", a.T
        if name.startswith("mask"):
            name = "mask"
        arrays[name] = np.ascontiguousarray(a)
    arrays["consts_f32"], arrays["consts_bf16"] = constants()

    nc = bacc.Bacc("TRN2", target_bir_lowering=False, num_devices=1)
    d = {name: nc.dram_tensor(f"in_{name}", a.shape, mybir.dt.from_np(a.dtype), kind="ExternalInput").ap()
         for name, a in arrays.items()}
    out = nc.dram_tensor("out", (NSEQ, P, P), F32, kind="ExternalOutput").ap()
    program(nc, d, out)
    result = run_bass_kernel_spmd(nc, [{f"in_{name}": a for name, a in arrays.items()}], core_ids=[0])
    return result.results[0]["out"]
```

```python
from contextlib import ExitStack

import concourse.bass as bass
import numpy as np
from concourse import mybir

F32 = mybir.dt.float32
BF16 = mybir.dt.bfloat16
I32 = mybir.dt.int32
U32 = mybir.dt.uint32
ALU = mybir.AluOpType
ACT = mybir.ActivationFunctionType
AX = mybir.AxisListType

P = 128
NSEQ = 32
PAIRS = NSEQ // 2
GROUP = 4
STEPS = NSEQ // GROUP // 2
NH, ND = 16, 8
WH, WD = 8, 64
SLOT = 64
LAYERS = 2
HID = 341
CHUNKS = [(0, 128), (128, 128), (256, HID - 256)]
EXPERTS = 8
EPS = 1e-5
MASKED = -1e9

CF = {}
_at = 0
for _name, _n in (("ident", P), ("rope_c", 2 * P), ("rope_s", 2 * P), ("xpos_c", 2 * WD), ("xpos_s", 2 * WD),
                  ("iota", EXPERTS)):
    CF[_name] = slice(_at, _at + _n)
    _at += _n
CF_COLS = _at
CB = {}
_at = 0
for _name, _n in (("ident", P), ("bias", 3 * P), ("band", P), ("band_t", P), ("pick_n", NH * P), ("pick_w", WH * P)):
    CB[_name] = slice(_at, _at + _n)
    _at += _n
CB_COLS = _at


def settle(eng, passed):
    eng.sem_inc(passed, 1)


class Chain:

    def __init__(self, eng, sem, step, per_step):
        self.eng, self.sem, self.base, self.per_step, self.n = eng, sem, step * per_step, per_step, 0

    def tag(self, ins):
        ins.then_inc(self.sem, 1)
        self.n += 1

    def wait(self):
        self.eng.wait_ge(self.sem, self.base + self.n)

    def end(self):
        assert self.n == self.per_step, (self.n, self.per_step)


def slot_head(slot):
    return 8 * (slot // 8) + 2 * (slot % 4) + slot % 8 // 4


def within(p, count):
    return not isinstance(p, int) or 0 <= p < count


def wait_of(eng, sem, p, per_step, k):
    if not isinstance(p, int) or p >= 0:
        eng.wait_ge(sem, p * per_step + k)


def run_steps(eng, step, count, ahead, behind):
    for it in range(-ahead, behind):
        step(it)
    with eng.Fori(behind, count - ahead) as it:
        step(it)
    for it in range(count - ahead, count + behind):
        step(it)


def narrow_stage(nc, g, first):
    tag = "n1_" if first else "n2_"
    with ExitStack() as ctx:
        def sb(name, shape, dt):
            return ctx.enter_context(nc.sbuf_tensor(tag + name, shape, dt))

        def ps(name, shape, dt):
            return ctx.enter_context(nc.psum_tensor(tag + name, shape, dt))

        used = []

        def sem(name):
            used.append(nc.alloc_semaphore(tag + name))
            return used[-1]

        x_all, z_all, ctx_all, cf, cb, ones_row = g["x"], g["z"], g["ctx"], g["cf"], g["cb"], g["ones_row"]
        xn_all = z_all
        ident, identb = cf[:, CF["ident"]], cb[:, CB["ident"]]
        bias3 = cb[:, CB["bias"]].rearrange("p (t k) -> p t k", t=3)
        pick = cb[0:2 * NH, CB["pick_n"]].rearrange("p (h k) -> p h k", h=NH)
        w = g["w_n1"] if first else g["w_n2"]
        wqkv, wout = w[:, 0:3 * P], w[:, 3 * P:4 * P]
        NORMS = 2 if first else 1

        stats = sb("stats", [P, 2, 2, 6], F32)
        mv = sb("mv", [P, 2, 2, 2], F32)
        var_eps = sb("var_eps", [P, 4], F32)
        rstd = sb("rstd", [P, 4], F32)
        minus_half = g["minus_half"]
        z_in = [sb(f"z_in{u}", [P, 2, P], F32) for u in range(2)]
        xT = [sb(f"xT{u}", [P, 2, P], F32) for u in range(2)]
        rot = [sb(f"rot{u}", [P, 2 * P], F32) for u in range(2)]
        rot_b = [sb(f"rot_b{u}", [P, 2 * P], F32) for u in range(2)]
        rest = [sb(f"rest{u}", [P, 2 * P], F32) for u in range(2)]
        rest2 = [sb(f"rest2{u}", [P, 2 * P], F32) for u in range(2)]
        stack = [sb(f"stack{u}", [P, 2, NH, SLOT], BF16) for u in range(2)]
        qT = [sb(f"qT{u}", [P, NH // 2, P], BF16) for u in range(2)]
        kT = [sb(f"kT{u}", [P, NH // 2, P], BF16) for u in range(2)]
        v_next = [sb(f"v_next{u}", [P, P], F32) for u in range(2)]
        vaug = [sb(f"vaug{u}", [P, NH, 32], F32) for u in range(2)]
        negmax = [sb(f"negmax{u}", [P, NH], F32) for u in range(2)]
        negrest = [sb(f"negrest{u}", [P, NH], F32) for u in range(2)]
        shift = [sb(f"shift{u}", [P, 2, NH], BF16) for u in range(2)]
        shiftT = [sb(f"shiftT{u}", [2 * NH, P], BF16) for u in range(2)]
        prob = [sb(f"prob{u}", [P, NH, P], F32) for u in range(2)]
        oT = [sb(f"oT{u}", [P, 4, P], F32) for u in range(2)]
        rsum = [sb(f"rsum{u}", [P, NH], F32) for u in range(2)]
        att = [sb(f"att{u}", [P, P], F32) for u in range(2)]
        attT = [sb(f"attT{u}", [P, P], F32) for u in range(2)]
        aoT = [sb(f"aoT{u}", [P, P], F32) for u in range(2)]
        gate = [sb(f"gate{u}", [P, P], F32) for u in range(2)]
        mix = [sb(f"mix{u}", [P, 3, P], F32) for u in range(2)]

        front = [ps(f"front{u}", [P, 512], F32) for u in range(2)]
        tile = [ps(f"tile{u}", [P, 1024], F32) for u in range(2)]
        obank = [ps(f"obank{u}", [P, 512], F32) for u in range(2)]

        stats_ready, rstd_ready = sem("stats_ready"), sem("rstd_ready")
        z_ready, ctx_ready = sem("z_ready"), sem("ctx_ready")
        zT_ready, xT_ready, qkv_ready, v_ready = sem("zT_ready"), sem("xT_ready"), sem("qkv_ready"), sem("v_ready")
        rot_ready, split_ready, vaug_ready = sem("rot_ready"), sem("split_ready"), sem("vaug_ready")
        stackT_ready, qT_ready, kT_ready = sem("stackT_ready"), sem("qT_ready"), sem("kT_ready")
        scores_ready, max_done = sem("scores_ready"), sem("max_done")
        shift_ready, shiftT_psum, shiftT_ready = sem("shift_ready"), sem("shiftT_psum"), sem("shiftT_ready")
        shifted_ready, exp_done, pv_ready = sem("shifted_ready"), sem("exp_done"), sem("pv_ready")
        oT_ready, o_ready, att_ready = sem("oT_ready"), sem("o_ready"), sem("att_ready")
        attT_psum, attT_ready, ao_ready, aoT_ready = sem("attT_psum"), sem("attT_ready"), sem("ao_ready"), sem("aoT_ready")
        gate_psum, gate_ready, x_done = sem("gate_psum"), sem("gate_ready"), sem("x_done")
        ones_set = sem("ones_set")
        dve_norm, dve_rot, dve_shift, dve_out = sem("dve_norm"), sem("dve_rot"), sem("dve_shift"), sem("dve_out")
        pool_norm, pool_split = sem("pool_norm"), sem("pool_split")

        def heads(ap, n=4):
            return ap.unsqueeze(1).broadcast_to([P, n, P])

        block = ctx.enter_context(nc.Block())

        @block.vector
        def _(dve):
            def norm_stats(p, ch):
                if not first:
                    for u in range(2):
                        xb = x_all[:, 2 * p + u, :]
                        ch.tag(dve.tensor_tensor(xb, xb, z_all[:, 2 * p + u, :], ALU.add))
                    ch.wait()
                    settle(dve, g["passed"])
                for u in range(2):
                    last = dve.bn_stats(stats[:, u, 0, :], x_all[:, 2 * p + u, :])
                    if first:
                        last = dve.bn_stats(stats[:, u, 1, :], ctx_all[:, 2 * p + u, :])
                ch.tag(last)
                ch.wait()
                settle(dve, g["passed"])
                for u in range(2):
                    last = dve.bn_aggr(mv[:, u, 0, :], stats[:, u, 0, :])
                    if first:
                        last = dve.bn_aggr(mv[:, u, 1, :], stats[:, u, 1, :])
                last.then_inc(stats_ready, 1)

            def norm_again(p, ch):
                dve.wait_ge(rstd_ready, p * 2 + 1)
                for u in range(2):
                    ch.tag(dve.tensor_scalar(xn_all[:, 2 * p + u, :], x_all[:, 2 * p + u, :], mv[:, u, 0, 0:1],
                                             rstd[:, 2 * u:2 * u + 1], ALU.subtract, ALU.mult))
                wait_of(dve, zT_ready, p - 1, 2, 2)
                for u in range(2):
                    dve.tensor_scalar(z_in[u][:, 1, :], ctx_all[:, 2 * p + u, :], mv[:, u, 1, 0:1],
                                      rstd[:, 2 * u + 1:2 * u + 2], ALU.subtract,
                                      ALU.mult).then_inc(ctx_ready, 1)
                ch.wait()
                settle(dve, g["passed"])
                for u in range(2):
                    last = dve.bn_stats(stats[:, u, 0, :], xn_all[:, 2 * p + u, :])
                ch.tag(last)
                ch.wait()
                settle(dve, g["passed"])
                for u in range(2):
                    last = dve.bn_aggr(mv[:, u, 0, :], stats[:, u, 0, :])
                last.then_inc(stats_ready, 1)

            def normed(p):
                dve.wait_ge(rstd_ready, p * NORMS + NORMS)
                wait_of(dve, zT_ready, p - 1, 2, 2)
                source = xn_all if first else x_all
                for u in range(2):
                    dve.tensor_scalar(z_in[u][:, 0, :], source[:, 2 * p + u, :], mv[:, u, 0, 0:1],
                                      rstd[:, 2 * u:2 * u + 1], ALU.subtract, ALU.mult).then_inc(z_ready, 1)

            def rotate(p):
                ch = Chain(dve, dve_rot, p, 4 if first else 0)
                for u in range(2):
                    dve.wait_ge(v_ready, p * 2 + u + 1)
                    wait_of(dve, split_ready, p - 1, 2, u + 1)
                    qk = front[u][:, 0:2 * P]
                    if first:
                        ch.tag(dve.tensor_tensor(rot[u][:, :], qk, cf[:, CF["rope_c"]], ALU.mult))
                        ch.tag(dve.tensor_tensor(
                            rot_b[u][:, :].rearrange("p (h t r) -> p h t r", t=2, r=4),
                            qk.rearrange("p (h t r) -> p h t r", t=2, r=4)[:, :, ::-1, :],
                            cf[:, CF["rope_s"]].rearrange("p (h t r) -> p h t r", t=2, r=4), ALU.mult))
                        ch.wait()
                        dve.tensor_tensor(rot[u][:, :], rot[u][:, :], rot_b[u][:, :],
                                          ALU.add).then_inc(rot_ready, 1)
                    else:
                        dve.tensor_scalar(rot[u][:, 0:P], qk[:, 0:P], g["q_scale"][:, 2 * p + u, :], None,
                                          ALU.mult)
                        dve.tensor_copy(rot[u][:, P:2 * P], qk[:, P:2 * P]).then_inc(rot_ready, 1)
                ch.end()

            def row_max(p, c, u):
                dve.wait_ge(scores_ready, p * 4 + 2 * c + u + 1)
                dve.tensor_reduce(negmax[u][:, 8 * c:8 * c + 8], tile[u][:, :].rearrange("p (h k) -> p h k", h=8),
                                  AX.X, ALU.max, negate=True).then_inc(max_done, 1)

            def shifts(p):
                ch = Chain(dve, dve_shift, p, 4)
                dve.wait_ge(max_done, p * 4 + 4)
                for u in range(2):
                    ch.tag(dve.tensor_copy(shift[u][:, 0, :], negmax[u][:, :]))
                ch.wait()
                for u in range(2):
                    ch.tag(dve.tensor_tensor(negrest[u][:, :], negmax[u][:, :], shift[u][:, 0, :], ALU.subtract))
                ch.wait()
                for u in range(2):
                    dve.tensor_copy(shift[u][:, 1, :], negrest[u][:, :]).then_inc(shift_ready, 1)
                for u in range(2):
                    dve.wait_ge(shiftT_psum, p * 2 + u + 1)
                    dve.tensor_copy(shiftT[u][:, :],
                                    tile[u][0:2 * NH, 0:64].bitcast(BF16)).then_inc(shiftT_ready, 1)
                ch.end()

            def divide(p, u, ch):
                dve.wait_ge(o_ready, p * 2 + u + 1)
                o = obank[u][:, :].rearrange("p (h r) -> p h r", r=32)
                ch.tag(dve.reciprocal(rsum[u][:, :], o[:, :, ND]))
                ch.wait()
                dve.tensor_tensor(att[u][:, :].rearrange("p (h r) -> p h r", r=ND), o[:, :, 0:ND],
                                  rsum[u][:, :].unsqueeze(2).broadcast_to([P, NH, ND]),
                                  ALU.mult).then_inc(att_ready, 1)

            def add_to_x(p, ch):
                for u in range(2):
                    xb = x_all[:, 2 * p + u, :]
                    if first:
                        xn = xn_all[:, 2 * p + u, :]
                        dve.wait_ge(gate_ready, p * 2 + u + 1)
                        ch.tag(dve.tensor_tensor(mix[u][:, 0, :], obank[u][:, 256:384], xn, ALU.subtract))
                        ch.wait()
                        ch.tag(dve.scalar_tensor_tensor(out=mix[u][:, 1, :], in0=gate[u][:, :], scalar=1.0,
                                                        in1=mix[u][:, 0, :], op0=ALU.add, op1=ALU.mult))
                        ch.wait()
                        ch.tag(dve.scalar_tensor_tensor(out=mix[u][:, 2, :], in0=mix[u][:, 1, :], scalar=0.5,
                                                        in1=xn, op0=ALU.mult, op1=ALU.add))
                        ch.wait()
                        dve.tensor_tensor(xb, xb, mix[u][:, 2, :], ALU.add).then_inc(x_done, 1)
                    else:
                        dve.wait_ge(ao_ready, p * 2 + u + 1)
                        dve.tensor_tensor(xb, xb, obank[u][:, P:2 * P], ALU.add).then_inc(x_done, 1)

            def step(it):
                norm, attend, after = it + 2, it, it - 1
                if within(norm, PAIRS):
                    ch_norm = Chain(dve, dve_norm, norm, 4 if first else 3)
                    norm_stats(norm, ch_norm)
                if within(attend, PAIRS):
                    for u in range(2):
                        dve.wait_ge(stackT_ready, attend * 2 + u + 1)
                        dve.tensor_copy(qT[u][:, :, :].rearrange("p h q -> p (h q)"),
                                        tile[u][:, 0:512].bitcast(BF16)).then_inc(qT_ready, 1)
                if within(after, PAIRS):
                    ch_out = Chain(dve, dve_out, after, 8 if first else 2)
                for u in range(2):
                    if within(attend, PAIRS):
                        row_max(attend, 0, u)
                    if within(after, PAIRS):
                        divide(after, u, ch_out)
                if within(attend, PAIRS):
                    for u in range(2):
                        row_max(attend, 1, u)
                    shifts(attend)
                if within(it + 1, PAIRS):
                    rotate(it + 1)
                if within(norm, PAIRS) and first:
                    norm_again(norm, ch_norm)
                if within(after, PAIRS):
                    add_to_x(after, ch_out)
                    ch_out.end()
                if within(norm, PAIRS):
                    normed(norm)
                    ch_norm.end()

            run_steps(dve, step, PAIRS, 2, 1)

        @block.gpsimd
        def _(pool):
            pairs = lambda buf: buf[:, 0:4].rearrange("p (u s) -> p u s", u=2)
            for u in range(2):
                pool.memset(stack[u][:, :, :, :], 0.0)
                pool.memset(vaug[u][:, :, :], 0.0).then_inc(ones_set, 1)
            pool.wait_ge(ones_set, 2)
            for u in range(2):
                pool.memset(vaug[u][:, :, ND:ND + 1], 1.0).then_inc(ones_set, 1)
            pool.wait_ge(ones_set, 4)

            def cast(out, src):
                return pool.tensor_scalar(out, src, 1.0, 0.0, ALU.mult, ALU.add)

            def inverse_deviation(p, n, ch):
                pool.wait_ge(stats_ready, p * NORMS + n + 1)
                settle(pool, g["passed"])
                of = slice(0, 2 if first else 1)
                ch.tag(pool.tensor_scalar(pairs(var_eps)[:, :, of], mv[:, :, of, 1], EPS, 1.0, ALU.add, ALU.mult))
                ch.wait()
                pool.tensor_tensor(pairs(rstd)[:, :, of], pairs(var_eps)[:, :, of], pairs(minus_half)[:, :, of],
                                   ALU.pow).then_inc(rstd_ready, 1)

            def split(p, u, ch):
                wait_of(pool, stackT_ready, p - 1, 2, u + 1)
                pool.wait_ge(rot_ready, p * 2 + u + 1)
                settle(pool, g["passed"])

                def slots(which, a, b, step=1):
                    v = stack[u][:, which, :, 0:6 * ND].rearrange("p h (s r) -> p h s r", r=ND)
                    return v[:, :, a:b:step, :]

                def part(buf, which, n):
                    v = buf[u][:, which * P:(which + 1) * P].rearrange("p (h r) -> p h r", r=ND)
                    return v.unsqueeze(2).broadcast_to([P, NH, n, ND])

                both = lambda s: stack[u][:, :, :, s * ND:(s + 1) * ND]
                whole = lambda buf: buf[u][:, :].rearrange("p (a h r) -> p a h r", a=2, r=ND)
                cast(slots(0, 0, 3), part(rot, 0, 3))
                cast(slots(1, 0, 4, 3), part(rot, 1, 2))
                ch.tag(cast(slots(1, 5, 6), part(rot, 1, 1)))
                ch.wait()
                ch.tag(pool.tensor_tensor(whole(rest), whole(rot), both(0), ALU.subtract))
                ch.wait()
                settle(pool, g["passed"])
                cast(slots(0, 3, 5), part(rest, 0, 2))
                ch.tag(cast(slots(1, 1, 5, 3), part(rest, 1, 2)))
                ch.wait()
                ch.tag(pool.tensor_tensor(whole(rest2), whole(rest), both(4), ALU.subtract))
                ch.wait()
                settle(pool, g["passed"])
                cast(slots(0, 5, 6), part(rest2, 0, 1))
                cast(slots(1, 2, 3), part(rest2, 1, 1)).then_inc(split_ready, 1)

            def step(it):
                norm, project = it + 2, it + 1
                if within(it, PAIRS):
                    for u in range(2):
                        pool.wait_ge(v_ready, it * 2 + u + 1)
                        wait_of(pool, pv_ready, it - 1, 2, u + 1)
                        settle(pool, g["passed"])
                        cast(vaug[u][:, :, 0:ND],
                             v_next[u][:, :].rearrange("p (h r) -> p h r", r=ND)).then_inc(vaug_ready, 1)
                if within(norm, PAIRS):
                    ch_norm = Chain(pool, pool_norm, norm, NORMS)
                    inverse_deviation(norm, 0, ch_norm)
                if within(project, PAIRS):
                    ch_split = Chain(pool, pool_split, project, 8)
                    split(project, 0, ch_split)
                if within(norm, PAIRS) and first:
                    inverse_deviation(norm, 1, ch_norm)
                if within(project, PAIRS):
                    split(project, 1, ch_split)
                    ch_split.end()
                if within(norm, PAIRS):
                    ch_norm.end()

            run_steps(pool, step, PAIRS, 2, 1)

        @block.scalar
        def _(act):
            def step(it):
                norm, project, after = it + 2, it + 1, it - 1
                if within(it, PAIRS):
                    for u in range(2):
                        act.wait_ge(stackT_ready, it * 2 + u + 1)
                        act.activation(kT[u][:, :, :].rearrange("p h k -> p (h k)"),
                                       tile[u][:, 512:1024].bitcast(BF16), ACT.Copy).then_inc(kT_ready, 1)
                if within(project, PAIRS):
                    for u in range(2):
                        act.wait_ge(zT_ready, project * 2 + u + 1)
                        zT = front[u][:, 0:2 * P]
                        out = xT[u][:, :, :].rearrange("p s t -> p (s t)")
                        if first:
                            act.activation(out, zT, ACT.Identity, scale=g["cols"][:, 0:1],
                                           bias=g["cols"][:, 1:2]).then_inc(xT_ready, 1)
                        else:
                            act.activation(out, zT, ACT.Copy).then_inc(xT_ready, 1)
                    for u in range(2):
                        act.wait_ge(qkv_ready, project * 2 + u + 1)
                        wait_of(act, vaug_ready, project - 1, 2, u + 1)
                        act.activation(v_next[u][:, :], front[u][:, 2 * P:3 * P], ACT.Copy).then_inc(v_ready, 1)
                if within(norm, PAIRS) and not first:
                    wait_of(act, zT_ready, norm - 1, 2, 2)
                    for u in range(2):
                        act.activation(z_in[u][:, 1, :], ctx_all[:, 2 * norm + u, :], ACT.Copy).then_inc(ctx_ready, 1)
                if within(after, PAIRS):
                    for u in range(2):
                        act.wait_ge(attT_psum, after * 2 + u + 1)
                        act.activation(attT[u][:, :], obank[u][:, 0:P], ACT.Copy).then_inc(attT_ready, 1)
                    if first:
                        for u in range(2):
                            act.wait_ge(ao_ready, after * 2 + u + 1)
                            act.activation(aoT[u][:, :], obank[u][:, P:2 * P], ACT.Identity,
                                           bias=g["cols"][:, 2:3]).then_inc(aoT_ready, 1)
                        for u in range(2):
                            act.wait_ge(gate_psum, after * 2 + u + 1)
                            act.activation(gate[u][:, :], obank[u][:, 384:512], ACT.Tanh,
                                           scale=0.5).then_inc(gate_ready, 1)
                if within(it, PAIRS):
                    for c in range(2):
                        for u in range(2):
                            act.wait_ge(shifted_ready, it * 4 + 2 * c + u + 1)
                            act.activation(prob[u][:, 8 * c:8 * c + 8, :].rearrange("p h q -> p (h q)"),
                                           tile[u][:, :], ACT.Exp).then_inc(exp_done, 1)
                    for u in range(2):
                        act.wait_ge(pv_ready, it * 2 + u + 1)
                        act.activation(oT[u][:, :, :].rearrange("p g q -> p (g q)"), obank[u][:, :],
                                       ACT.Copy).then_inc(oT_ready, 1)

            run_steps(act, step, PAIRS, 2, 1)

        @block.tensor
        def _(pe):
            def stack_pair(u, h):
                rows = slice(SLOT * (h % 2), SLOT * (h % 2) + SLOT)
                return qT[u][rows, h // 2, :], kT[u][rows, h // 2, :]

            def transpose_stack(p, u):
                pe.wait_ge(split_ready, p * 2 + u + 1)
                wait_of(pe, exp_done, p - 1, 4, 2 + u + 1)
                for which in range(2):
                    into = tile[u][:, 512 * which:512 * which + 512].bitcast(BF16)
                    for pair in range(NH // 2):
                        last = pe.transpose(into[:, pair * P:(pair + 1) * P],
                                            stack[u][:, which, 2 * pair:2 * pair + 2, :]
                                            .rearrange("p h s -> p (h s)"), identb)
                last.then_inc(stackT_ready, 1)

            def transpose_inputs(p, u):
                pe.wait_ge(z_ready, p * 2 + u + 1)
                pe.wait_ge(ctx_ready, p * 2 + u + 1)
                wait_of(pe, rot_ready, p - 1, 2, u + 1)
                pe.transpose(front[u][:, 0:P], z_in[u][:, 0, :], ident)
                pe.transpose(front[u][:, P:2 * P], z_in[u][:, 1, :], ident).then_inc(zT_ready, 1)

            def project_inputs(p, u):
                pe.wait_ge(xT_ready, p * 2 + u + 1)
                for which, at in ((0, 0), (1, P), (1, 2 * P)):
                    into = front[u][:, at:at + P]
                    if not first:
                        pe.matmul(into, ones_row[0:1, :], g["row_n2"][0:1, at:at + P], start=True, stop=False)
                    last = pe.matmul(into, xT[u][:, which, :], wqkv[:, at:at + P], start=first, stop=True)
                last.then_inc(qkv_ready, 1)

            def scores(p, u, c):
                if c == 0:
                    pe.wait_ge(qT_ready, p * 2 + u + 1)
                    pe.wait_ge(kT_ready, p * 2 + u + 1)
                else:
                    pe.wait_ge(max_done, p * 4 + u + 1)
                for half in range(2):
                    if not first:
                        pe.matmul(tile[u][:, 512 * half:512 * half + 512], identb,
                                  heads(g["neg_mask"][:, 2 * p + u, :]), start=True, stop=False,
                                  skip_group_check=True)
                for j in range(8):
                    slot = 4 * (j % 2) + j // 2
                    q, k = stack_pair(u, slot_head(8 * c + slot))
                    last = pe.matmul(tile[u][:, P * slot:P * (slot + 1)], q, k, start=first, stop=True,
                                     skip_group_check=True)
                last.then_inc(scores_ready, 1)

            def shifted_scores(p, u, c):
                if c == 0:
                    pe.wait_ge(shiftT_ready, p * 2 + u + 1)
                else:
                    pe.wait_ge(exp_done, p * 4 + u + 1)
                for half in range(2):
                    bank = tile[u][:, 512 * half:512 * half + 512]
                    if first:
                        for t in range(3):
                            pe.matmul(bank, identb, heads(bias3[:, t, :]), start=(t == 0), stop=False,
                                      skip_group_check=True)
                    else:
                        pe.matmul(bank, identb, heads(g["neg_maskT"][:, 2 * p + u, :]), start=True, stop=False,
                                  skip_group_check=True)
                for j in range(8):
                    slot = 4 * (j % 2) + j // 2
                    q, k = stack_pair(u, slot_head(8 * c + slot))
                    pe.matmul(tile[u][:, P * slot:P * (slot + 1)], k, q, start=False, stop=False,
                              skip_group_check=True)
                for slot in range(8):
                    last = pe.matmul(tile[u][:, P * slot:P * (slot + 1)], pick[:, 8 * c + slot, :],
                                     shiftT[u][:, :], start=False, stop=True, skip_group_check=True)
                last.then_inc(shifted_ready, 1)

            def values(p, u, c):
                if c == 0:
                    pe.wait_ge(vaug_ready, p * 2 + u + 1)
                    wait_of(pe, x_done, p - 1, 2, u + 1)
                else:
                    pe.wait_ge(exp_done, p * 4 + 2 + u + 1)
                for h in range(8 * c, 8 * c + 8):
                    row = 32 * (h % 4)
                    slot = 8 * c + 4 * (h % 2) + h % 8 // 2
                    last = pe.matmul(obank[u][row:row + 32, P * (h // 4):P * (h // 4) + P], vaug[u][:, h, :],
                                     prob[u][:, slot, :], start=True, stop=True)
                return last

            def turn_back(p, u):
                pe.wait_ge(oT_ready, p * 2 + u + 1)
                for n in range(4):
                    last = pe.transpose(obank[u][:, n * P:(n + 1) * P], oT[u][:, n, :], ident)
                last.then_inc(o_ready, 1)

            def transpose_attended(p, u):
                pe.wait_ge(att_ready, p * 2 + u + 1)
                pe.transpose(obank[u][:, 0:P], att[u][:, :], ident).then_inc(attT_psum, 1)

            def project_attended(p, u):
                pe.wait_ge(attT_ready, p * 2 + u + 1)
                if first:
                    pe.matmul(obank[u][:, 2 * P:3 * P], ones_row[0:1, :], g["row_n1"][0:1, 0:P],
                              start=True, stop=False)
                    pe.matmul(obank[u][:, 2 * P:3 * P], attT[u][:, :], wout, start=False, stop=True)
                    pe.matmul(obank[u][:, P:2 * P], wout, attT[u][:, :], start=True,
                              stop=True).then_inc(ao_ready, 1)
                else:
                    pe.matmul(obank[u][:, P:2 * P], ones_row[0:1, :], g["row_n2"][0:1, 3 * P:4 * P],
                              start=True, stop=False)
                    pe.matmul(obank[u][:, P:2 * P], attT[u][:, :], wout, start=False,
                              stop=True).then_inc(ao_ready, 1)

            def project_gate(p, u):
                pe.wait_ge(aoT_ready, p * 2 + u + 1)
                pe.matmul(obank[u][:, 384:512], ones_row[0:1, :], g["row_n1"][0:1, P:2 * P], start=True, stop=False)
                pe.matmul(obank[u][:, 384:512], aoT[u][:, :], w[:, 4 * P:5 * P], start=False,
                          stop=True).then_inc(gate_psum, 1)

            def step(it):
                project, after = it + 1, it - 1
                is_now, is_next, is_last = within(it, PAIRS), within(project, PAIRS), within(after, PAIRS)
                if is_now:
                    for u in range(2):
                        transpose_stack(it, u)
                if is_next:
                    for u in range(2):
                        transpose_inputs(project, u)
                for u in range(2):
                    if is_last:
                        turn_back(after, u)
                    if is_now:
                        scores(it, u, 0)
                for u in range(2):
                    if is_next:
                        project_inputs(project, u)
                    if is_now:
                        scores(it, u, 1)
                if is_last:
                    for u in range(2):
                        transpose_attended(after, u)
                    for u in range(2):
                        project_attended(after, u)
                if is_last and first:
                    for u in range(2):
                        project_gate(after, u)
                if is_now:
                    for u in range(2):
                        pe.wait_ge(shift_ready, it * 2 + u + 1)
                        pe.transpose(tile[u][0:2 * NH, 0:64].bitcast(BF16),
                                     shift[u][:, :, :].rearrange("p t h -> p (t h)"), identb).then_inc(shiftT_psum, 1)
                    for u in range(2):
                        shifted_scores(it, u, 0)
                    for u in range(2):
                        shifted_scores(it, u, 1)
                        values(it, u, 0)
                    for u in range(2):
                        values(it, u, 1).then_inc(pv_ready, 1)

            run_steps(pe, step, PAIRS, 2, 1)

    nc.clear_and_free_semaphores(used)
    nc.all_engine_barrier()


def norm_stage(nc, g):
    N = 2 * GROUP
    with ExitStack() as ctx:
        stats = ctx.enter_context(nc.sbuf_tensor("nz_stats", [P, N, 6], F32))
        mv = ctx.enter_context(nc.sbuf_tensor("nz_mv", [P, N, 2], F32))
        var_eps = ctx.enter_context(nc.sbuf_tensor("nz_var_eps", [P, N], F32))
        rstd = ctx.enter_context(nc.sbuf_tensor("nz_rstd", [P, N], F32))
        row_max = ctx.enter_context(nc.sbuf_tensor("nz_row_max", [P, NSEQ], F32))
        mask = [ctx.enter_context(nc.sbuf_tensor(f"nz_mask{k}", [P, N, P], I32)) for k in range(NSEQ // N)]
        turned = [ctx.enter_context(nc.psum_tensor(f"nz_turned{k}", [P, 512], F32)) for k in range(NSEQ // N)]
        stats_ready = ctx.enter_context(nc.semaphore("nz_stats_ready"))
        rstd_ready = ctx.enter_context(nc.semaphore("nz_rstd_ready"))
        dve_chain = ctx.enter_context(nc.semaphore("nz_dve_chain"))
        pool_chain = ctx.enter_context(nc.semaphore("nz_pool_chain"))
        mask_loaded = ctx.enter_context(nc.semaphore("nz_mask_loaded"))
        neg_mask_ready = ctx.enter_context(nc.semaphore("nz_neg_mask_ready"))
        row_max_ready = ctx.enter_context(nc.semaphore("nz_row_max_ready"))
        turned_ready = ctx.enter_context(nc.semaphore("nz_turned_ready"))
        block = ctx.enter_context(nc.Block())
        parts = [slice(N * k, N * (k + 1)) for k in range(NSEQ // N)]

        @block.sync
        def _(sp):
            for k, seqs in enumerate(parts):
                sp.dma_start(mask[k][:, :, :], g["d_mask"][seqs, 0, :, :].rearrange("b q k -> q b k")
                             ).then_inc(mask_loaded, 16)

        @block.vector
        def _(dve):
            with dve.Fori(0, NSEQ // N) as it:
                ch = Chain(dve, dve_chain, it, 1)
                for n in range(N):
                    last = dve.bn_stats(stats[:, n, :], g["x"][:, N * it + n, :])
                ch.tag(last)
                ch.wait()
                settle(dve, g["passed"])
                for n in range(N):
                    last = dve.bn_aggr(mv[:, n, :], stats[:, n, :])
                last.then_inc(stats_ready, 1)
                dve.wait_ge(rstd_ready, it + 1)
                for n in range(N):
                    dve.tensor_scalar(g["z"][:, N * it + n, :], g["x"][:, N * it + n, :], mv[:, n, 0:1],
                                      rstd[:, n:n + 1], ALU.subtract, ALU.mult)
                ch.end()
            for k, seqs in enumerate(parts):
                dve.wait_ge(neg_mask_ready, k + 1)
                last = dve.tensor_reduce(row_max[:, seqs], g["neg_mask"][:, seqs, :], AX.X, ALU.max)
                last.then_inc(row_max_ready, 1)
            dve.wait_ge(row_max_ready, NSEQ // N)
            dve.tensor_scalar(g["q_scale"][:, :, 0], row_max[:, :], 0.0, float(ND) ** -0.5, ALU.is_equal, ALU.mult)

        @block.gpsimd
        def _(pool):
            with pool.Fori(0, NSEQ // N) as it:
                ch = Chain(pool, pool_chain, it, 1)
                pool.wait_ge(stats_ready, it + 1)
                settle(pool, g["passed"])
                ch.tag(pool.tensor_scalar(var_eps[:, :], mv[:, :, 1], EPS, 1.0, ALU.add, ALU.mult))
                ch.wait()
                pool.tensor_tensor(rstd[:, :], var_eps[:, :], g["minus_half"][:, 0:N], ALU.pow).then_inc(rstd_ready, 1)
                ch.end()
            for k, seqs in enumerate(parts):
                pool.wait_ge(mask_loaded, 16 * len(parts))
                pool.tensor_scalar(g["neg_mask"][:, seqs, :], mask[k][:, :, :], 0.0, MASKED, ALU.is_equal,
                                   ALU.mult).then_inc(neg_mask_ready, 1)

        @block.tensor
        def _(pe):
            for k, seqs in enumerate(parts):
                pe.wait_ge(neg_mask_ready, k + 1)
                for n in range(N):
                    last = pe.transpose(turned[k][:, :].bitcast(BF16)[:, n * P:(n + 1) * P],
                                        g["neg_mask"][:, N * k + n, :], g["cb"][:, CB["ident"]])
                last.then_inc(turned_ready, 1)

        @block.scalar
        def _(act):
            for k, seqs in enumerate(parts):
                act.wait_ge(turned_ready, k + 1)
                act.activation(g["neg_maskT"][:, seqs, :].rearrange("p n q -> p (n q)"),
                               turned[k][:, :].bitcast(BF16), ACT.Copy)


WIDE_SEMS = ["wqkv_loaded", "wo_loaded", "gain_loaded", "tables_ready", "dve_rot", "inv_sum_ready", "pool_norm", "zc_ready",
             "raw_ready", "square_ready", "norm2_ready", "half_turn_ready", "inv_norm_ready", "rot_ready",
             "scores_ready", "max_ready", "exp_done", "probT_psum", "probT_ready", "pv_ready", "att_ready",
             "out_ready", "z_done", "edge_ready", "zT_ready", "hT_ready", "qk_ready", "v_psum", "v_ready", "v_taken",
             "qkT_psum", "qkT_ready", "attT_psum", "attT_ready"]


def wide_stage(nc, g, layer, s):
    with ExitStack() as ctx:
        def sb(name, shape, dt):
            return ctx.enter_context(nc.sbuf_tensor("w_" + name, shape, dt))

        def ps(name, shape, dt):
            return ctx.enter_context(nc.psum_tensor("w_" + name, shape, dt))

        z_all, cf, cb = g["z"], g["cf"], g["cb"]
        ident, identb = cf[:, CF["ident"]], cb[:, CB["ident"]]
        band = cb[:, CB["band"]]
        IN = WH * WD
        wqkv = sb("wqkv", [P, 3 * IN], F32)
        wo = sb("wo", [P, 4, P], F32)
        qk_gain = sb("qk_gain", [P, 2, WD], F32)
        rot_c = sb("rot_c", [P, 2, WD], F32)
        rot_s = sb("rot_s", [P, 2, WD], F32)
        zc = [sb(f"zc{u}", [P, P], F32) for u in range(2)]
        hT = [sb(f"hT{u}", [P, P], F32) for u in range(2)]
        square = [sb(f"square{u}", [P, 2 * IN], F32) for u in range(2)]
        raw = [sb(f"raw{u}", [P, 2 * IN], F32) for u in range(2)]
        rot = [sb(f"rot{u}", [P, 2 * IN], F32) for u in range(2)]
        half_turn = [sb(f"half_turn{u}", [P, 2 * IN], F32) for u in range(2)]
        norm2 = [sb(f"norm2{u}", [P, 2 * WH], F32) for u in range(2)]
        clipped = [sb(f"clipped{u}", [P, 2 * WH], F32) for u in range(2)]
        inv_norm = [sb(f"inv_norm{u}", [P, 2 * WH], F32) for u in range(2)]
        qkT = [sb(f"qkT{u}", [P, WH, P], F32) for u in range(2)]
        v_next = [sb(f"v_next{u}", [P, IN], F32) for u in range(2)]
        value = [sb(f"value{u}", [P, WH, WD], F32) for u in range(2)]
        negmax = [sb(f"negmax{u}", [P, WH], F32) for u in range(2)]
        prob = [sb(f"prob{u}", [P, WH, P], F32) for u in range(2)]
        probT = [sb(f"probT{u}", [P, WH, P], F32) for u in range(2)]
        row_sum = [sb(f"row_sum{u}", [P, WH], F32) for u in range(2)]
        inv_sum = [sb(f"inv_sum{u}", [P, WH], F32) for u in range(2)]
        att = [sb(f"att{u}", [P, IN], F32) for u in range(2)]
        attT = [sb(f"attT{u}", [P, 4, P], F32) for u in range(2)]

        qk_bank = ps("qk_bank", [P, 2 * IN], F32)
        v_bank = ps("v_bank", [P, IN], F32)
        tile = [ps(f"tile{u}", [P, 1024], F32) for u in range(2)]
        obank = ps("obank", [P, 512], F32)

        block = ctx.enter_context(nc.Block())
        n0 = layer * PAIRS

        def wait(eng, name, p, per_step, k):
            if not isinstance(p, int) or p >= 0:
                eng.wait_ge(s[name], (n0 + p) * per_step + k)

        @block.sync
        def _(sp):
            one = bass.ds(layer, 1)
            sp.dma_start(wqkv[:, :], g["d_wqkv"][one, :, :].rearrange("a p n -> p (a n)")).then_inc(
                s["wqkv_loaded"], 16)
            sp.dma_start(wo[:, :, :], g["d_wo"][one, :, :].rearrange("a (c p) n -> p (a c) n", p=P)).then_inc(
                s["wo_loaded"], 16)
            for k, name in enumerate(("d_qs", "d_ks")):
                sp.dma_start(qk_gain[:, k, :], g[name][one, :].broadcast_to([P, WD])).then_inc(s["gain_loaded"], 16)

        @block.vector
        def _(dve):
            for u in range(2):
                dve.memset(hT[u][WD:P, 0:1], 0.0).then_inc(s["edge_ready"], 1)
            dve.wait_ge(s["gain_loaded"], 32 * layer + 32)
            gain = qk_gain[:, :, :].rearrange("p a (t r) -> p a t r", t=2)
            dve.tensor_tensor(rot_c[:, :, :], qk_gain[:, :, :],
                              cf[:, CF["xpos_c"]].rearrange("p (a r) -> p a r", a=2), ALU.mult)
            dve.tensor_tensor(rot_s[:, :, :].rearrange("p a (t r) -> p a t r", t=2), gain[:, :, ::-1, :],
                              cf[:, CF["xpos_s"]].rearrange("p (a t r) -> p a t r", a=2, t=2),
                              ALU.mult).then_inc(s["tables_ready"], 1)
            dve.wait_ge(s["tables_ready"], layer + 1)
            settle(dve, g["passed"])

            def norms_and_cosines(p, u, ch):
                wait(dve, "raw_ready", p, 2, u + 1)
                wait(dve, "qkT_psum", p - 1, 2, u + 1)
                for a in range(2):
                    by_head = lambda buf: buf[u][:, a * IN:(a + 1) * IN].rearrange("p (h r) -> p h r", h=WH)
                    last = dve.tensor_tensor(by_head(rot), by_head(raw),
                                             rot_c[:, a, :].unsqueeze(1).broadcast_to([P, WH, WD]), ALU.mult)
                ch.tag(last)

            def squared_norms(p, u):
                wait(dve, "square_ready", p, 2, u + 1)
                dve.tensor_reduce(norm2[u][:, :], square[u][:, :].rearrange("p (h r) -> p h r", r=WD), AX.X,
                                  ALU.add).then_inc(s["norm2_ready"], 1)

            def add_sines(p, u, ch):
                wait(dve, "half_turn_ready", p, 2, u + 1)
                ch.wait()
                ch.tag(dve.tensor_tensor(rot[u][:, :], rot[u][:, :], half_turn[u][:, :], ALU.add))

            def normalise(p, u, ch):
                ch.wait()
                wait(dve, "inv_norm_ready", p, 2, u + 1)
                by_head = rot[u][:, :].rearrange("p (h r) -> p h r", r=WD)
                dve.tensor_tensor(by_head, by_head, inv_norm[u][:, :].unsqueeze(2).broadcast_to([P, 2 * WH, WD]),
                                  ALU.mult).then_inc(s["rot_ready"], 1)

            def row_max(p, u):
                wait(dve, "scores_ready", p, 2, u + 1)
                dve.tensor_reduce(negmax[u][:, :], tile[u][:, :].rearrange("p (h k) -> p h k", h=WH), AX.X,
                                  ALU.max, negate=True).then_inc(s["max_ready"], 1)

            def take_probT(p, u):
                wait(dve, "probT_psum", p, 2, u + 1)
                dve.tensor_copy(probT[u][:, :, :].rearrange("p h q -> p (h q)"), tile[u][:, :]).then_inc(
                    s["probT_ready"], 1)
                dve.reciprocal(inv_sum[u][:, :], row_sum[u][:, :]).then_inc(s["inv_sum_ready"], 1)

            def divide(p, u):
                wait(dve, "pv_ready", p, 2, u + 1)
                wait(dve, "inv_sum_ready", p, 2, u + 1)
                by_head = lambda ap: ap.rearrange("p (j b r) -> p j b r", b=2, r=WD)
                sums = inv_sum[u][:, :].rearrange("p (b j) -> p j b", b=2)
                dve.tensor_tensor(by_head(att[u][:, :]), by_head(obank[:, :]),
                                  sums.unsqueeze(3).broadcast_to([P, WH // 2, 2, WD]),
                                  ALU.mult).then_inc(s["att_ready"], 1)

            def add_to_z(p, u):
                wait(dve, "out_ready", p, 2, u + 1)
                zb = z_all[:, 2 * p + u, :]
                dve.tensor_tensor(zb, zb, obank[:, 0:P], ALU.add).then_inc(s["z_done"], 1)

            def step(it):
                project, after = it + 1, it - 1
                is_now, is_next, is_last = within(it, PAIRS), within(project, PAIRS), within(after, PAIRS)
                if is_next:
                    ch = Chain(dve, s["dve_rot"], n0 + project, 4)
                    norms_and_cosines(project, 0, ch)
                    squared_norms(project, 0)
                if is_last:
                    divide(after, 0)
                if is_next:
                    add_sines(project, 0, ch)
                if is_now:
                    row_max(it, 0)
                if is_next:
                    normalise(project, 0, ch)
                if is_now:
                    row_max(it, 1)
                if is_last:
                    add_to_z(after, 0)
                if is_next:
                    norms_and_cosines(project, 1, ch)
                if is_last:
                    divide(after, 1)
                if is_now:
                    take_probT(it, 0)
                if is_next:
                    squared_norms(project, 1)
                if is_last:
                    add_to_z(after, 1)
                if is_now:
                    take_probT(it, 1)
                if is_next:
                    add_sines(project, 1, ch)
                    normalise(project, 1, ch)
                    ch.end()

            run_steps(dve, step, PAIRS, 1, 1)

        @block.gpsimd
        def _(pool):
            pool.wait_ge(s["tables_ready"], layer + 1)
            settle(pool, g["passed"])

            def half_turns(p, u):
                wait(pool, "raw_ready", p, 2, u + 1)
                for a in range(2):
                    for t in range(2):
                        half = lambda buf, t: buf[u][:, a * IN:(a + 1) * IN].rearrange(
                            "p (h t r) -> p h t r", h=WH, t=2)[:, :, t, :]
                        table = rot_s[:, a, t * WD // 2:(t + 1) * WD // 2].unsqueeze(1).broadcast_to(
                            [P, WH, WD // 2])
                        last = pool.tensor_tensor(half(half_turn, t), half(raw, 1 - t), table, ALU.mult)
                last.then_inc(s["half_turn_ready"], 1)

            def take_values(p, u):
                wait(pool, "v_ready", p, 2, u + 1)
                wait(pool, "pv_ready", p - 1, 2, u + 1)
                settle(pool, g["passed"])
                pool.tensor_scalar(value[u][:, :, :].rearrange("p h r -> p (h r)"), v_next[u][:, :], 1.0, 0.0,
                                   ALU.mult, ALU.add).then_inc(s["v_taken"], 1)

            def inverse_norms(p, u, ch):
                wait(pool, "norm2_ready", p, 2, u + 1)
                settle(pool, g["passed"])
                ch.tag(pool.tensor_scalar(clipped[u][:, :], norm2[u][:, :], 1e-24, 1.0, ALU.max, ALU.mult))
                ch.wait()
                pool.tensor_tensor(inv_norm[u][:, :], clipped[u][:, :], g["minus_half"][:, 0:2 * WH],
                                   ALU.pow).then_inc(s["inv_norm_ready"], 1)

            def step(it):
                project = it + 1
                if within(project, PAIRS):
                    ch = Chain(pool, s["pool_norm"], n0 + project, 2)
                for u in range(2):
                    if within(project, PAIRS):
                        half_turns(project, u)
                    if within(it, PAIRS):
                        take_values(it, u)
                    if within(project, PAIRS):
                        inverse_norms(project, u, ch)
                if within(project, PAIRS):
                    ch.end()

            run_steps(pool, step, PAIRS, 1, 1)

        @block.scalar
        def _(act):
            act.wait_ge(s["edge_ready"], 2 * layer + 2)
            settle(act, g["passed"])

            def copy_z(p, u):
                act.activation(zc[u][:, :], z_all[:, 2 * p + u, :], ACT.Copy).then_inc(s["zc_ready"], 1)

            def shift_tokens(p, u):
                wait(act, "zT_ready", p, 1, 1)
                at = P * u
                act.activation(hT[u][0:WD, :], v_bank[0:WD, at:at + P], ACT.Copy)
                act.activation(hT[u][WD:P, 1:P], v_bank[WD:P, at:at + P - 1], ACT.Copy).then_inc(s["hT_ready"], 1)

            def take_qk(p, u):
                wait(act, "qk_ready", p, 2, u + 1)
                wait(act, "rot_ready", p - 1, 2, u + 1)
                act.activation(raw[u][:, :], qk_bank[:, :], ACT.Copy).then_inc(s["raw_ready"], 1)
                act.activation(square[u][:, :], qk_bank[:, :], ACT.Square).then_inc(s["square_ready"], 1)

            def take_v(p, u):
                wait(act, "v_psum", p, 2, u + 1)
                wait(act, "v_taken", p - 1, 2, u + 1)
                act.activation(v_next[u][:, :], v_bank[:, :], ACT.Copy).then_inc(s["v_ready"], 1)

            def take_qkT(p, u):
                wait(act, "qkT_psum", p, 2, u + 1)
                act.activation(qkT[u][:, :, :].rearrange("p h k -> p (h k)"), tile[u][:, :],
                               ACT.Copy).then_inc(s["qkT_ready"], 1)

            def exponentials(p, u):
                wait(act, "max_ready", p, 2, u + 1)
                for slot in range(WH):
                    last = act.activation(prob[u][:, slot, :], tile[u][:, slot * P:(slot + 1) * P], ACT.Exp,
                                          bias=negmax[u][:, slot:slot + 1], accum_out=row_sum[u][:, slot:slot + 1])
                    if slot % 4 == 3:
                        last.then_inc(s["exp_done"], 1)

            def take_attT(p, u):
                wait(act, "attT_psum", p, 2, u + 1)
                act.activation(attT[u][:, :, :].rearrange("p c q -> p (c q)"), obank[:, :],
                               ACT.Copy).then_inc(s["attT_ready"], 1)

            def step(it):
                project, after = it + 1, it - 1
                is_now, is_next, is_last = within(it, PAIRS), within(project, PAIRS), within(after, PAIRS)
                if is_next:
                    for u in range(2):
                        copy_z(project, u)
                if is_now:
                    take_qkT(it, 0)
                if is_next:
                    for u in range(2):
                        shift_tokens(project, u)
                    take_qk(project, 0)
                if is_now:
                    take_qkT(it, 1)
                if is_next:
                    take_v(project, 0)
                if is_last:
                    take_attT(after, 0)
                if is_now:
                    for u in range(2):
                        exponentials(it, u)
                if is_next:
                    take_qk(project, 1)
                    take_v(project, 1)
                if is_last:
                    take_attT(after, 1)

            run_steps(act, step, PAIRS, 1, 1)

        @block.tensor
        def _(pe):
            pe.wait_ge(s["wqkv_loaded"], 16 * layer + 16)
            pe.wait_ge(s["wo_loaded"], 16 * layer + 16)
            settle(pe, g["passed"])

            def transpose_z(p):
                wait(pe, "v_ready", p - 1, 2, 2)
                for u in range(2):
                    wait(pe, "zc_ready", p, 2, u + 1)
                    last = pe.transpose(v_bank[:, u * P:(u + 1) * P], zc[u][:, :], ident)
                last.then_inc(s["zT_ready"], 1)

            def project_qkv(p, u):
                wait(pe, "hT_ready", p, 2, 2)
                if u == 0:
                    wait(pe, "square_ready", p - 1, 2, 2)
                else:
                    wait(pe, "square_ready", p, 2, 1)
                    wait(pe, "v_ready", p, 2, 1)
                for half in range(2):
                    last = pe.matmul(qk_bank[:, 512 * half:512 * half + 512], hT[u][:, :],
                                     wqkv[:, IN * half:IN * (half + 1)], start=True, stop=True)
                last.then_inc(s["qk_ready"], 1)
                pe.matmul(v_bank[:, :], hT[u][:, :], wqkv[:, 2 * IN:3 * IN], start=True,
                          stop=True).then_inc(s["v_psum"], 1)

            def transpose_qk(p, u):
                wait(pe, "rot_ready", p, 2, u + 1)
                wait(pe, "probT_ready", p - 1, 2, u + 1)
                for j in range(WH):
                    last = pe.transpose(tile[u][:, j * P:(j + 1) * P], rot[u][:, j * P:(j + 1) * P], ident)
                last.then_inc(s["qkT_psum"], 1)

            def scores(p, u):
                wait(pe, "qkT_ready", p, 2, u + 1)
                for half in range(2):
                    bank = tile[u][:, 512 * half:512 * half + 512]
                    pe.matmul(bank, identb, band.unsqueeze(1).broadcast_to([P, 4, P]), start=True, stop=False,
                              skip_group_check=True)
                for j in range(8):
                    slot = 4 * (j % 2) + j // 2
                    h = slot_head(slot)
                    rows = slice(WD * (h % 2), WD * (h % 2) + WD)
                    last = pe.matmul(tile[u][:, P * slot:P * (slot + 1)], qkT[u][rows, h // 2, :],
                                     qkT[u][rows, WH // 2 + h // 2, :], start=False, stop=True,
                                     skip_group_check=True)
                last.then_inc(s["scores_ready"], 1)

            def transpose_prob(p, u):
                for slot in range(WH):
                    if slot % 4 == 0:
                        wait(pe, "exp_done", p, 4, 2 * u + slot // 4 + 1)
                    last = pe.transpose(tile[u][:, slot * P:(slot + 1) * P], prob[u][:, slot, :], ident)
                last.then_inc(s["probT_psum"], 1)

            def times_values(p, u):
                wait(pe, "probT_ready", p, 2, u + 1)
                wait(pe, "v_taken", p, 2, u + 1)
                if u == 0:
                    wait(pe, "z_done", p - 1, 2, 2)
                else:
                    wait(pe, "z_done", p, 2, 1)
                for h in range(WH):
                    last = pe.matmul(obank[:, h * WD:(h + 1) * WD], probT[u][:, 4 * (h % 2) + h // 2, :],
                                     value[u][:, h, :], start=True, stop=True)
                last.then_inc(s["pv_ready"], 1)

            def transpose_attended(p, u):
                wait(pe, "att_ready", p, 2, u + 1)
                for c in range(4):
                    last = pe.transpose(obank[:, c * P:(c + 1) * P], att[u][:, c * P:(c + 1) * P], ident)
                last.then_inc(s["attT_psum"], 1)

            def project_attended(p, u):
                wait(pe, "attT_ready", p, 2, u + 1)
                for c in range(4):
                    last = pe.matmul(obank[:, 0:P], attT[u][:, c, :], wo[:, c, :], start=(c == 0), stop=(c == 3))
                last.then_inc(s["out_ready"], 1)

            def step(it):
                project, after = it + 1, it - 1
                is_now, is_next, is_last = within(it, PAIRS), within(project, PAIRS), within(after, PAIRS)
                if is_now:
                    transpose_qk(it, 0)
                if is_next:
                    transpose_z(project)
                    project_qkv(project, 0)
                if is_now:
                    transpose_qk(it, 1)
                if is_last:
                    times_values(after, 0)
                if is_now:
                    scores(it, 0)
                if is_last:
                    transpose_attended(after, 0)
                if is_now:
                    scores(it, 1)
                if is_last:
                    project_attended(after, 0)
                if is_next:
                    project_qkv(project, 1)
                if is_last:
                    times_values(after, 1)
                if is_now:
                    transpose_prob(it, 0)
                if is_last:
                    transpose_attended(after, 1)
                    project_attended(after, 1)
                if is_now:
                    transpose_prob(it, 1)

            run_steps(pe, step, PAIRS, 1, 1)


GLU_SEMS = ["before_ready", "w1_loaded", "w2_loaded", "b1_loaded", "b2_loaded", "ln_loaded", "first_row_zero",
            "dve_chain", "pool_chain", "stats_ready", "rstd_ready", "hn_ready", "lin_ready", "gel_ready",
            "gated_ready", "y_ready", "turn_ready", "hT_ready", "gate_ready"]


def glu_stage(nc, g, layer, s):
    with ExitStack() as ctx:
        def sb(name, shape, dt):
            return ctx.enter_context(nc.sbuf_tensor("m_" + name, shape, dt))

        def ps(name, shape, dt):
            return ctx.enter_context(nc.psum_tensor("m_" + name, shape, dt))

        z_all, cf, ones_row = g["z"], g["cf"], g["ones_row"]
        ident = cf[:, CF["ident"]]
        N = GROUP * P
        w1 = sb("w1", [P, 2 * HID], F32)
        w2 = sb("w2", [P, 3, P], F32)
        b1 = sb("b1", [P, 2, 3], F32)
        b2 = sb("b2", [1, P], F32)
        ln = sb("ln", [P, 2], F32)
        before = sb("before", [P, NSEQ, WD], F32)
        stats = [sb(f"stats{u}", [P, GROUP, 2, 6], F32) for u in range(2)]
        mv = [sb(f"mv{u}", [P, GROUP, 2], F32) for u in range(2)]
        var_eps = [sb(f"var_eps{u}", [P, GROUP], F32) for u in range(2)]
        rstd = [sb(f"rstd{u}", [P, GROUP], F32) for u in range(2)]
        hn = [sb(f"hn{u}", [P, GROUP, P], F32) for u in range(2)]
        hT = [sb(f"hT{u}", [P, N], F32) for u in range(2)]
        gel = [sb(f"gel{u}", [P, N], F32) for u in range(2)]
        gated = [[sb(f"gated{u}{c}", [P, N], F32) for c in range(3)] for u in range(2)]
        turn = [ps(f"turn{u}", [P, N], F32) for u in range(2)]
        gate = [ps(f"gate{i}", [P, N], F32) for i in range(2)]
        lin = [ps(f"lin{i}", [P, N], F32) for i in range(2)]
        y = [ps(f"y{u}", [P, GROUP, P], F32) for u in range(2)]
        block = ctx.enter_context(nc.Block())
        n0 = layer * STEPS

        @block.sync
        def _(sp):
            one = bass.ds(layer, 1)
            for k in range(4):
                seqs = slice(NSEQ // 4 * k, NSEQ // 4 * (k + 1))
                sp.dma_start(before[1:P, seqs, :], z_all[0:P - 1, seqs, WD:P]).then_inc(s["before_ready"], 16)
            sp.dma_start(w1[:, :], g["d_w1"][one, :, :].rearrange("a p n -> p (a n)")).then_inc(s["w1_loaded"], 16)
            for c, (at, n) in enumerate(CHUNKS):
                sp.dma_start(w2[0:n, c, :], g["d_w2"][one, at:at + n, :].rearrange("a p n -> p (a n)")).then_inc(
                    s["w2_loaded"], 16)
                for a in range(2):
                    sp.dma_start(b1[0:n, a, c:c + 1],
                                 g["d_b1"][one, a * HID + at:a * HID + at + n].rearrange("a p -> p a")).then_inc(
                        s["b1_loaded"], 16)
            sp.dma_start(b2[0:1, :], g["d_b2"][one, :]).then_inc(s["b2_loaded"], 16)
            sp.dma_start(ln[:, 0:1], g["d_ln_g"][one, :].rearrange("a p -> p a")).then_inc(s["ln_loaded"], 16)
            sp.dma_start(ln[:, 1:2], g["d_ln_b"][one, :].rearrange("a p -> p a")).then_inc(s["ln_loaded"], 16)

        @block.vector
        def _(dve):
            dve.wait_ge(s["before_ready"], 64 * layer + 64)
            dve.wait_ge(s["first_row_zero"], layer + 1)
            dve.wait_ge(s["b1_loaded"], 96 * layer + 96)
            settle(dve, g["passed"])
            with dve.Fori(0, STEPS) as it:
                n = n0 + it
                ch = Chain(dve, s["dve_chain"], n, 4)
                for u in range(2):
                    for j in range(GROUP):
                        b = 2 * GROUP * it + (GROUP * u + j)
                        dve.bn_stats(stats[u][:, j, 0, :], z_all[:, b, 0:WD])
                        last = dve.bn_stats(stats[u][:, j, 1, :], before[:, b, :])
                    ch.tag(last)
                    ch.wait()
                    settle(dve, g["passed"])
                    for j in range(GROUP):
                        last = dve.bn_aggr(mv[u][:, j, :], stats[u][:, j, :, :].rearrange("p a b -> p (a b)"))
                    last.then_inc(s["stats_ready"], 1)
                for u in range(2):
                    dve.wait_ge(s["rstd_ready"], n * 2 + u + 1)
                    for j in range(GROUP):
                        b = 2 * GROUP * it + (GROUP * u + j)
                        dve.tensor_scalar(hn[u][:, j, 0:WD], z_all[:, b, 0:WD], mv[u][:, j, 0:1], rstd[u][:, j:j + 1],
                                          ALU.subtract, ALU.mult)
                        last = dve.tensor_scalar(hn[u][:, j, WD:P], before[:, b, :], mv[u][:, j, 0:1],
                                                 rstd[u][:, j:j + 1], ALU.subtract, ALU.mult)
                    last.then_inc(s["hn_ready"], 1)
                for u in range(2):
                    for c, (at, rows) in enumerate(CHUNKS):
                        i = 3 * u + c
                        dve.wait_ge(s["lin_ready"], n * 6 + i + 1)
                        dve.wait_ge(s["gel_ready"], n * 6 + i + 1)
                        dve.scalar_tensor_tensor(out=gated[u][c][0:rows, :], in0=lin[i % 2][0:rows, :],
                                                 scalar=b1[0:rows, 0, c:c + 1], in1=gel[i % 2][0:rows, :],
                                                 op0=ALU.add, op1=ALU.mult).then_inc(s["gated_ready"], 1)
                for u in range(2):
                    dve.wait_ge(s["y_ready"], n * 2 + u + 1)
                    zs = z_all[:, bass.ds(2 * GROUP * it + GROUP * u, GROUP), :]
                    ch.tag(dve.tensor_tensor(zs, zs, y[u][:, :, :], ALU.add))
                ch.end()

        @block.gpsimd
        def _(pool):
            pool.memset(before[0:1, :, :], 0.0).then_inc(s["first_row_zero"], 1)
            with pool.Fori(0, STEPS) as it:
                n = n0 + it
                ch = Chain(pool, s["pool_chain"], n, 2)
                for u in range(2):
                    pool.wait_ge(s["stats_ready"], n * 2 + u + 1)
                    settle(pool, g["passed"])
                    ch.tag(pool.tensor_scalar(var_eps[u][:, :], mv[u][:, :, 1], EPS, 1.0, ALU.add, ALU.mult))
                    ch.wait()
                    pool.tensor_tensor(rstd[u][:, :], var_eps[u][:, :], g["minus_half"][:, 0:GROUP],
                                       ALU.pow).then_inc(s["rstd_ready"], 1)
                ch.end()

        @block.scalar
        def _(act):
            act.wait_ge(s["ln_loaded"], 32 * layer + 32)
            act.wait_ge(s["b1_loaded"], 96 * layer + 96)
            settle(act, g["passed"])
            with act.Fori(0, STEPS) as it:
                n = n0 + it
                for u in range(2):
                    act.wait_ge(s["turn_ready"], n * 2 + u + 1)
                    act.activation(hT[u][:, :], turn[u][:, :], ACT.Identity, scale=ln[:, 0:1],
                                   bias=ln[:, 1:2]).then_inc(s["hT_ready"], 1)
                for i in range(6):
                    c, rows = i % 3, CHUNKS[i % 3][1]
                    act.wait_ge(s["gate_ready"], n * 6 + i + 1)
                    if i >= 2:
                        act.wait_ge(s["gated_ready"], n * 6 + i - 1)
                    act.activation(gel[i % 2][0:rows, :], gate[i % 2][0:rows, :], ACT.Gelu,
                                   bias=b1[0:rows, 1, c:c + 1]).then_inc(s["gel_ready"], 1)

        @block.tensor
        def _(pe):
            pe.wait_ge(s["w1_loaded"], 16 * layer + 16)
            pe.wait_ge(s["w2_loaded"], 48 * layer + 48)
            pe.wait_ge(s["b2_loaded"], 16 * layer + 16)
            settle(pe, g["passed"])
            with pe.Fori(0, STEPS) as it:
                n = n0 + it
                for u in range(2):
                    pe.wait_ge(s["hn_ready"], n * 2 + u + 1)
                    for j in range(GROUP):
                        last = pe.transpose(turn[u][:, j * P:(j + 1) * P], hn[u][:, j, :], ident)
                    last.then_inc(s["turn_ready"], 1)
                for u in range(2):
                    pe.wait_ge(s["hT_ready"], n * 2 + u + 1)
                    for c, (at, rows) in enumerate(CHUNKS):
                        i = 3 * u + c
                        if i >= 2:
                            pe.wait_ge(s["gel_ready"], n * 6 + i - 1)
                        pe.matmul(gate[i % 2][0:rows, :], w1[:, HID + at:HID + at + rows], hT[u][:, :], start=True,
                                  stop=True).then_inc(s["gate_ready"], 1)
                        if i >= 2:
                            pe.wait_ge(s["gated_ready"], n * 6 + i - 1)
                        pe.matmul(lin[i % 2][0:rows, :], w1[:, at:at + rows], hT[u][:, :], start=True,
                                  stop=True).then_inc(s["lin_ready"], 1)
                for u in range(2):
                    pe.wait_ge(s["gated_ready"], n * 6 + 3 * u + 3)
                    for j in range(GROUP):
                        pe.matmul(y[u][:, j, :], ones_row[0:1, :], b2[0:1, :], start=True, stop=False)
                        for c, (at, rows) in enumerate(CHUNKS):
                            last = pe.matmul(y[u][:, j, :], gated[u][c][0:rows, j * P:(j + 1) * P], w2[0:rows, c, :],
                                             start=False, stop=(c == 2))
                    last.then_inc(s["y_ready"], 1)


def expert_stage(nc, g, out):
    with ExitStack() as ctx:
        def sb(name, shape, dt):
            return ctx.enter_context(nc.sbuf_tensor("x_" + name, shape, dt))

        def ps(name, shape, dt):
            return ctx.enter_context(nc.psum_tensor("x_" + name, shape, dt))

        def sem(name):
            return ctx.enter_context(nc.semaphore("x_" + name))

        x_all, cf, ones_row = g["x"], g["cf"], g["ones_row"]
        ident, iota = cf[:, CF["ident"]], cf[:, CF["iota"]]
        N = GROUP * P
        E, ALL = EXPERTS, EXPERTS + 1
        w1, w2, b1, b2 = g["e_w1"], g["e_w2"], g["e_b1"], g["e_b2"]
        stats = [sb(f"stats{u}", [P, GROUP, 6], F32) for u in range(2)]
        mv = [sb(f"mv{u}", [P, GROUP, 2], F32) for u in range(2)]
        var_eps = [sb(f"var_eps{u}", [P, GROUP], F32) for u in range(2)]
        rstd = [sb(f"rstd{u}", [P, GROUP], F32) for u in range(2)]
        zn = [sb(f"zn{u}", [P, GROUP, P], F32) for u in range(2)]
        zT = [sb(f"zT{u}", [P, N], F32) for u in range(2)]
        top = [sb(f"top{u}", [P, GROUP], F32) for u in range(2)]
        less = [sb(f"less{u}", [P, GROUP, E], F32) for u in range(2)]
        raised = [sb(f"raised{u}", [P, GROUP, E], F32) for u in range(2)]
        total = [sb(f"total{u}", [P, GROUP], F32) for u in range(2)]
        inv_total = [sb(f"inv_total{u}", [P, GROUP], F32) for u in range(2)]
        prob = [sb(f"prob{u}", [P, GROUP, E], F32) for u in range(2)]
        sorted8 = [sb(f"sorted{u}", [P, GROUP, 8], F32) for u in range(2)]
        order = [sb(f"order{u}", [P, GROUP, 8], U32) for u in range(2)]
        orderf = [sb(f"orderf{u}", [P, GROUP, 8], F32) for u in range(2)]
        pick = [[sb(f"pick{u}{k}", [P, GROUP, E], F32) for k in range(2)] for u in range(2)]
        weight = [sb(f"weight{u}", [P, GROUP, ALL], F32) for u in range(2)]
        weightT = [sb(f"weightT{u}", [ALL, N], F32) for u in range(2)]
        hg = [sb(f"hg{i}", [P, N], F32) for i in range(3)]
        acc = [sb(f"acc{u}", [P, GROUP, P], F32) for u in range(2)]
        turn = [ps(f"turn{u}", [P, 512], F32) for u in range(2)]
        hid = [ps(f"hid{i}", [P, N], F32) for i in range(3)]
        y = [ps(f"y{i}", [P, GROUP, P], F32) for i in range(3)]

        stats_ready, rstd_ready = sem("stats_ready"), sem("rstd_ready")
        zn_ready, turn_ready, zT_ready = sem("zn_ready"), sem("turn_ready"), sem("zT_ready")
        logits_ready, less_ready, raised_ready = sem("logits_ready"), sem("less_ready"), sem("raised_ready")
        weight_ready, weightT_psum, weightT_ready = sem("weight_ready"), sem("weightT_psum"), sem("weightT_ready")
        hid_ready, hg_ready, y_ready, y_used = sem("hid_ready"), sem("hg_ready"), sem("y_ready"), sem("y_used")
        acc_free = [sem(f"acc_free{u}") for u in range(2)]
        dve_chain, pool_chain, shared_one = sem("dve_chain"), sem("pool_chain"), sem("shared_one")
        block = ctx.enter_context(nc.Block())

        @block.vector
        def _(dve):
            dve.sem_inc(y_used, 3)
            dve.wait_ge(shared_one, 2)
            with dve.Fori(0, STEPS) as it:
                ch = Chain(dve, dve_chain, it, 18)
                for u in range(2):
                    for j in range(GROUP):
                        last = dve.bn_stats(stats[u][:, j, :], x_all[:, 2 * GROUP * it + (GROUP * u + j), :])
                    ch.tag(last)
                    ch.wait()
                    settle(dve, g["passed"])
                    for j in range(GROUP):
                        last = dve.bn_aggr(mv[u][:, j, :], stats[u][:, j, :])
                    last.then_inc(stats_ready, 1)
                for u in range(2):
                    dve.wait_ge(rstd_ready, it * 2 + u + 1)
                    for j in range(GROUP):
                        last = dve.tensor_scalar(zn[u][:, j, :], x_all[:, 2 * GROUP * it + (GROUP * u + j), :],
                                                 mv[u][:, j, 0:1], rstd[u][:, j:j + 1], ALU.subtract, ALU.mult)
                    last.then_inc(zn_ready, 1)
                for u in range(2):
                    dve.wait_ge(logits_ready, it * 2 + u + 1)
                    logits = turn[u][:, 0:GROUP * E].rearrange("p (j e) -> p j e", e=E)
                    ch.tag(dve.tensor_reduce(top[u][:, :], logits, AX.X, ALU.max))
                    ch.wait()
                    dve.tensor_tensor(less[u][:, :, :], logits, top[u][:, :].unsqueeze(2).broadcast_to([P, GROUP, E]),
                                      ALU.subtract).then_inc(less_ready, 1)
                for u in range(2):
                    dve.wait_ge(raised_ready, it * 2 + u + 1)
                    ch.tag(dve.tensor_reduce(total[u][:, :], raised[u][:, :, :], AX.X, ALU.add))
                    ch.wait()
                    ch.tag(dve.reciprocal(inv_total[u][:, :], total[u][:, :]))
                    ch.wait()
                    ch.tag(dve.tensor_tensor(prob[u][:, :, :], raised[u][:, :, :],
                                             inv_total[u][:, :].unsqueeze(2).broadcast_to([P, GROUP, E]), ALU.mult))
                    ch.wait()
                    settle(dve, g["passed"])
                    for j in range(GROUP):
                        last = dve.max(sorted8[u][:, j, :], prob[u][:, j, :])
                    ch.tag(last)
                    ch.wait()
                    settle(dve, g["passed"])
                    for j in range(GROUP):
                        last = dve.max_index(order[u][:, j, :], sorted8[u][:, j, :], prob[u][:, j, :])
                    ch.tag(last)
                    ch.wait()
                    ch.tag(dve.tensor_copy(orderf[u][:, :, :], order[u][:, :, :]))
                    ch.wait()
                    for k in range(2):
                        for j in range(GROUP):
                            last = dve.scalar_tensor_tensor(out=pick[u][k][:, j, :], in0=iota,
                                                            scalar=orderf[u][:, j, k:k + 1], in1=prob[u][:, j, :],
                                                            op0=ALU.is_equal, op1=ALU.mult)
                    ch.tag(last)
                    ch.wait()
                    dve.tensor_tensor(weight[u][:, :, 0:E], pick[u][0][:, :, :], pick[u][1][:, :, :],
                                      ALU.add).then_inc(weight_ready, 1)
                dve.wait_ge(weight_ready, it * 2 + 2)
                for u in range(2):
                    dve.wait_ge(acc_free[u], 16 * it + 16)
                    for e in range(ALL):
                        k = ALL * u + e
                        dve.wait_ge(y_ready, it * 2 * ALL + k + 1)
                        if e:
                            dve.wait_ge(y_used, it * 2 * ALL + k + 3)
                        if e < E:
                            for j in range(GROUP):
                                before = x_all[:, 2 * GROUP * it + GROUP * u + j, :] if e == 0 else acc[u][:, j, :]
                                last = dve.scalar_tensor_tensor(out=acc[u][:, j, :], in0=y[k % 3][:, j, :],
                                                                scalar=weight[u][:, j, e:e + 1], in1=before,
                                                                op0=ALU.mult, op1=ALU.add)
                        else:
                            last = dve.tensor_tensor(acc[u][:, :, :], y[k % 3][:, :, :], acc[u][:, :, :], ALU.add)
                        last.then_inc(y_used, 1)
                ch.end()

        @block.gpsimd
        def _(pool):
            for u in range(2):
                pool.memset(weight[u][:, :, E:ALL], 1.0).then_inc(shared_one, 1)
            with pool.Fori(0, STEPS) as it:
                ch = Chain(pool, pool_chain, it, 2)
                for u in range(2):
                    pool.wait_ge(stats_ready, it * 2 + u + 1)
                    settle(pool, g["passed"])
                    ch.tag(pool.tensor_scalar(var_eps[u][:, :], mv[u][:, :, 1], EPS, 1.0, ALU.add, ALU.mult))
                    ch.wait()
                    pool.tensor_tensor(rstd[u][:, :], var_eps[u][:, :], g["minus_half"][:, 0:GROUP],
                                       ALU.pow).then_inc(rstd_ready, 1)
                ch.end()

        @block.sync
        def _(sp):
            for u in range(2):
                sp.sem_inc(acc_free[u], 16)
            with sp.Fori(0, STEPS) as it:
                for u in range(2):
                    sp.wait_ge(y_used, it * 2 * ALL + ALL * (u + 1) + 3)
                    sp.dma_start(out[bass.ds(2 * GROUP * it + GROUP * u, GROUP), :, :].rearrange("b t d -> t b d"),
                                 acc[u][:, :, :]).then_inc(acc_free[u], 16)
            for u in range(2):
                sp.wait_ge(acc_free[u], 16 * STEPS + 16)

        @block.scalar
        def _(act):
            with act.Fori(0, STEPS) as it:
                for u in range(2):
                    act.wait_ge(turn_ready, it * 2 + u + 1)
                    act.activation(zT[u][:, :], turn[u][:, :], ACT.Copy).then_inc(zT_ready, 1)
                for u in range(2):
                    act.wait_ge(less_ready, it * 2 + u + 1)
                    act.activation(raised[u][:, :, :], less[u][:, :, :], ACT.Exp).then_inc(raised_ready, 1)
                for u in range(2):
                    for e in range(ALL):
                        k = ALL * u + e
                        act.wait_ge(hid_ready, it * 2 * ALL + k + 1)
                        act.activation(hg[k % 3][:, :], hid[k % 3][:, :], ACT.Gelu,
                                       bias=b1[:, e:e + 1]).then_inc(hg_ready, 1)
                        if e == E - 3:
                            act.wait_ge(weightT_psum, it * 2 + u + 1)
                            act.activation(weightT[u][:, :], turn[u][0:ALL, :], ACT.Copy).then_inc(weightT_ready, 1)

        @block.tensor
        def _(pe):
            with pe.Fori(0, STEPS) as it:
                for u in range(2):
                    pe.wait_ge(zn_ready, it * 2 + u + 1)
                    for j in range(GROUP):
                        last = pe.transpose(turn[u][:, j * P:(j + 1) * P], zn[u][:, j, :], ident)
                    last.then_inc(turn_ready, 1)
                for u in range(2):
                    pe.wait_ge(zT_ready, it * 2 + u + 1)
                    for j in range(GROUP):
                        logits = turn[u][:, E * j:E * (j + 1)]
                        pe.matmul(logits, ones_row[0:1, :], g["e_gate_b"][0:1, :], start=True, stop=False)
                        last = pe.matmul(logits, zT[u][:, j * P:(j + 1) * P], g["e_gate_w"][:, :], start=False,
                                         stop=True)
                    last.then_inc(logits_ready, 1)

                def hidden(k):
                    pe.matmul(hid[k % 3][:, :], w1[:, k % ALL, :], zT[k // ALL][:, :], start=True,
                              stop=True).then_inc(hid_ready, 1)

                def project(k):
                    u, e = k // ALL, k % ALL
                    pe.wait_ge(hg_ready, it * 2 * ALL + k + 1)
                    pe.wait_ge(y_used, it * 2 * ALL + k + 1)
                    if e == E:
                        pe.wait_ge(weightT_ready, it * 2 + u + 1)
                    for j in range(GROUP):
                        if e == E:
                            pe.matmul(y[k % 3][:, j, :], weightT[u][:, j * P:(j + 1) * P], b2[:, :], start=True,
                                      stop=False)
                        last = pe.matmul(y[k % 3][:, j, :], hg[k % 3][:, j * P:(j + 1) * P], w2[:, e, :],
                                         start=(e < E), stop=True)
                    last.then_inc(y_ready, 1)

                for k in range(2 * ALL):
                    hidden(k)
                    if k >= 1:
                        project(k - 1)
                    if k % ALL == 4:
                        u = k // ALL
                        pe.wait_ge(weight_ready, it * 2 + u + 1)
                        for j in range(GROUP):
                            last = pe.transpose(turn[u][0:ALL, j * P:(j + 1) * P], weight[u][:, j, :], ident)
                        last.then_inc(weightT_psum, 1)
                project(2 * ALL - 1)


def program(nc, d, out):
    with ExitStack() as ctx:
        def sb(name, shape, dt=F32):
            return ctx.enter_context(nc.sbuf_tensor(name, shape, dt))

        def sem(name):
            return ctx.enter_context(nc.semaphore(name))

        g = {
            "x": sb("x_all", [P, NSEQ, P]), "z": sb("z_all", [P, NSEQ, P]), "ctx": sb("ctx_all", [P, NSEQ, P]),
            "cf": sb("consts_f32", [P, CF_COLS]), "cb": sb("consts_bf16", [P, CB_COLS], BF16),
            "ones_row": sb("ones_row", [1, P]), "minus_half": sb("minus_half", [P, 16]),
            "w_n1": sb("w_n1", [P, 5 * P]), "w_n2": sb("w_n2", [P, 4 * P]),
            "row_n1": sb("row_n1", [1, 2 * P]), "row_n2": sb("row_n2", [1, 4 * P]), "cols": sb("cols", [P, 3]),
            "e_w1": sb("e_w1", [P, EXPERTS + 1, P]), "e_w2": sb("e_w2", [P, EXPERTS + 1, P]),
            "e_b1": sb("e_b1", [P, EXPERTS + 1]), "e_b2": sb("e_b2", [EXPERTS + 1, P]),
            "e_gate_w": sb("e_gate_w", [P, EXPERTS]), "e_gate_b": sb("e_gate_b", [1, EXPERTS]),
            "passed": sem("passed"),
            "neg_mask": sb("neg_mask", [P, NSEQ, P], BF16), "neg_maskT": sb("neg_maskT", [P, NSEQ, P], BF16),
            "q_scale": sb("q_scale", [P, NSEQ, 1]), "d_mask": d["mask"],
            "d_wqkv": d["L0_ffn_wqkv"], "d_wo": d["L0_ffn_wo"], "d_qs": d["L0_ffn_q_scale"],
            "d_ks": d["L0_ffn_k_scale"], "d_w1": d["L0_ffn_w1"], "d_w2": d["L0_ffn_w2"], "d_b1": d["L0_ffn_b1"],
            "d_b2": d["L0_ffn_b2"], "d_ln_g": d["L0_ffn_ln_g"], "d_ln_b": d["L0_ffn_ln_b"],
        }
        loaded, set_up = sem("loaded"), sem("set_up")
        wide = {n: sem(n) for n in WIDE_SEMS}
        glu = {n: sem("m_" + n) for n in GLU_SEMS}

        with nc.Block() as block:
            @block.sync
            def _(sp):
                n = 0

                def load(dst, src):
                    nonlocal n
                    sp.dma_start(dst, src).then_inc(loaded, 16)
                    n += 16

                col = lambda name: d[name].rearrange("(p a) -> p a", a=1)
                row = lambda name: d[name].rearrange("(a p) -> a p", a=1)
                for k in range(4):
                    seqs = slice(NSEQ // 4 * k, NSEQ // 4 * (k + 1))
                    load(g["x"][:, seqs, :], d["x"][seqs, :, :].rearrange("b t d -> t b d"))
                    load(g["ctx"][:, seqs, :], d["ctx_1024"][seqs, :, :].rearrange("b t d -> t b d"))
                load(g["cf"][:, :], d["consts_f32"])
                load(g["cb"][:, :], d["consts_bf16"].bitcast(BF16))
                load(g["w_n1"][:, 0:3 * P], d["L0_xattn_WqkvT"])
                load(g["w_n1"][:, 3 * P:4 * P], d["L0_xattn_WoutT"])
                load(g["w_n1"][:, 4 * P:5 * P], d["L0_xattn_WgateT"])
                load(g["row_n1"][0:1, 0:P], row("L0_xattn_b_out"))
                load(g["row_n1"][0:1, P:2 * P], row("L0_xattn_b_gate"))
                for k, name in enumerate(("L0_xattn_gamma", "L0_xattn_beta", "L0_xattn_b_out")):
                    load(g["cols"][:, k:k + 1], col(name))
                for k, name in enumerate("qkvo"):
                    load(g["w_n2"][:, k * P:(k + 1) * P], d[f"L1_xattn_W{name}T"])
                    load(g["row_n2"][0:1, k * P:(k + 1) * P], row(f"L1_xattn_b{name}"))
                load(g["e_w1"][:, 0:EXPERTS, :], d["L1_ffn_w1"].rearrange("e d f -> d e f"))
                load(g["e_w1"][:, EXPERTS, :], d["L1_ffn_sw1"])
                load(g["e_w2"][:, 0:EXPERTS, :], d["L1_ffn_w2"].rearrange("e d f -> d e f"))
                load(g["e_w2"][:, EXPERTS, :], d["L1_ffn_sw2"])
                load(g["e_b1"][:, 0:EXPERTS], d["L1_ffn_b1T"])
                load(g["e_b1"][:, EXPERTS:EXPERTS + 1], col("L1_ffn_sb1"))
                load(g["e_b2"][0:EXPERTS, :], d["L1_ffn_b2"])
                load(g["e_b2"][EXPERTS:EXPERTS + 1, :], row("L1_ffn_sb2"))
                load(g["e_gate_w"][:, :], d["L1_ffn_gate_w"])
                load(g["e_gate_b"][0:1, :], row("L1_ffn_gate_b"))
                sp.wait_ge(loaded, n)

            @block.gpsimd
            def _(pool):
                pool.memset(g["ones_row"][:, :], 1.0).then_inc(set_up, 1)
                pool.memset(g["minus_half"][:, :], -0.5).then_inc(set_up, 1)
                pool.wait_ge(set_up, 2)

        narrow_stage(nc, g, True)
        norm_stage(nc, g)
        with nc.Fori(0, LAYERS) as layer:
            wide_stage(nc, g, layer, wide)
            glu_stage(nc, g, layer, glu)
        narrow_stage(nc, g, False)
        expert_stage(nc, g, out)


def constants():
    f = np.float32
    cf = np.zeros((P, CF_COLS), f)
    cb = np.zeros((P, CB_COLS), f)
    cf[:, CF["ident"]] = np.eye(P)
    cb[:, CB["ident"]] = np.eye(P)
    t = np.arange(P, dtype=f)
    half = ND // 2
    freqs = t[:, None] * (f(1) / f(10000) ** (np.arange(0, ND, 2, dtype=f) / f(ND)))[None, :]
    c, s = np.cos(freqs).astype(f), np.sin(freqs).astype(f)
    c, s = np.tile(np.concatenate([c, c], 1), (1, NH)), np.tile(np.concatenate([-s, s], 1), (1, NH))
    cf[:, CF["rope_c"]] = np.concatenate([c * f(ND ** -0.5), c], 1)
    cf[:, CF["rope_s"]] = np.concatenate([s * f(ND ** -0.5), s], 1)
    idx = np.arange(0, WD, 2, dtype=f)
    freqs = t[:, None] * (f(1) / f(10000) ** (idx / f(WD)))[None, :]
    base = (idx + f(0.4 * WD)) / f(1.4 * WD)
    scale = base[None, :] ** ((t - P // 2) / f(32))[:, None]
    c, s = np.cos(freqs).astype(f), np.sin(freqs).astype(f)
    both = lambda a, b: np.concatenate([a, b], 1)
    cf[:, CF["xpos_c"]] = both(both(c * scale, c * scale) * f(8), both(c / scale, c / scale))
    cf[:, CF["xpos_s"]] = both(both(-s * scale, s * scale) * f(8), both(-s / scale, s / scale))
    cf[:, CF["iota"]] = np.arange(EXPERTS)
    dist = np.abs(t[None, :] - t[:, None])
    rest = (np.exp(-dist * f(0.1)) - dist * f(0.05)).astype(f)
    for n in range(3):
        term = (rest.view(np.uint32) & np.uint32(0xFFFF0000)).view(f)
        cb[:, CB["bias"].start + n * P:CB["bias"].start + (n + 1) * P] = term
        rest = rest - term
    i, j = np.arange(P)[:, None], np.arange(P)[None, :]
    band = np.where((i < j) | (i > j + 64), f(-2.0 ** 100), f(0))
    cb[:, CB["band"]] = band
    cb[:, CB["band_t"]] = band.T
    for name, heads in (("pick_n", NH), ("pick_w", WH)):
        pick = np.zeros((P, heads, P), f)
        for h in range(heads):
            pick[[h, heads + h], h, :] = 1
        cb[:, CB[name]] = pick.reshape(P, heads * P)
    return cf, (cb.view(np.uint32) >> 16).astype(np.uint16)


def kernel(**inputs):
    from concourse import bacc
    from concourse.bass_utils import run_bass_kernel_spmd

    arrays = {}
    for name, a in inputs.items():
        a = np.asarray(a)
        if name == "L0_xattn_Wqkv" or name in ("L0_xattn_Wout", "L0_xattn_Wgate") or \
                name.startswith("L1_xattn_W") or name == "L1_ffn_b1":
            name, a = name + "T", a.T
        if name.startswith("mask"):
            name = "mask"
        arrays[name] = np.ascontiguousarray(a)
    arrays["consts_f32"], arrays["consts_bf16"] = constants()

    nc = bacc.Bacc("TRN2", target_bir_lowering=False, num_devices=1)
    d = {name: nc.dram_tensor(f"in_{name}", a.shape, mybir.dt.from_np(a.dtype), kind="ExternalInput").ap()
         for name, a in arrays.items()}
    out = nc.dram_tensor("out", (NSEQ, P, P), F32, kind="ExternalOutput").ap()
    program(nc, d, out)
    result = run_bass_kernel_spmd(nc, [{f"in_{name}": a for name, a in arrays.items()}], core_ids=[0])
    return result.results[0]["out"]
```

```python
from contextlib import ExitStack

import concourse.bass as bass
import numpy as np
from concourse import mybir

F32 = mybir.dt.float32
BF16 = mybir.dt.bfloat16
I32 = mybir.dt.int32
U32 = mybir.dt.uint32
ALU = mybir.AluOpType
ACT = mybir.ActivationFunctionType
AX = mybir.AxisListType

P = 128
NSEQ = 32
PAIRS = NSEQ // 2
GROUP = 4
STEPS = NSEQ // GROUP // 2
NH, ND = 16, 8
WH, WD = 8, 64
SLOT = 64
LAYERS = 2
HID = 341
CHUNKS = [(0, 128), (128, 128), (256, HID - 256)]
EXPERTS = 8
EPS = 1e-5
MASKED = -1e9

CF = {}
_at = 0
for _name, _n in (("ident", P), ("rope_c", 2 * P), ("rope_s", 2 * P), ("xpos_c", 2 * WD), ("xpos_s", 2 * WD),
                  ("iota", EXPERTS)):
    CF[_name] = slice(_at, _at + _n)
    _at += _n
CF_COLS = _at
CB = {}
_at = 0
for _name, _n in (("ident", P), ("bias", 3 * P), ("band", P), ("band_t", P), ("pick_n", NH * P), ("pick_w", WH * P)):
    CB[_name] = slice(_at, _at + _n)
    _at += _n
CB_COLS = _at


def settle(eng, passed):
    eng.sem_inc(passed, 1)


class Chain:

    def __init__(self, eng, sem, step, per_step):
        self.eng, self.sem, self.base, self.per_step, self.n = eng, sem, step * per_step, per_step, 0

    def tag(self, ins):
        ins.then_inc(self.sem, 1)
        self.n += 1

    def wait(self):
        self.eng.wait_ge(self.sem, self.base + self.n)

    def end(self):
        assert self.n == self.per_step, (self.n, self.per_step)


def slot_head(slot):
    return 8 * (slot // 8) + 2 * (slot % 4) + slot % 8 // 4


def within(p, count):
    return not isinstance(p, int) or 0 <= p < count


def wait_of(eng, sem, p, per_step, k):
    if not isinstance(p, int) or p >= 0:
        eng.wait_ge(sem, p * per_step + k)


def run_steps(eng, step, count, ahead, behind):
    for it in range(-ahead, behind):
        step(it)
    with eng.Fori(behind, count - ahead) as it:
        step(it)
    for it in range(count - ahead, count + behind):
        step(it)


def narrow_stage(nc, g, first):
    tag = "n1_" if first else "n2_"
    with ExitStack() as ctx:
        def sb(name, shape, dt):
            return ctx.enter_context(nc.sbuf_tensor(tag + name, shape, dt))

        def ps(name, shape, dt):
            return ctx.enter_context(nc.psum_tensor(tag + name, shape, dt))

        used = []

        def sem(name):
            used.append(nc.alloc_semaphore(tag + name))
            return used[-1]

        x_all, z_all, ctx_all, cf, cb = g["x"], g["z"], g["ctx"], g["cf"], g["cb"]
        xn_all = z_all
        ident, identb = cf[:, CF["ident"]], cb[:, CB["ident"]]
        bias3 = cb[:, CB["bias"]].rearrange("p (t k) -> p t k", t=3)
        pick = cb[0:2 * NH, CB["pick_n"]].rearrange("p (h k) -> p h k", h=NH)
        w = g["w_n1"] if first else g["w_n2"]
        wqkv, wout = w[:, 0:3 * P], w[:, 3 * P:4 * P]
        NORMS = 2 if first else 1

        stats = sb("stats", [P, 2, 2, 6], F32)
        mv = sb("mv", [P, 2, 2, 2], F32)
        var_eps = sb("var_eps", [P, 4], F32)
        rstd = sb("rstd", [P, 4], F32)
        minus_half = g["minus_half"]
        z_in = [sb(f"z_in{u}", [P, 2, P], F32) for u in range(2)]
        xT = [sb(f"xT{u}", [P, 2, P], F32) for u in range(2)]
        rot = [sb(f"rot{u}", [P, 2 * P], F32) for u in range(2)]
        rot_b = [sb(f"rot_b{u}", [P, 2 * P], F32) for u in range(2)]
        rest = [sb(f"rest{u}", [P, 2 * P], F32) for u in range(2)]
        rest2 = [sb(f"rest2{u}", [P, 2 * P], F32) for u in range(2)]
        stack = [sb(f"stack{u}", [P, 2, NH, SLOT], BF16) for u in range(2)]
        qT = [sb(f"qT{u}", [P, NH // 2, P], BF16) for u in range(2)]
        kT = [sb(f"kT{u}", [P, NH // 2, P], BF16) for u in range(2)]
        v_next = [sb(f"v_next{u}", [P, P], F32) for u in range(2)]
        vaug = [sb(f"vaug{u}", [P, NH, 32], F32) for u in range(2)]
        negmax = [sb(f"negmax{u}", [P, NH], F32) for u in range(2)]
        negrest = [sb(f"negrest{u}", [P, NH], F32) for u in range(2)]
        shift = [sb(f"shift{u}", [P, 2, NH], BF16) for u in range(2)]
        shiftT = [sb(f"shiftT{u}", [2 * NH, P], BF16) for u in range(2)]
        prob = [sb(f"prob{u}", [P, NH, P], F32) for u in range(2)]
        oT = [sb(f"oT{u}", [P, 4, P], F32) for u in range(2)]
        rsum = [sb(f"rsum{u}", [P, NH], F32) for u in range(2)]
        att = [sb(f"att{u}", [P, P], F32) for u in range(2)]
        attT = [sb(f"attT{u}", [P, P], F32) for u in range(2)]
        aoT = [sb(f"aoT{u}", [P, P], F32) for u in range(2)]
        gate = [sb(f"gate{u}", [P, P], F32) for u in range(2)]
        with_out = [sb(f"with_out{u}", [P, P], F32) for u in range(2)]
        mix = [sb(f"mix{u}", [P, 3, P], F32) for u in range(2)]
        z_stats = sb("z_stats", [P, 2, 6], F32)
        z_mv = sb("z_mv", [P, 2, 2], F32)
        z_var_eps = sb("z_var_eps", [P, 2], F32)
        z_rstd = sb("z_rstd", [P, 2], F32)

        front = [ps(f"front{u}", [P, 512], F32) for u in range(2)]
        tile = [ps(f"tile{u}", [P, 1024], F32) for u in range(2)]
        obank = [ps(f"obank{u}", [P, 512], F32) for u in range(2)]

        stats_ready, rstd_ready = sem("stats_ready"), sem("rstd_ready")
        z_ready, ctx_ready = sem("z_ready"), sem("ctx_ready")
        zT_ready, xT_ready, qkv_ready, v_ready = sem("zT_ready"), sem("xT_ready"), sem("qkv_ready"), sem("v_ready")
        rot_ready, split_ready, vaug_ready = sem("rot_ready"), sem("split_ready"), sem("vaug_ready")
        stackT_ready, qT_ready, kT_ready = sem("stackT_ready"), sem("qT_ready"), sem("kT_ready")
        scores_ready, max_done = sem("scores_ready"), sem("max_done")
        shift_ready, shiftT_psum, shiftT_ready = sem("shift_ready"), sem("shiftT_psum"), sem("shiftT_ready")
        shifted_ready, exp_done, pv_ready = sem("shifted_ready"), sem("exp_done"), sem("pv_ready")
        oT_ready, o_ready, att_ready = sem("oT_ready"), sem("o_ready"), sem("att_ready")
        attT_psum, attT_ready, ao_ready, aoT_ready = sem("attT_psum"), sem("attT_ready"), sem("ao_ready"), sem("aoT_ready")
        gate_psum, gate_ready, x_done = sem("gate_psum"), sem("gate_ready"), sem("x_done")
        ones_set = sem("ones_set")
        dve_norm, dve_rot, dve_shift, dve_out = sem("dve_norm"), sem("dve_rot"), sem("dve_shift"), sem("dve_out")
        pool_norm, pool_split = sem("pool_norm"), sem("pool_split")
        z_stats_ready, z_rstd_ready = sem("z_stats_ready"), sem("z_rstd_ready")
        dve_z, pool_z = sem("dve_z"), sem("pool_z")

        def heads(ap, n=4):
            return ap.unsqueeze(1).broadcast_to([P, n, P])

        block = ctx.enter_context(nc.Block())
        if first:
            block.sync(g["load_all"])

        @block.vector
        def _(dve):
            def norm_stats(p, ch):
                if first and isinstance(p, int) and p == 0:
                    dve.wait_ge(g["first_quarter"], 32)
                if first and isinstance(p, int) and p == 2:
                    dve.wait_ge(g["other_quarters"], 96)
                if not first:
                    for u in range(2):
                        xb = x_all[:, 2 * p + u, :]
                        ch.tag(dve.tensor_tensor(xb, xb, z_all[:, 2 * p + u, :], ALU.add))
                    ch.wait()
                    settle(dve, g["passed"])
                for u in range(2):
                    last = dve.bn_stats(stats[:, u, 0, :], x_all[:, 2 * p + u, :])
                    if first:
                        last = dve.bn_stats(stats[:, u, 1, :], ctx_all[:, 2 * p + u, :])
                ch.tag(last)
                ch.wait()
                settle(dve, g["passed"])
                for u in range(2):
                    last = dve.bn_aggr(mv[:, u, 0, :], stats[:, u, 0, :])
                    if first:
                        last = dve.bn_aggr(mv[:, u, 1, :], stats[:, u, 1, :])
                last.then_inc(stats_ready, 1)

            def norm_again(p, ch):
                dve.wait_ge(rstd_ready, p * 2 + 1)
                for u in range(2):
                    ch.tag(dve.tensor_scalar(xn_all[:, 2 * p + u, :], x_all[:, 2 * p + u, :], mv[:, u, 0, 0:1],
                                             rstd[:, 2 * u:2 * u + 1], ALU.subtract, ALU.mult))
                wait_of(dve, zT_ready, p - 1, 2, 2)
                for u in range(2):
                    dve.tensor_scalar(z_in[u][:, 1, :], ctx_all[:, 2 * p + u, :], mv[:, u, 1, 0:1],
                                      rstd[:, 2 * u + 1:2 * u + 2], ALU.subtract,
                                      ALU.mult).then_inc(ctx_ready, 1)
                ch.wait()
                settle(dve, g["passed"])
                for u in range(2):
                    last = dve.bn_stats(stats[:, u, 0, :], xn_all[:, 2 * p + u, :])
                ch.tag(last)
                ch.wait()
                settle(dve, g["passed"])
                for u in range(2):
                    last = dve.bn_aggr(mv[:, u, 0, :], stats[:, u, 0, :])
                last.then_inc(stats_ready, 1)

            def normed(p):
                dve.wait_ge(rstd_ready, p * NORMS + NORMS)
                wait_of(dve, zT_ready, p - 1, 2, 2)
                source = xn_all if first else x_all
                for u in range(2):
                    dve.tensor_scalar(z_in[u][:, 0, :], source[:, 2 * p + u, :], mv[:, u, 0, 0:1],
                                      rstd[:, 2 * u:2 * u + 1], ALU.subtract, ALU.mult).then_inc(z_ready, 1)

            def rotate(p):
                ch = Chain(dve, dve_rot, p, 4 if first else 2)
                if first and isinstance(p, int) and p == 0:
                    dve.wait_ge(g["tables_loaded"], g["tables_count"])
                for u in range(2):
                    dve.wait_ge(v_ready, p * 2 + u + 1)
                    wait_of(dve, split_ready, p - 1, 2, u + 1)
                    qk = front[u][:, 0:2 * P]
                    if first:
                        ch.tag(dve.tensor_tensor(rot[u][:, :], qk, cf[:, CF["rope_c"]], ALU.mult))
                        ch.tag(dve.tensor_tensor(
                            rot_b[u][:, :].rearrange("p (h t r) -> p h t r", t=2, r=4),
                            qk.rearrange("p (h t r) -> p h t r", t=2, r=4)[:, :, ::-1, :],
                            cf[:, CF["rope_s"]].rearrange("p (h t r) -> p h t r", t=2, r=4), ALU.mult))
                        ch.wait()
                        dve.tensor_tensor(rot[u][:, :], rot[u][:, :], rot_b[u][:, :],
                                          ALU.add).then_inc(rot_ready, 1)
                    else:
                        ch.tag(dve.tensor_tensor(rot[u][:, :], qk, g["row_n2"][:, 0:2 * P], ALU.add))
                        ch.wait()
                        dve.tensor_scalar(rot[u][:, 0:P], rot[u][:, 0:P], g["q_scale"][:, 2 * p + u, :], None,
                                          ALU.mult).then_inc(rot_ready, 1)
                ch.end()

            def row_max(p, c, u):
                dve.wait_ge(scores_ready, p * 4 + 2 * c + u + 1)
                dve.tensor_reduce(negmax[u][:, 8 * c:8 * c + 8], tile[u][:, :].rearrange("p (h k) -> p h k", h=8),
                                  AX.X, ALU.max, negate=True).then_inc(max_done, 1)

            def shifts(p):
                ch = Chain(dve, dve_shift, p, 4)
                dve.wait_ge(max_done, p * 4 + 4)
                for u in range(2):
                    ch.tag(dve.tensor_copy(shift[u][:, 0, :], negmax[u][:, :]))
                ch.wait()
                for u in range(2):
                    ch.tag(dve.tensor_tensor(negrest[u][:, :], negmax[u][:, :], shift[u][:, 0, :], ALU.subtract))
                ch.wait()
                for u in range(2):
                    dve.tensor_copy(shift[u][:, 1, :], negrest[u][:, :]).then_inc(shift_ready, 1)
                for u in range(2):
                    dve.wait_ge(shiftT_psum, p * 2 + u + 1)
                    dve.tensor_copy(shiftT[u][:, :],
                                    tile[u][0:2 * NH, 0:64].bitcast(BF16)).then_inc(shiftT_ready, 1)
                ch.end()

            def divide(p, u, ch):
                dve.wait_ge(o_ready, p * 2 + u + 1)
                o = obank[u][:, :].rearrange("p (h r) -> p h r", r=32)
                ch.tag(dve.reciprocal(rsum[u][:, :], o[:, :, ND]))
                ch.wait()
                dve.tensor_tensor(att[u][:, :].rearrange("p (h r) -> p h r", r=ND), o[:, :, 0:ND],
                                  rsum[u][:, :].unsqueeze(2).broadcast_to([P, NH, ND]),
                                  ALU.mult).then_inc(att_ready, 1)

            def add_to_x(p, ch):
                for u in range(2):
                    xb = x_all[:, 2 * p + u, :]
                    if first:
                        xn = xn_all[:, 2 * p + u, :]
                        dve.wait_ge(gate_ready, p * 2 + u + 1)
                        ch.tag(dve.tensor_tensor(with_out[u][:, :], obank[u][:, 256:384], g["row_n1"][:, 0:P],
                                                 ALU.add))
                        ch.wait()
                        ch.tag(dve.tensor_tensor(mix[u][:, 0, :], with_out[u][:, :], xn, ALU.subtract))
                        ch.wait()
                        ch.tag(dve.scalar_tensor_tensor(out=mix[u][:, 1, :], in0=gate[u][:, :], scalar=1.0,
                                                        in1=mix[u][:, 0, :], op0=ALU.add, op1=ALU.mult))
                        ch.wait()
                        ch.tag(dve.scalar_tensor_tensor(out=mix[u][:, 2, :], in0=mix[u][:, 1, :], scalar=0.5,
                                                        in1=xn, op0=ALU.mult, op1=ALU.add))
                        ch.wait()
                        dve.tensor_tensor(xb, xb, mix[u][:, 2, :], ALU.add).then_inc(x_done, 1)
                    else:
                        dve.wait_ge(ao_ready, p * 2 + u + 1)
                        ch.tag(dve.tensor_tensor(mix[u][:, 0, :], obank[u][:, P:2 * P], g["row_n2"][:, 3 * P:4 * P],
                                                 ALU.add))
                        ch.wait()
                        dve.tensor_tensor(xb, xb, mix[u][:, 0, :], ALU.add).then_inc(x_done, 1)

            def z_norm_stats(p):
                ch = Chain(dve, dve_z, p, 1)
                dve.wait_ge(x_done, p * 2 + 2)
                settle(dve, g["passed"])
                for u in range(2):
                    last = dve.bn_stats(z_stats[:, u, :], x_all[:, 2 * p + u, :])
                ch.tag(last)
                ch.wait()
                settle(dve, g["passed"])
                for u in range(2):
                    last = dve.bn_aggr(z_mv[:, u, :], z_stats[:, u, :])
                last.then_inc(z_stats_ready, 1)
                ch.end()

            def z_normed(p):
                dve.wait_ge(z_rstd_ready, p + 1)
                for u in range(2):
                    dve.tensor_scalar(z_all[:, 2 * p + u, :], x_all[:, 2 * p + u, :], z_mv[:, u, 0:1],
                                      z_rstd[:, u:u + 1], ALU.subtract, ALU.mult)

            def step(it):
                norm, attend, after = it + 2, it, it - 1
                if within(norm, PAIRS):
                    ch_norm = Chain(dve, dve_norm, norm, 4 if first else 3)
                    norm_stats(norm, ch_norm)
                if within(attend, PAIRS):
                    for u in range(2):
                        dve.wait_ge(stackT_ready, attend * 2 + u + 1)
                        dve.tensor_copy(qT[u][:, :, :].rearrange("p h q -> p (h q)"),
                                        tile[u][:, 0:512].bitcast(BF16)).then_inc(qT_ready, 1)
                if within(after, PAIRS):
                    ch_out = Chain(dve, dve_out, after, 10 if first else 4)
                for u in range(2):
                    if within(attend, PAIRS):
                        row_max(attend, 0, u)
                    if within(after, PAIRS):
                        divide(after, u, ch_out)
                if within(attend, PAIRS):
                    for u in range(2):
                        row_max(attend, 1, u)
                    shifts(attend)
                if within(it + 1, PAIRS):
                    rotate(it + 1)
                if within(it - 2, PAIRS):
                    z_normed(it - 2)
                if within(norm, PAIRS) and first:
                    norm_again(norm, ch_norm)
                if within(after, PAIRS):
                    add_to_x(after, ch_out)
                    ch_out.end()
                    z_norm_stats(after)
                if within(norm, PAIRS):
                    normed(norm)
                    ch_norm.end()

            run_steps(dve, step, PAIRS, 2, 2)

        @block.gpsimd
        def _(pool):
            if first:
                pool.memset(g["ones_row"][:, :], 1.0).then_inc(g["set_up"], 1)
                pool.memset(g["minus_half"][:, :], -0.5).then_inc(g["set_up"], 1)
                pool.wait_ge(g["set_up"], 2)
            pairs = lambda buf: buf[:, 0:4].rearrange("p (u s) -> p u s", u=2)
            for u in range(2):
                pool.memset(stack[u][:, :, :, :], 0.0)
                pool.memset(vaug[u][:, :, :], 0.0).then_inc(ones_set, 1)
            pool.wait_ge(ones_set, 2)
            for u in range(2):
                pool.memset(vaug[u][:, :, ND:ND + 1], 1.0).then_inc(ones_set, 1)
            pool.wait_ge(ones_set, 4)

            def cast(out, src):
                return pool.tensor_scalar(out, src, 1.0, 0.0, ALU.mult, ALU.add)

            def inverse_deviation(p, n, ch):
                pool.wait_ge(stats_ready, p * NORMS + n + 1)
                settle(pool, g["passed"])
                of = slice(0, 2 if first else 1)
                ch.tag(pool.tensor_scalar(pairs(var_eps)[:, :, of], mv[:, :, of, 1], EPS, 1.0, ALU.add, ALU.mult))
                ch.wait()
                pool.tensor_tensor(pairs(rstd)[:, :, of], pairs(var_eps)[:, :, of], pairs(minus_half)[:, :, of],
                                   ALU.pow).then_inc(rstd_ready, 1)

            def split(p, u, ch):
                wait_of(pool, stackT_ready, p - 1, 2, u + 1)
                pool.wait_ge(rot_ready, p * 2 + u + 1)
                settle(pool, g["passed"])

                def slots(which, a, b, step=1):
                    v = stack[u][:, which, :, 0:6 * ND].rearrange("p h (s r) -> p h s r", r=ND)
                    return v[:, :, a:b:step, :]

                def part(buf, which, n):
                    v = buf[u][:, which * P:(which + 1) * P].rearrange("p (h r) -> p h r", r=ND)
                    return v.unsqueeze(2).broadcast_to([P, NH, n, ND])

                both = lambda s: stack[u][:, :, :, s * ND:(s + 1) * ND]
                whole = lambda buf: buf[u][:, :].rearrange("p (a h r) -> p a h r", a=2, r=ND)
                cast(slots(0, 0, 3), part(rot, 0, 3))
                cast(slots(1, 0, 4, 3), part(rot, 1, 2))
                ch.tag(cast(slots(1, 5, 6), part(rot, 1, 1)))
                ch.wait()
                ch.tag(pool.tensor_tensor(whole(rest), whole(rot), both(0), ALU.subtract))
                ch.wait()
                settle(pool, g["passed"])
                cast(slots(0, 3, 5), part(rest, 0, 2))
                ch.tag(cast(slots(1, 1, 5, 3), part(rest, 1, 2)))
                ch.wait()
                ch.tag(pool.tensor_tensor(whole(rest2), whole(rest), both(4), ALU.subtract))
                ch.wait()
                settle(pool, g["passed"])
                cast(slots(0, 5, 6), part(rest2, 0, 1))
                cast(slots(1, 2, 3), part(rest2, 1, 1)).then_inc(split_ready, 1)

            def z_inverse_deviation(p):
                ch = Chain(pool, pool_z, p, 1)
                pool.wait_ge(z_stats_ready, p + 1)
                settle(pool, g["passed"])
                ch.tag(pool.tensor_scalar(z_var_eps[:, :], z_mv[:, :, 1], EPS, 1.0, ALU.add, ALU.mult))
                ch.wait()
                pool.tensor_tensor(z_rstd[:, :], z_var_eps[:, :], minus_half[:, 0:2], ALU.pow).then_inc(
                    z_rstd_ready, 1)
                ch.end()

            def step(it):
                norm, project = it + 2, it + 1
                if within(it, PAIRS):
                    for u in range(2):
                        pool.wait_ge(v_ready, it * 2 + u + 1)
                        wait_of(pool, pv_ready, it - 1, 2, u + 1)
                        settle(pool, g["passed"])
                        by_head = lambda ap: ap.rearrange("p (h r) -> p h r", r=ND)
                        if first:
                            cast(vaug[u][:, :, 0:ND], by_head(v_next[u][:, :])).then_inc(vaug_ready, 1)
                        else:
                            pool.tensor_tensor(vaug[u][:, :, 0:ND], by_head(v_next[u][:, :]),
                                               by_head(g["row_n2"][:, 2 * P:3 * P]), ALU.add).then_inc(vaug_ready, 1)
                if within(norm, PAIRS):
                    ch_norm = Chain(pool, pool_norm, norm, NORMS)
                    inverse_deviation(norm, 0, ch_norm)
                if within(project, PAIRS):
                    ch_split = Chain(pool, pool_split, project, 8)
                    split(project, 0, ch_split)
                if within(norm, PAIRS) and first:
                    inverse_deviation(norm, 1, ch_norm)
                if within(project, PAIRS):
                    split(project, 1, ch_split)
                    ch_split.end()
                if within(it - 1, PAIRS):
                    z_inverse_deviation(it - 1)
                if within(norm, PAIRS):
                    ch_norm.end()

            run_steps(pool, step, PAIRS, 2, 1)

        @block.scalar
        def _(act):
            if first:
                act.wait_ge(g["tables_loaded"], g["tables_count"])

            def step(it):
                norm, project, after = it + 2, it + 1, it - 1
                if within(it, PAIRS):
                    for u in range(2):
                        act.wait_ge(stackT_ready, it * 2 + u + 1)
                        act.activation(kT[u][:, :, :].rearrange("p h k -> p (h k)"),
                                       tile[u][:, 512:1024].bitcast(BF16), ACT.Copy).then_inc(kT_ready, 1)
                if within(project, PAIRS):
                    for u in range(2):
                        act.wait_ge(zT_ready, project * 2 + u + 1)
                        zT = front[u][:, 0:2 * P]
                        out = xT[u][:, :, :].rearrange("p s t -> p (s t)")
                        if first:
                            act.activation(out, zT, ACT.Identity, scale=g["cols"][:, 0:1],
                                           bias=g["cols"][:, 1:2]).then_inc(xT_ready, 1)
                        else:
                            act.activation(out, zT, ACT.Copy).then_inc(xT_ready, 1)
                    for u in range(2):
                        act.wait_ge(qkv_ready, project * 2 + u + 1)
                        wait_of(act, vaug_ready, project - 1, 2, u + 1)
                        act.activation(v_next[u][:, :], front[u][:, 2 * P:3 * P], ACT.Copy).then_inc(v_ready, 1)
                if within(norm, PAIRS) and not first:
                    wait_of(act, zT_ready, norm - 1, 2, 2)
                    for u in range(2):
                        act.activation(z_in[u][:, 1, :], ctx_all[:, 2 * norm + u, :], ACT.Copy).then_inc(ctx_ready, 1)
                if within(after, PAIRS):
                    for u in range(2):
                        act.wait_ge(attT_psum, after * 2 + u + 1)
                        act.activation(attT[u][:, :], obank[u][:, 0:P], ACT.Copy).then_inc(attT_ready, 1)
                    if first:
                        for u in range(2):
                            act.wait_ge(ao_ready, after * 2 + u + 1)
                            act.activation(aoT[u][:, :], obank[u][:, P:2 * P], ACT.Identity,
                                           bias=g["cols"][:, 2:3]).then_inc(aoT_ready, 1)
                        for u in range(2):
                            act.wait_ge(gate_psum, after * 2 + u + 1)
                            act.activation(gate[u][:, :], obank[u][:, 384:512], ACT.Tanh,
                                           scale=0.5).then_inc(gate_ready, 1)
                if within(it, PAIRS):
                    for c in range(2):
                        for u in range(2):
                            act.wait_ge(shifted_ready, it * 4 + 2 * c + u + 1)
                            act.activation(prob[u][:, 8 * c:8 * c + 8, :].rearrange("p h q -> p (h q)"),
                                           tile[u][:, :], ACT.Exp).then_inc(exp_done, 1)
                    for u in range(2):
                        act.wait_ge(pv_ready, it * 2 + u + 1)
                        act.activation(oT[u][:, :, :].rearrange("p g q -> p (g q)"), obank[u][:, :],
                                       ACT.Copy).then_inc(oT_ready, 1)

            run_steps(act, step, PAIRS, 2, 1)

        @block.tensor
        def _(pe):
            if first:
                pe.wait_ge(g["tables_loaded"], g["tables_count"])
                pe.wait_ge(g["set_up"], 2)

            def stack_pair(u, h):
                rows = slice(SLOT * (h % 2), SLOT * (h % 2) + SLOT)
                return qT[u][rows, h // 2, :], kT[u][rows, h // 2, :]

            def transpose_stack(p, u):
                pe.wait_ge(split_ready, p * 2 + u + 1)
                wait_of(pe, exp_done, p - 1, 4, 2 + u + 1)
                for which in range(2):
                    into = tile[u][:, 512 * which:512 * which + 512].bitcast(BF16)
                    for pair in range(NH // 2):
                        last = pe.transpose(into[:, pair * P:(pair + 1) * P],
                                            stack[u][:, which, 2 * pair:2 * pair + 2, :]
                                            .rearrange("p h s -> p (h s)"), identb)
                last.then_inc(stackT_ready, 1)

            def transpose_inputs(p, u):
                pe.wait_ge(z_ready, p * 2 + u + 1)
                pe.wait_ge(ctx_ready, p * 2 + u + 1)
                wait_of(pe, rot_ready, p - 1, 2, u + 1)
                pe.transpose(front[u][:, 0:P], z_in[u][:, 0, :], ident)
                pe.transpose(front[u][:, P:2 * P], z_in[u][:, 1, :], ident).then_inc(zT_ready, 1)

            def project_inputs(p, u):
                pe.wait_ge(xT_ready, p * 2 + u + 1)
                for which, at in ((0, 0), (1, P), (1, 2 * P)):
                    last = pe.matmul(front[u][:, at:at + P], xT[u][:, which, :], wqkv[:, at:at + P], start=True,
                                     stop=True)
                last.then_inc(qkv_ready, 1)

            def scores(p, u, c):
                if c == 0:
                    pe.wait_ge(qT_ready, p * 2 + u + 1)
                    pe.wait_ge(kT_ready, p * 2 + u + 1)
                else:
                    pe.wait_ge(max_done, p * 4 + u + 1)
                for half in range(2):
                    if not first:
                        pe.matmul(tile[u][:, 512 * half:512 * half + 512], identb,
                                  heads(g["neg_mask"][:, 2 * p + u, :]), start=True, stop=False,
                                  skip_group_check=True)
                for j in range(8):
                    slot = 4 * (j % 2) + j // 2
                    q, k = stack_pair(u, slot_head(8 * c + slot))
                    last = pe.matmul(tile[u][:, P * slot:P * (slot + 1)], q, k, start=first, stop=True,
                                     skip_group_check=True)
                last.then_inc(scores_ready, 1)

            def shifted_scores(p, u, c):
                if c == 0:
                    pe.wait_ge(shiftT_ready, p * 2 + u + 1)
                else:
                    pe.wait_ge(exp_done, p * 4 + u + 1)
                for half in range(2):
                    bank = tile[u][:, 512 * half:512 * half + 512]
                    if first:
                        for t in range(3):
                            pe.matmul(bank, identb, heads(bias3[:, t, :]), start=(t == 0), stop=False,
                                      skip_group_check=True)
                    else:
                        pe.matmul(bank, identb, heads(g["neg_maskT"][:, 2 * p + u, :]), start=True, stop=False,
                                  skip_group_check=True)
                for j in range(8):
                    slot = 4 * (j % 2) + j // 2
                    q, k = stack_pair(u, slot_head(8 * c + slot))
                    pe.matmul(tile[u][:, P * slot:P * (slot + 1)], k, q, start=False, stop=False,
                              skip_group_check=True)
                for slot in range(8):
                    last = pe.matmul(tile[u][:, P * slot:P * (slot + 1)], pick[:, 8 * c + slot, :],
                                     shiftT[u][:, :], start=False, stop=True, skip_group_check=True)
                last.then_inc(shifted_ready, 1)

            def values(p, u, c):
                if c == 0:
                    pe.wait_ge(vaug_ready, p * 2 + u + 1)
                    wait_of(pe, x_done, p - 1, 2, u + 1)
                else:
                    pe.wait_ge(exp_done, p * 4 + 2 + u + 1)
                for h in range(8 * c, 8 * c + 8):
                    row = 32 * (h % 4)
                    slot = 8 * c + 4 * (h % 2) + h % 8 // 2
                    last = pe.matmul(obank[u][row:row + 32, P * (h // 4):P * (h // 4) + P], vaug[u][:, h, :],
                                     prob[u][:, slot, :], start=True, stop=True)
                return last

            def turn_back(p, u):
                pe.wait_ge(oT_ready, p * 2 + u + 1)
                for n in range(4):
                    last = pe.transpose(obank[u][:, n * P:(n + 1) * P], oT[u][:, n, :], ident)
                last.then_inc(o_ready, 1)

            def transpose_attended(p, u):
                pe.wait_ge(att_ready, p * 2 + u + 1)
                pe.transpose(obank[u][:, 0:P], att[u][:, :], ident).then_inc(attT_psum, 1)

            def project_attended(p, u):
                pe.wait_ge(attT_ready, p * 2 + u + 1)
                if first:
                    pe.matmul(obank[u][:, 2 * P:3 * P], attT[u][:, :], wout, start=True, stop=True)
                    pe.matmul(obank[u][:, P:2 * P], wout, attT[u][:, :], start=True,
                              stop=True).then_inc(ao_ready, 1)
                else:
                    pe.matmul(obank[u][:, P:2 * P], attT[u][:, :], wout, start=True,
                              stop=True).then_inc(ao_ready, 1)

            def project_gate(p, u):
                pe.wait_ge(aoT_ready, p * 2 + u + 1)
                pe.matmul(obank[u][:, 384:512], g["ones_row"][0:1, :], g["row_n1"][0:1, P:2 * P], start=True,
                          stop=False)
                pe.matmul(obank[u][:, 384:512], aoT[u][:, :], w[:, 4 * P:5 * P], start=False,
                          stop=True).then_inc(gate_psum, 1)

            def step(it):
                project, after = it + 1, it - 1
                is_now, is_next, is_last = within(it, PAIRS), within(project, PAIRS), within(after, PAIRS)
                if is_now:
                    for u in range(2):
                        transpose_stack(it, u)
                if is_next:
                    for u in range(2):
                        transpose_inputs(project, u)
                for u in range(2):
                    if is_last:
                        turn_back(after, u)
                    if is_now:
                        scores(it, u, 0)
                if is_now:
                    scores(it, 0, 1)
                if is_next:
                    project_inputs(project, 0)
                    if first:
                        project_inputs(project, 1)
                if is_now:
                    scores(it, 1, 1)
                if is_last:
                    for u in range(2):
                        transpose_attended(after, u)
                if is_next and not first:
                    project_inputs(project, 1)
                if is_last:
                    for u in range(2):
                        project_attended(after, u)
                if is_last and first:
                    for u in range(2):
                        project_gate(after, u)
                if is_now:
                    for u in range(2):
                        pe.wait_ge(shift_ready, it * 2 + u + 1)
                        pe.transpose(tile[u][0:2 * NH, 0:64].bitcast(BF16),
                                     shift[u][:, :, :].rearrange("p t h -> p (t h)"), identb).then_inc(shiftT_psum, 1)
                    for u in range(2):
                        shifted_scores(it, u, 0)
                    for u in range(2):
                        shifted_scores(it, u, 1)
                        values(it, u, 0)
                    for u in range(2):
                        values(it, u, 1).then_inc(pv_ready, 1)

            run_steps(pe, step, PAIRS, 2, 1)

    nc.clear_and_free_semaphores(used)
    nc.all_engine_barrier()


def mask_stage(nc, g):
    N = 2 * GROUP
    with ExitStack() as ctx:
        row_max = ctx.enter_context(nc.sbuf_tensor("mk_row_max", [P, NSEQ], F32))
        mask = ctx.enter_context(nc.sbuf_tensor("mk_mask", [P, NSEQ, P], I32))
        turned = [ctx.enter_context(nc.psum_tensor(f"mk_turned{k}", [P, 512], F32)) for k in range(NSEQ // N)]
        mask_loaded = [ctx.enter_context(nc.semaphore(f"mk_mask_loaded{k}")) for k in range(NSEQ // N)]
        neg_mask_ready = ctx.enter_context(nc.semaphore("mk_neg_mask_ready"))
        row_max_ready = ctx.enter_context(nc.semaphore("mk_row_max_ready"))
        turned_ready = ctx.enter_context(nc.semaphore("mk_turned_ready"))
        block = ctx.enter_context(nc.Block())
        parts = [slice(N * k, N * (k + 1)) for k in range(NSEQ // N)]

        @block.sync
        def _(sp):
            for k, seqs in enumerate(parts):
                sp.dma_start(mask[:, seqs, :], g["d_mask"][seqs, 0, :, :].rearrange("b q k -> q b k")
                             ).then_inc(mask_loaded[k], 16)

        @block.vector
        def _(dve):
            for k, seqs in enumerate(parts):
                dve.wait_ge(mask_loaded[k], 16)
                dve.tensor_scalar(g["neg_mask"][:, seqs, :], mask[:, seqs, :], 0.0, MASKED, ALU.is_equal,
                                  ALU.mult).then_inc(neg_mask_ready, 1)
            for k, seqs in enumerate(parts):
                dve.wait_ge(neg_mask_ready, k + 1)
                dve.tensor_reduce(row_max[:, seqs], g["neg_mask"][:, seqs, :], AX.X, ALU.max).then_inc(
                    row_max_ready, 1)
            dve.wait_ge(row_max_ready, NSEQ // N)
            dve.tensor_scalar(g["q_scale"][:, :, 0], row_max[:, :], 0.0, float(ND) ** -0.5, ALU.is_equal, ALU.mult)

        @block.tensor
        def _(pe):
            for k, seqs in enumerate(parts):
                pe.wait_ge(neg_mask_ready, k + 1)
                for n in range(N):
                    last = pe.transpose(turned[k][:, :].bitcast(BF16)[:, n * P:(n + 1) * P],
                                        g["neg_mask"][:, N * k + n, :], g["cb"][:, CB["ident"]])
                last.then_inc(turned_ready, 1)

        @block.scalar
        def _(act):
            for k, seqs in enumerate(parts):
                act.wait_ge(turned_ready, k + 1)
                act.activation(g["neg_maskT"][:, seqs, :].rearrange("p n q -> p (n q)"),
                               turned[k][:, :].bitcast(BF16), ACT.Copy)


WIDE_SEMS = ["wqkv_loaded", "wo_loaded", "gain_loaded", "tables_ready", "dve_rot", "pool_norm", "zc_ready",
             "raw_ready", "square_ready", "norm2_ready", "half_turn_ready", "inv_norm_ready", "rot_ready",
             "scores_ready", "max_ready", "exp_done", "inv_sum_ready", "prob_ready", "probT_psum", "first_probT_ready",
             "second_probT_ready",
             "pv_ready", "out_ready", "z_done", "edge_ready", "zT_ready", "hT_ready", "qk_ready", "v_psum", "v_ready", "v_taken",
             "qkT_psum", "qkT_ready", "attT_ready"]


def wide_stage(nc, g, layer, s):
    with ExitStack() as ctx:
        def sb(name, shape, dt):
            return ctx.enter_context(nc.sbuf_tensor("w_" + name, shape, dt))

        def ps(name, shape, dt):
            return ctx.enter_context(nc.psum_tensor("w_" + name, shape, dt))

        z_all, cf, cb = g["z"], g["cf"], g["cb"]
        ident, identb = cf[:, CF["ident"]], cb[:, CB["ident"]]
        band = cb[:, CB["band"]]
        IN = WH * WD
        wqkv = sb("wqkv", [P, 3 * IN], F32)
        wo = sb("wo", [P, 4, P], F32)
        qk_gain = sb("qk_gain", [P, 2, WD], F32)
        rot_c = sb("rot_c", [P, 2, WD], F32)
        rot_s = sb("rot_s", [P, 2, WD], F32)
        zc = [sb(f"zc{u}", [P, P], F32) for u in range(2)]
        hT = [sb(f"hT{u}", [P, P], F32) for u in range(2)]
        square = [sb(f"square{u}", [P, 2 * IN], F32) for u in range(2)]
        raw = [sb(f"raw{u}", [P, 2 * IN], F32) for u in range(2)]
        rot = [sb(f"rot{u}", [P, 2 * IN], F32) for u in range(2)]
        half_turn = [sb(f"half_turn{u}", [P, 2 * IN], F32) for u in range(2)]
        norm2 = [sb(f"norm2{u}", [P, 2 * WH], F32) for u in range(2)]
        clipped = [sb(f"clipped{u}", [P, 2 * WH], F32) for u in range(2)]
        inv_norm = [sb(f"inv_norm{u}", [P, 2 * WH], F32) for u in range(2)]
        qkT = [sb(f"qkT{u}", [P, WH, P], F32) for u in range(2)]
        v_next = [sb(f"v_next{u}", [P, IN], F32) for u in range(2)]
        value = [sb(f"value{u}", [P, WH, WD], F32) for u in range(2)]
        negmax = [sb(f"negmax{u}", [P, WH], F32) for u in range(2)]
        prob = [sb(f"prob{u}", [P, WH, P], F32) for u in range(2)]
        probT = [sb(f"probT{u}", [P, WH, P], F32) for u in range(2)]
        row_sum = [sb(f"row_sum{u}", [P, WH], F32) for u in range(2)]
        inv_sum = [sb(f"inv_sum{u}", [P, WH], F32) for u in range(2)]
        attT = [sb(f"attT{u}", [P, 4, P], F32) for u in range(2)]

        qk_bank = ps("qk_bank", [P, 2 * IN], F32)
        v_bank = ps("v_bank", [P, IN], F32)
        tile = [ps(f"tile{u}", [P, 1024], F32) for u in range(2)]
        obank = ps("obank", [P, 512], F32)

        block = ctx.enter_context(nc.Block())
        n0 = layer * PAIRS

        def wait(eng, name, p, per_step, k):
            if not isinstance(p, int) or p >= 0:
                eng.wait_ge(s[name], (n0 + p) * per_step + k)

        @block.sync
        def _(sp):
            one = bass.ds(layer, 1)
            sp.dma_start(wqkv[:, :], g["d_wqkv"][one, :, :].rearrange("a p n -> p (a n)")).then_inc(
                s["wqkv_loaded"], 16)
            sp.dma_start(wo[:, :, :], g["d_wo"][one, :, :].rearrange("a (c p) n -> p (a c) n", p=P)).then_inc(
                s["wo_loaded"], 16)
            for k, name in enumerate(("d_qs", "d_ks")):
                sp.dma_start(qk_gain[:, k, :], g[name][one, :].broadcast_to([P, WD])).then_inc(s["gain_loaded"], 16)

        @block.vector
        def _(dve):
            for u in range(2):
                dve.memset(hT[u][WD:P, 0:1], 0.0).then_inc(s["edge_ready"], 1)
            dve.wait_ge(s["gain_loaded"], 32 * layer + 32)
            gain = qk_gain[:, :, :].rearrange("p a (t r) -> p a t r", t=2)
            dve.tensor_tensor(rot_c[:, :, :], qk_gain[:, :, :],
                              cf[:, CF["xpos_c"]].rearrange("p (a r) -> p a r", a=2), ALU.mult)
            dve.tensor_tensor(rot_s[:, :, :].rearrange("p a (t r) -> p a t r", t=2), gain[:, :, ::-1, :],
                              cf[:, CF["xpos_s"]].rearrange("p (a t r) -> p a t r", a=2, t=2),
                              ALU.mult).then_inc(s["tables_ready"], 1)
            dve.wait_ge(s["tables_ready"], layer + 1)
            settle(dve, g["passed"])

            def norms_and_cosines(p, u, ch):
                wait(dve, "raw_ready", p, 2, u + 1)
                wait(dve, "qkT_psum", p - 1, 2, u + 1)
                for a in range(2):
                    by_head = lambda buf: buf[u][:, a * IN:(a + 1) * IN].rearrange("p (h r) -> p h r", h=WH)
                    last = dve.tensor_tensor(by_head(rot), by_head(raw),
                                             rot_c[:, a, :].unsqueeze(1).broadcast_to([P, WH, WD]), ALU.mult)
                ch.tag(last)

            def squared_norms(p, u):
                wait(dve, "square_ready", p, 2, u + 1)
                dve.tensor_reduce(norm2[u][:, :], square[u][:, :].rearrange("p (h r) -> p h r", r=WD), AX.X,
                                  ALU.add).then_inc(s["norm2_ready"], 1)

            def add_sines(p, u, ch):
                wait(dve, "half_turn_ready", p, 2, u + 1)
                ch.wait()
                ch.tag(dve.tensor_tensor(rot[u][:, :], rot[u][:, :], half_turn[u][:, :], ALU.add))

            def normalise(p, u, ch):
                ch.wait()
                wait(dve, "inv_norm_ready", p, 2, u + 1)
                by_head = rot[u][:, :].rearrange("p (h r) -> p h r", r=WD)
                dve.tensor_tensor(by_head, by_head, inv_norm[u][:, :].unsqueeze(2).broadcast_to([P, 2 * WH, WD]),
                                  ALU.mult).then_inc(s["rot_ready"], 1)

            def row_max(p, u):
                wait(dve, "scores_ready", p, 2, u + 1)
                dve.tensor_reduce(negmax[u][:, :], tile[u][:, :].rearrange("p (h k) -> p h k", h=WH), AX.X,
                                  ALU.max, negate=True).then_inc(s["max_ready"], 1)

            def divide(p, u):
                for half in range(2):
                    slots = slice(4 * half, 4 * half + 4)
                    wait(dve, "exp_done", p, 4, 2 * u + half + 1)
                    dve.reciprocal(inv_sum[u][:, slots], row_sum[u][:, slots]).then_inc(s["inv_sum_ready"], 1)
                    wait(dve, "inv_sum_ready", p, 4, 2 * u + half + 1)
                    dve.tensor_tensor(prob[u][:, slots, :], prob[u][:, slots, :],
                                      inv_sum[u][:, slots].unsqueeze(2).broadcast_to([P, 4, P]),
                                      ALU.mult).then_inc(s["prob_ready"], 1)

            def take_first_probT(p):
                wait(dve, "probT_psum", p, 2, 1)
                dve.tensor_copy(probT[0][:, :, :].rearrange("p h q -> p (h q)"), tile[0][:, :]).then_inc(
                    s["first_probT_ready"], 1)

            def add_to_z(p, u):
                wait(dve, "out_ready", p, 2, u + 1)
                zb = z_all[:, 2 * p + u, :]
                dve.tensor_tensor(zb, zb, obank[:, 0:P], ALU.add).then_inc(s["z_done"], 1)

            def step(it):
                project, after = it + 1, it - 1
                is_now, is_next, is_last = within(it, PAIRS), within(project, PAIRS), within(after, PAIRS)
                if is_next:
                    ch = Chain(dve, s["dve_rot"], n0 + project, 4)
                    norms_and_cosines(project, 0, ch)
                    squared_norms(project, 0)
                    add_sines(project, 0, ch)
                if is_now:
                    row_max(it, 0)
                if is_last:
                    add_to_z(after, 0)
                if is_now:
                    divide(it, 0)
                if is_next:
                    normalise(project, 0, ch)
                if is_now:
                    row_max(it, 1)
                if is_next:
                    norms_and_cosines(project, 1, ch)
                    squared_norms(project, 1)
                if is_now:
                    divide(it, 1)
                    take_first_probT(it)
                if is_last:
                    add_to_z(after, 1)
                if is_next:
                    add_sines(project, 1, ch)
                    normalise(project, 1, ch)
                    ch.end()

            run_steps(dve, step, PAIRS, 1, 1)

        @block.gpsimd
        def _(pool):
            pool.wait_ge(s["tables_ready"], layer + 1)
            settle(pool, g["passed"])

            def half_turns(p, u):
                wait(pool, "raw_ready", p, 2, u + 1)
                for a in range(2):
                    for t in range(2):
                        half = lambda buf, t: buf[u][:, a * IN:(a + 1) * IN].rearrange(
                            "p (h t r) -> p h t r", h=WH, t=2)[:, :, t, :]
                        table = rot_s[:, a, t * WD // 2:(t + 1) * WD // 2].unsqueeze(1).broadcast_to(
                            [P, WH, WD // 2])
                        last = pool.tensor_tensor(half(half_turn, t), half(raw, 1 - t), table, ALU.mult)
                last.then_inc(s["half_turn_ready"], 1)

            def take_values(p, u):
                wait(pool, "v_ready", p, 2, u + 1)
                wait(pool, "pv_ready", p - 1, 2, u + 1)
                settle(pool, g["passed"])
                pool.tensor_scalar(value[u][:, :, :].rearrange("p h r -> p (h r)"), v_next[u][:, :], 1.0, 0.0,
                                   ALU.mult, ALU.add).then_inc(s["v_taken"], 1)

            def inverse_norms(p, u, ch):
                wait(pool, "norm2_ready", p, 2, u + 1)
                settle(pool, g["passed"])
                ch.tag(pool.tensor_scalar(clipped[u][:, :], norm2[u][:, :], 1e-24, 1.0, ALU.max, ALU.mult))
                ch.wait()
                pool.tensor_tensor(inv_norm[u][:, :], clipped[u][:, :], g["minus_half"][:, 0:2 * WH],
                                   ALU.pow).then_inc(s["inv_norm_ready"], 1)

            def step(it):
                project = it + 1
                if within(project, PAIRS):
                    ch = Chain(pool, s["pool_norm"], n0 + project, 2)
                is_now, is_next = within(it, PAIRS), within(project, PAIRS)
                if is_next:
                    half_turns(project, 0)
                if is_now:
                    take_values(it, 0)
                if is_next:
                    inverse_norms(project, 0, ch)
                if is_next:
                    half_turns(project, 1)
                if is_now:
                    take_values(it, 1)
                if is_next:
                    inverse_norms(project, 1, ch)
                    ch.end()

            run_steps(pool, step, PAIRS, 1, 1)

        @block.scalar
        def _(act):
            act.wait_ge(s["edge_ready"], 2 * layer + 2)
            settle(act, g["passed"])

            def copy_z(p, u):
                act.activation(zc[u][:, :], z_all[:, 2 * p + u, :], ACT.Copy).then_inc(s["zc_ready"], 1)

            def shift_tokens(p, u):
                wait(act, "zT_ready", p, 1, 1)
                at = P * u
                act.activation(hT[u][0:WD, :], v_bank[0:WD, at:at + P], ACT.Copy)
                act.activation(hT[u][WD:P, 1:P], v_bank[WD:P, at:at + P - 1], ACT.Copy).then_inc(s["hT_ready"], 1)

            def take_qk(p, u):
                wait(act, "qk_ready", p, 2, u + 1)
                wait(act, "rot_ready", p - 1, 2, u + 1)
                act.activation(raw[u][:, :], qk_bank[:, :], ACT.Copy).then_inc(s["raw_ready"], 1)
                act.activation(square[u][:, :], qk_bank[:, :], ACT.Square).then_inc(s["square_ready"], 1)

            def take_v(p, u):
                wait(act, "v_psum", p, 2, u + 1)
                wait(act, "v_taken", p - 1, 2, u + 1)
                act.activation(v_next[u][:, :], v_bank[:, :], ACT.Copy).then_inc(s["v_ready"], 1)

            def take_qkT(p, u):
                wait(act, "qkT_psum", p, 2, u + 1)
                act.activation(qkT[u][:, :, :].rearrange("p h k -> p (h k)"), tile[u][:, :],
                               ACT.Copy).then_inc(s["qkT_ready"], 1)

            def exponentials(p, u, half):
                wait(act, "max_ready", p, 2, u + 1)
                for slot in range(4 * half, 4 * half + 4):
                    last = act.activation(prob[u][:, slot, :], tile[u][:, slot * P:(slot + 1) * P], ACT.Exp,
                                          bias=negmax[u][:, slot:slot + 1], accum_out=row_sum[u][:, slot:slot + 1])
                last.then_inc(s["exp_done"], 1)

            def take_second_probT(p):
                wait(act, "probT_psum", p, 2, 2)
                act.activation(probT[1][:, :, :].rearrange("p h q -> p (h q)"), tile[1][:, :], ACT.Copy).then_inc(
                    s["second_probT_ready"], 1)

            def take_attT(p, u):
                wait(act, "pv_ready", p, 2, u + 1)
                act.activation(attT[u][:, :, :].rearrange("p c q -> p (c q)"), obank[:, :],
                               ACT.Copy).then_inc(s["attT_ready"], 1)

            def step(it):
                project, after = it + 1, it - 1
                is_now, is_next, is_last = within(it, PAIRS), within(project, PAIRS), within(after, PAIRS)
                if is_next:
                    for u in range(2):
                        shift_tokens(project, u)
                if within(it + 2, PAIRS):
                    for u in range(2):
                        copy_z(it + 2, u)
                if is_now:
                    take_qkT(it, 0)
                if is_next:
                    take_qk(project, 0)
                if is_now:
                    take_qkT(it, 1)
                if is_last:
                    take_attT(after, 0)
                if is_next:
                    take_v(project, 0)
                if is_now:
                    exponentials(it, 0, 0)
                    exponentials(it, 0, 1)
                if is_next:
                    take_qk(project, 1)
                if is_now:
                    exponentials(it, 1, 0)
                if is_last:
                    take_attT(after, 1)
                if is_now:
                    exponentials(it, 1, 1)
                if is_next:
                    take_v(project, 1)
                if is_now:
                    take_second_probT(it)

            run_steps(act, step, PAIRS, 2, 1)

        @block.tensor
        def _(pe):
            pe.wait_ge(s["wqkv_loaded"], 16 * layer + 16)
            pe.wait_ge(s["wo_loaded"], 16 * layer + 16)
            settle(pe, g["passed"])

            def transpose_z(p):
                wait(pe, "v_ready", p - 1, 2, 2)
                for u in range(2):
                    wait(pe, "zc_ready", p, 2, u + 1)
                    last = pe.transpose(v_bank[:, u * P:(u + 1) * P], zc[u][:, :], ident)
                last.then_inc(s["zT_ready"], 1)

            def project_qkv(p, u):
                wait(pe, "hT_ready", p, 2, 2)
                if u == 0:
                    wait(pe, "square_ready", p - 1, 2, 2)
                else:
                    wait(pe, "square_ready", p, 2, 1)
                    wait(pe, "v_ready", p, 2, 1)
                for half in range(2):
                    last = pe.matmul(qk_bank[:, 512 * half:512 * half + 512], hT[u][:, :],
                                     wqkv[:, IN * half:IN * (half + 1)], start=True, stop=True)
                last.then_inc(s["qk_ready"], 1)
                pe.matmul(v_bank[:, :], hT[u][:, :], wqkv[:, 2 * IN:3 * IN], start=True,
                          stop=True).then_inc(s["v_psum"], 1)

            def transpose_qk(p, u):
                wait(pe, "rot_ready", p, 2, u + 1)
                wait(pe, ("first_probT_ready", "second_probT_ready")[u], p - 1, 1, 1)
                for j in range(WH):
                    last = pe.transpose(tile[u][:, j * P:(j + 1) * P], rot[u][:, j * P:(j + 1) * P], ident)
                last.then_inc(s["qkT_psum"], 1)

            def scores(p, u):
                wait(pe, "qkT_ready", p, 2, u + 1)
                for half in range(2):
                    bank = tile[u][:, 512 * half:512 * half + 512]
                    pe.matmul(bank, identb, band.unsqueeze(1).broadcast_to([P, 4, P]), start=True, stop=False,
                              skip_group_check=True)
                for j in range(8):
                    slot = 4 * (j % 2) + j // 2
                    h = slot_head(slot)
                    rows = slice(WD * (h % 2), WD * (h % 2) + WD)
                    last = pe.matmul(tile[u][:, P * slot:P * (slot + 1)], qkT[u][rows, h // 2, :],
                                     qkT[u][rows, WH // 2 + h // 2, :], start=False, stop=True,
                                     skip_group_check=True)
                last.then_inc(s["scores_ready"], 1)

            def transpose_prob(p, u):
                for slot in range(WH):
                    if slot % 4 == 0:
                        wait(pe, "prob_ready", p, 4, 2 * u + slot // 4 + 1)
                    last = pe.transpose(tile[u][:, slot * P:(slot + 1) * P], prob[u][:, slot, :], ident)
                last.then_inc(s["probT_psum"], 1)

            def times_values(p, u):
                wait(pe, ("first_probT_ready", "second_probT_ready")[u], p, 1, 1)
                wait(pe, "v_taken", p, 2, u + 1)
                if u == 0:
                    wait(pe, "z_done", p - 1, 2, 2)
                else:
                    wait(pe, "z_done", p, 2, 1)
                for h in range(WH):
                    row, at = WD * (h % 2), P * (h // 2)
                    last = pe.matmul(obank[row:row + WD, at:at + P], value[u][:, h, :],
                                     probT[u][:, 4 * (h % 2) + h // 2, :], start=True, stop=True)
                last.then_inc(s["pv_ready"], 1)

            def project_attended(p, u):
                wait(pe, "attT_ready", p, 2, u + 1)
                for c in range(4):
                    last = pe.matmul(obank[:, 0:P], attT[u][:, c, :], wo[:, c, :], start=(c == 0), stop=(c == 3))
                last.then_inc(s["out_ready"], 1)

            def step(it):
                project, after = it + 1, it - 1
                is_now, is_next, is_last = within(it, PAIRS), within(project, PAIRS), within(after, PAIRS)
                if is_next:
                    transpose_z(project)
                if is_now:
                    transpose_qk(it, 0)
                if is_next:
                    project_qkv(project, 0)
                if is_now:
                    transpose_qk(it, 1)
                if is_last:
                    times_values(after, 0)
                if is_now:
                    scores(it, 0)
                if is_last:
                    project_attended(after, 0)
                if is_next:
                    project_qkv(project, 1)
                if is_now:
                    scores(it, 1)
                if is_last:
                    times_values(after, 1)
                if is_now:
                    transpose_prob(it, 0)
                if is_last:
                    project_attended(after, 1)
                if is_now:
                    transpose_prob(it, 1)

            run_steps(pe, step, PAIRS, 1, 1)


GLU_SEMS = ["before_first", "before_rest", "w1_loaded", "w2_loaded", "b1_loaded", "ln_loaded", "first_row_zero",
            "one_row", "dve_stats", "pool_var", "stats_ready", "rstd_ready", "hn_ready", "lin_ready", "gel_ready",
            "gated_ready", "y_ready", "z_done", "turn_ready", "hT_ready", "gate_ready"]


def glu_stage(nc, g, layer, s):
    with ExitStack() as ctx:
        def sb(name, shape, dt):
            return ctx.enter_context(nc.sbuf_tensor("m_" + name, shape, dt))

        def ps(name, shape, dt):
            return ctx.enter_context(nc.psum_tensor("m_" + name, shape, dt))

        z_all, cf = g["z"], g["cf"]
        ident = cf[:, CF["ident"]]
        N = GROUP * P
        LAST = CHUNKS[2][1]
        w1 = sb("w1", [P, 2 * HID], F32)
        w2 = sb("w2", [P, 3, P], F32)
        b1 = sb("b1", [P, 2, 3], F32)
        ln = sb("ln", [P, 2], F32)
        before = sb("before", [P, NSEQ, WD], F32)
        stats = [sb(f"stats{u}", [P, GROUP, 2, 6], F32) for u in range(2)]
        mv = [sb(f"mv{u}", [P, GROUP, 2], F32) for u in range(2)]
        var_eps = [sb(f"var_eps{u}", [P, GROUP], F32) for u in range(2)]
        rstd = [sb(f"rstd{u}", [P, GROUP], F32) for u in range(2)]
        hn = [sb(f"hn{u}", [P, GROUP, P], F32) for u in range(2)]
        hT = [sb(f"hT{u}", [P, N], F32) for u in range(2)]
        gel = [sb(f"gel{i}", [P, N], F32) for i in range(2)]
        gated = [[sb(f"gated{u}{c}", [P, N], F32) for c in range(3)] for u in range(2)]
        turn = [ps(f"turn{u}", [P, N], F32) for u in range(2)]
        gate = [ps(f"gate{i}", [P, N], F32) for i in range(2)]
        lin = [ps(f"lin{i}", [P, N], F32) for i in range(2)]
        y = [ps(f"y{u}", [P, GROUP, P], F32) for u in range(2)]
        block = ctx.enter_context(nc.Block())
        n0 = layer * STEPS

        def wait(eng, name, p, per_step, k):
            if not isinstance(p, int) or p >= 0:
                eng.wait_ge(s[name], (n0 + p) * per_step + k)

        def chunk_before(eng, name, p, i):
            if not isinstance(p, int) or p > 0 or i >= 2:
                eng.wait_ge(s[name], (n0 + p) * 6 + i - 1)

        @block.sync
        def _(sp):
            one = bass.ds(layer, 1)
            first, rest = slice(0, 2 * GROUP), slice(2 * GROUP, NSEQ)
            sp.dma_start(before[1:P, first, :], z_all[0:P - 1, first, WD:P]).then_inc(s["before_first"], 16)
            for k, name in enumerate(("d_ln_g", "d_ln_b")):
                sp.dma_start(ln[:, k:k + 1], g[name][one, :].rearrange("a p -> p a")).then_inc(s["ln_loaded"], 16)
            sp.dma_start(w1[:, :], g["d_w1"][one, :, :].rearrange("a p n -> p (a n)")).then_inc(s["w1_loaded"], 16)
            sp.dma_start(before[1:P, rest, :], z_all[0:P - 1, rest, WD:P]).then_inc(s["before_rest"], 16)
            for c, (at, n) in enumerate(CHUNKS):
                for a in range(2):
                    sp.dma_start(b1[0:n, a, c:c + 1],
                                 g["d_b1"][one, a * HID + at:a * HID + at + n].rearrange("a p -> p a")).then_inc(
                        s["b1_loaded"], 16)
                sp.dma_start(w2[0:n, c, :], g["d_w2"][one, at:at + n, :].rearrange("a p n -> p (a n)")).then_inc(
                    s["w2_loaded"], 16)
            sp.dma_start(w2[LAST:LAST + 1, 2, :], g["d_b2"][one, :]).then_inc(s["w2_loaded"], 16)

        @block.vector
        def _(dve):
            dve.wait_ge(s["before_first"], 16 * layer + 16)
            dve.wait_ge(s["first_row_zero"], layer + 1)
            dve.wait_ge(s["one_row"], 2 * layer + 2)
            settle(dve, g["passed"])

            def norm_stats(p, u, ch):
                if isinstance(p, int) and p == 1 and u == 0:
                    dve.wait_ge(s["before_rest"], 16 * layer + 16)
                    settle(dve, g["passed"])
                for j in range(GROUP):
                    b = 2 * GROUP * p + (GROUP * u + j)
                    dve.bn_stats(stats[u][:, j, 0, :], z_all[:, b, 0:WD])
                    last = dve.bn_stats(stats[u][:, j, 1, :], before[:, b, :])
                ch.tag(last)
                ch.wait()
                settle(dve, g["passed"])
                for j in range(GROUP):
                    last = dve.bn_aggr(mv[u][:, j, :], stats[u][:, j, :, :].rearrange("p a b -> p (a b)"))
                last.then_inc(s["stats_ready"], 1)

            def normed(p, u):
                wait(dve, "rstd_ready", p, 2, u + 1)
                wait(dve, "turn_ready", p - 1, 2, u + 1)
                for j in range(GROUP):
                    b = 2 * GROUP * p + (GROUP * u + j)
                    dve.tensor_scalar(hn[u][:, j, 0:WD], z_all[:, b, 0:WD], mv[u][:, j, 0:1], rstd[u][:, j:j + 1],
                                      ALU.subtract, ALU.mult)
                    last = dve.tensor_scalar(hn[u][:, j, WD:P], before[:, b, :], mv[u][:, j, 0:1],
                                             rstd[u][:, j:j + 1], ALU.subtract, ALU.mult)
                last.then_inc(s["hn_ready"], 1)

            def take_hT(p, u):
                if isinstance(p, int) and p == 0 and u == 0:
                    dve.wait_ge(s["ln_loaded"], 32 * layer + 32)
                wait(dve, "turn_ready", p, 2, u + 1)
                wait(dve, "lin_ready", p - 1, 6, 3 * u + 3)
                dve.tensor_scalar(hT[u][:, :], turn[u][:, :], ln[:, 0:1], ln[:, 1:2], ALU.mult,
                                  ALU.add).then_inc(s["hT_ready"], 1)

            def gate_chunk(p, i):
                u, c, rows = i // 3, i % 3, CHUNKS[i % 3][1]
                if isinstance(p, int) and p == 0 and i == 0:
                    dve.wait_ge(s["b1_loaded"], 96 * layer + 96)
                wait(dve, "lin_ready", p, 6, i + 1)
                wait(dve, "gel_ready", p, 6, i + 1)
                wait(dve, "y_ready", p - 1, 2, u + 1)
                dve.scalar_tensor_tensor(out=gated[u][c][0:rows, :], in0=lin[i % 2][0:rows, :],
                                         scalar=b1[0:rows, 0, c:c + 1], in1=gel[i % 2][0:rows, :],
                                         op0=ALU.add, op1=ALU.mult).then_inc(s["gated_ready"], 1)

            def add_to_z(p, u):
                wait(dve, "y_ready", p, 2, u + 1)
                zs = z_all[:, bass.ds(2 * GROUP * p + GROUP * u, GROUP), :]
                dve.tensor_tensor(zs, zs, y[u][:, :, :], ALU.add).then_inc(s["z_done"], 1)

            def step(it):
                norm, after = it + 1, it - 1
                is_now, is_next, is_last = within(it, STEPS), within(norm, STEPS), within(after, STEPS)
                if is_now:
                    take_hT(it, 1)
                if is_next:
                    ch = Chain(dve, s["dve_stats"], n0 + norm, 2)
                    for u in range(2):
                        norm_stats(norm, u, ch)
                    ch.end()
                if is_now:
                    gate_chunk(it, 0)
                if is_last:
                    add_to_z(after, 1)
                if is_next:
                    normed(norm, 0)
                if is_now:
                    gate_chunk(it, 1)
                if is_next:
                    normed(norm, 1)
                if is_now:
                    gate_chunk(it, 2)
                    gate_chunk(it, 3)
                if is_next:
                    take_hT(norm, 0)
                if is_now:
                    gate_chunk(it, 4)
                    add_to_z(it, 0)
                    gate_chunk(it, 5)

            run_steps(dve, step, STEPS, 1, 1)

        @block.gpsimd
        def _(pool):
            pool.memset(before[0:1, :, :], 0.0).then_inc(s["first_row_zero"], 1)
            for u in range(2):
                pool.memset(gated[u][2][WD:P, :], 1.0).then_inc(s["one_row"], 1)
            with pool.Fori(0, STEPS) as it:
                n = n0 + it
                ch = Chain(pool, s["pool_var"], n, 2)
                for u in range(2):
                    pool.wait_ge(s["stats_ready"], n * 2 + u + 1)
                    settle(pool, g["passed"])
                    ch.tag(pool.tensor_scalar(var_eps[u][:, :], mv[u][:, :, 1], EPS, 1.0, ALU.add, ALU.mult))
                    ch.wait()
                    pool.tensor_tensor(rstd[u][:, :], var_eps[u][:, :], g["minus_half"][:, 0:GROUP],
                                       ALU.pow).then_inc(s["rstd_ready"], 1)
                ch.end()

        @block.scalar
        def _(act):
            act.wait_ge(s["b1_loaded"], 96 * layer + 96)
            settle(act, g["passed"])

            def step(it):
                for i in range(6):
                    c, rows = i % 3, CHUNKS[i % 3][1]
                    wait(act, "gate_ready", it, 6, i + 1)
                    chunk_before(act, "gated_ready", it, i)
                    act.activation(gel[i % 2][0:rows, :], gate[i % 2][0:rows, :], ACT.Gelu,
                                   bias=b1[0:rows, 1, c:c + 1]).then_inc(s["gel_ready"], 1)

            step(0)
            with act.Fori(1, STEPS) as it:
                step(it)

        @block.tensor
        def _(pe):
            def turn_tile(p, u):
                wait(pe, "hn_ready", p, 2, u + 1)
                wait(pe, "hT_ready", p - 1, 2, u + 1)
                for j in range(GROUP):
                    last = pe.transpose(turn[u][:, j * P:(j + 1) * P], hn[u][:, j, :], ident)
                last.then_inc(s["turn_ready"], 1)

            def project_chunk(p, i):
                u, c, (at, rows) = i // 3, i % 3, CHUNKS[i % 3]
                if isinstance(p, int) and p == 0 and i == 0:
                    pe.wait_ge(s["w1_loaded"], 16 * layer + 16)
                wait(pe, "hT_ready", p, 2, u + 1)
                chunk_before(pe, "gel_ready", p, i)
                pe.matmul(gate[i % 2][0:rows, :], w1[:, HID + at:HID + at + rows], hT[u][:, :], start=True,
                          stop=True).then_inc(s["gate_ready"], 1)
                chunk_before(pe, "gated_ready", p, i)
                pe.matmul(lin[i % 2][0:rows, :], w1[:, at:at + rows], hT[u][:, :], start=True,
                          stop=True).then_inc(s["lin_ready"], 1)

            def project_back(p, u):
                if isinstance(p, int) and p == 0 and u == 0:
                    pe.wait_ge(s["w2_loaded"], 64 * layer + 64)
                wait(pe, "gated_ready", p, 6, 3 * u + 3)
                wait(pe, "z_done", p - 1, 2, u + 1)
                for j in range(GROUP):
                    for c, (at, rows) in enumerate(CHUNKS):
                        rows = rows + 1 if c == 2 else rows
                        last = pe.matmul(y[u][:, j, :], gated[u][c][0:rows, j * P:(j + 1) * P], w2[0:rows, c, :],
                                         start=(c == 0), stop=(c == 2))
                last.then_inc(s["y_ready"], 1)

            def step(it):
                norm, after = it + 1, it - 1
                is_now, is_next, is_last = within(it, STEPS), within(norm, STEPS), within(after, STEPS)
                if is_now:
                    project_chunk(it, 0)
                if is_last:
                    project_back(after, 1)
                if is_now:
                    project_chunk(it, 1)
                    project_chunk(it, 2)
                    project_chunk(it, 3)
                if is_next:
                    turn_tile(norm, 0)
                    turn_tile(norm, 1)
                if is_now:
                    project_chunk(it, 4)
                    project_back(it, 0)
                    project_chunk(it, 5)

            run_steps(pe, step, STEPS, 1, 1)


def expert_stage(nc, g, out):
    with ExitStack() as ctx:
        def sb(name, shape, dt):
            return ctx.enter_context(nc.sbuf_tensor("x_" + name, shape, dt))

        def ps(name, shape, dt):
            return ctx.enter_context(nc.psum_tensor("x_" + name, shape, dt))

        def sem(name):
            return ctx.enter_context(nc.semaphore("x_" + name))

        x_all, z_all, cf = g["x"], g["z"], g["cf"]
        ident, iota = cf[:, CF["ident"]], cf[:, CF["iota"]]
        N = GROUP * P
        E, ALL = EXPERTS, EXPERTS + 1
        TILES = NSEQ // GROUP
        HALF = NSEQ // 2
        LAG = 2
        w1, w2, b1, b2 = g["e_w1"], g["e_w2"], g["e_b1"], g["e_b2"]
        zT_all = g["ctx"]
        logits = [sb(f"logits{k}", [P, HALF, E], F32) for k in range(2)]
        top = [sb(f"top{k}", [P, HALF], F32) for k in range(2)]
        less = [sb(f"less{k}", [P, HALF, E], F32) for k in range(2)]
        raised = [sb(f"raised{k}", [P, HALF, E], F32) for k in range(2)]
        total = [sb(f"total{k}", [P, HALF], F32) for k in range(2)]
        inv_total = [sb(f"inv_total{k}", [P, HALF], F32) for k in range(2)]
        prob = [sb(f"prob{k}", [P, HALF, E], F32) for k in range(2)]
        sorted8 = [sb(f"sorted{k}", [P, HALF, 8], F32) for k in range(2)]
        order = [sb(f"order{k}", [P, HALF, 8], U32) for k in range(2)]
        orderf = [sb(f"orderf{k}", [P, HALF, 8], F32) for k in range(2)]
        is_pick = [[sb(f"is_pick{k}{r}", [P, HALF, E], F32) for r in range(2)] for k in range(2)]
        picked = [sb(f"picked{k}", [P, HALF, E], F32) for k in range(2)]
        weight = sb("weight", [P, NSEQ, ALL], F32)
        weightT_all = sb("weightT_all", [ALL, NSEQ, P], F32)
        weightT = sb("weightT", [ALL, GROUP, P], F32)
        hg = [sb(f"hg{i}", [P, N], F32) for i in range(3)]
        turn = [ps(f"turn{i}", [P, 512], F32) for i in range(2)]
        hid = [ps(f"hid{i}", [P, N], F32) for i in range(3)]
        y = [ps(f"y{i}", [P, GROUP, P], F32) for i in range(3)]

        turn_ready, zT_ready, logits_ready, logits_read = (sem("turn_ready"), sem("zT_ready"), sem("logits_ready"),
                                                           sem("logits_read"))
        less_ready, raised_ready, weight_ready = sem("less_ready"), sem("raised_ready"), sem("weight_ready")
        weightT_psum, weightT_all_ready, weightT_ready = (sem("weightT_psum"), sem("weightT_all_ready"),
                                                          sem("weightT_ready"))
        hid_ready, hg_ready, y_ready, y_used = sem("hid_ready"), sem("hg_ready"), sem("y_ready"), sem("y_used")
        stored, routed, shared_one = sem("stored"), sem("routed"), sem("shared_one")
        block = ctx.enter_context(nc.Block())

        @block.vector
        def _(dve):
            ch = Chain(dve, routed, 0, 20)
            for half in range(2):
                dve.wait_ge(logits_ready, half + 1)
                seen = y[half][:, :, :].rearrange("p a b -> p (a b)")[:, 0:HALF * E].rearrange("p (n e) -> p n e", e=E)
                each = lambda ap: ap.unsqueeze(2).broadcast_to([P, HALF, E])
                ins = dve.tensor_tensor(logits[half][:, :, :], seen,
                                        g["e_gate_b"][:, :].unsqueeze(1).broadcast_to([P, HALF, E]), ALU.add)
                ins.then_inc(logits_read, 1)
                dve.wait_ge(logits_read, half + 1)
                ch.tag(dve.tensor_reduce(top[half][:, :], logits[half][:, :, :], AX.X, ALU.max))
                ch.wait()
                dve.tensor_tensor(less[half][:, :, :], logits[half][:, :, :], each(top[half][:, :]),
                                  ALU.subtract).then_inc(less_ready, 1)
                dve.wait_ge(raised_ready, half + 1)
                ch.tag(dve.tensor_reduce(total[half][:, :], raised[half][:, :, :], AX.X, ALU.add))
                ch.wait()
                ch.tag(dve.reciprocal(inv_total[half][:, :], total[half][:, :]))
                ch.wait()
                ch.tag(dve.tensor_tensor(prob[half][:, :, :], raised[half][:, :, :], each(inv_total[half][:, :]),
                                         ALU.mult))
                ch.wait()
                for n in range(HALF):
                    last = dve.max(sorted8[half][:, n, :], prob[half][:, n, :])
                ch.tag(last)
                ch.wait()
                for n in range(HALF):
                    last = dve.max_index(order[half][:, n, :], sorted8[half][:, n, :], prob[half][:, n, :])
                ch.tag(last)
                ch.wait()
                ch.tag(dve.tensor_copy(orderf[half][:, :, :], order[half][:, :, :]))
                ch.wait()
                for r in range(2):
                    ch.tag(dve.tensor_tensor(is_pick[half][r][:, :, :],
                                             iota.unsqueeze(1).broadcast_to([P, HALF, E]),
                                             each(orderf[half][:, :, r]), ALU.is_equal))
                ch.wait()
                ch.tag(dve.tensor_tensor(picked[half][:, :, :], is_pick[half][0][:, :, :],
                                         is_pick[half][1][:, :, :], ALU.add))
                ch.wait()
                dve.tensor_tensor(weight[:, HALF * half:HALF * (half + 1), 0:E], picked[half][:, :, :],
                                  prob[half][:, :, :], ALU.mult).then_inc(weight_ready, 1)
            ch.end()
            dve.sem_inc(y_used, 3)
            dve.wait_ge(weight_ready, 2)
            dve.wait_ge(shared_one, 1)
            with dve.Fori(0, TILES) as t:
                for e in range(ALL):
                    dve.wait_ge(y_ready, t * ALL + e + 1)
                    if e:
                        dve.wait_ge(y_used, t * ALL + e + 3)
                    if e < E:
                        for j in range(GROUP):
                            x = x_all[:, GROUP * t + j, :]
                            last = dve.scalar_tensor_tensor(out=x, in0=y[e % 3][:, j, :],
                                                            scalar=weight[:, GROUP * t + j, e:e + 1], in1=x,
                                                            op0=ALU.mult, op1=ALU.add)
                    else:
                        x = x_all[:, bass.ds(GROUP * t, GROUP), :]
                        last = dve.tensor_tensor(x, y[e % 3][:, :, :], x, ALU.add)
                    last.then_inc(y_used, 1)

        @block.gpsimd
        def _(pool):
            pool.memset(weight[:, :, E:ALL], 1.0).then_inc(shared_one, 1)

        @block.sync
        def _(sp):
            with sp.Fori(0, TILES) as t:
                sp.wait_ge(y_used, t * ALL + ALL + 3)
                of = bass.ds(GROUP * t, GROUP)
                sp.dma_start(out[of, :, :].rearrange("b t d -> t b d"), x_all[:, of, :]).then_inc(stored, 16)
            sp.wait_ge(stored, 16 * TILES)

        @block.scalar
        def _(act):
            for half in range(2):
                for i in range(TILES // 2 * half, TILES // 2 * (half + 1)):
                    act.wait_ge(turn_ready, i + 1)
                    act.activation(zT_all[:, GROUP * i:GROUP * (i + 1), :].rearrange("p n t -> p (n t)"),
                                   turn[i % 2][:, :], ACT.Copy).then_inc(zT_ready, 1)
            for half in range(2):
                act.wait_ge(less_ready, half + 1)
                act.activation(raised[half][:, :, :], less[half][:, :, :], ACT.Exp).then_inc(raised_ready, 1)
            for i in range(TILES):
                act.wait_ge(weightT_psum, i + 1)
                act.activation(weightT_all[:, GROUP * i:GROUP * (i + 1), :].rearrange("p n t -> p (n t)"),
                               turn[i % 2][0:ALL, :], ACT.Copy).then_inc(weightT_all_ready, 1)
            act.wait_ge(weightT_all_ready, TILES)
            with act.Fori(0, TILES) as t:
                for e in range(ALL):
                    act.wait_ge(hid_ready, t * ALL + e + 1)
                    act.activation(hg[e % 3][:, :], hid[e % 3][:, :], ACT.Gelu,
                                   bias=b1[:, e:e + 1]).then_inc(hg_ready, 1)
                    if e == 4:
                        act.activation(weightT[:, :, :], weightT_all[:, bass.ds(GROUP * t, GROUP), :],
                                       ACT.Copy).then_inc(weightT_ready, 1)

        @block.tensor
        def _(pe):
            def route(i):
                half = i // (TILES // 2)
                pe.wait_ge(zT_ready, i + 1)
                for n in range(GROUP * i, GROUP * (i + 1)):
                    at = E * (n - HALF * half)
                    last = pe.matmul(y[half][:, at // P, at % P:at % P + E], zT_all[:, n, :], g["e_gate_w"][:, :],
                                     start=True, stop=True)
                if i % (TILES // 2) == TILES // 2 - 1:
                    last.then_inc(logits_ready, 1)

            for i in range(TILES):
                if i >= 2:
                    pe.wait_ge(zT_ready, i - 1)
                for j in range(GROUP):
                    last = pe.transpose(turn[i % 2][:, j * P:(j + 1) * P], z_all[:, GROUP * i + j, :], ident)
                last.then_inc(turn_ready, 1)
                if i:
                    route(i - 1)
            route(TILES - 1)
            for i in range(TILES):
                if i % (TILES // 2) == 0:
                    pe.wait_ge(weight_ready, i // (TILES // 2) + 1)
                    pe.wait_ge(shared_one, 1)
                if i >= 2:
                    pe.wait_ge(weightT_all_ready, i - 1)
                for j in range(GROUP):
                    last = pe.transpose(turn[i % 2][0:ALL, j * P:(j + 1) * P], weight[:, GROUP * i + j, :], ident)
                last.then_inc(weightT_psum, 1)

            def hidden(t, e):
                pe.matmul(hid[e % 3][:, :], w1[:, e, :], zT_all[:, bass.ds(GROUP * t, GROUP), :], start=True,
                          stop=True).then_inc(hid_ready, 1)

            def project(t, e):
                pe.wait_ge(hg_ready, t * ALL + e + 1)
                pe.wait_ge(y_used, t * ALL + e + 1)
                if e == E:
                    pe.wait_ge(weightT_ready, t + 1)
                for j in range(GROUP):
                    if e == E:
                        pe.matmul(y[e % 3][:, j, :], weightT[:, j, :], b2[:, :], start=True, stop=False)
                    last = pe.matmul(y[e % 3][:, j, :], hg[e % 3][:, j * P:(j + 1) * P], w2[:, e, :],
                                     start=(e < E), stop=True)
                last.then_inc(y_ready, 1)

            def step(t):
                for e in range(ALL):
                    if within(t, TILES):
                        hidden(t, e)
                    if e >= LAG:
                        if within(t, TILES):
                            project(t, e - LAG)
                    elif within(t - 1, TILES):
                        project(t - 1, ALL + e - LAG)

            run_steps(pe, step, TILES, 0, 1)


def program(nc, d, out):
    with ExitStack() as ctx:
        def sb(name, shape, dt=F32):
            return ctx.enter_context(nc.sbuf_tensor(name, shape, dt))

        def sem(name):
            return ctx.enter_context(nc.semaphore(name))

        g = {
            "x": sb("x_all", [P, NSEQ, P]), "z": sb("z_all", [P, NSEQ, P]), "ctx": sb("ctx_all", [P, NSEQ, P]),
            "cf": sb("consts_f32", [P, CF_COLS]), "cb": sb("consts_bf16", [P, CB_COLS], BF16),
            "ones_row": sb("ones_row", [1, P]), "minus_half": sb("minus_half", [P, 16]),
            "w_n1": sb("w_n1", [P, 5 * P]), "w_n2": sb("w_n2", [P, 4 * P]),
            "row_n1": sb("row_n1", [P, 2 * P]), "row_n2": sb("row_n2", [P, 4 * P]), "cols": sb("cols", [P, 3]),
            "e_w1": sb("e_w1", [P, EXPERTS + 1, P]), "e_w2": sb("e_w2", [P, EXPERTS + 1, P]),
            "e_b1": sb("e_b1", [P, EXPERTS + 1]), "e_b2": sb("e_b2", [EXPERTS + 1, P]),
            "e_gate_w": sb("e_gate_w", [P, EXPERTS]), "e_gate_b": sb("e_gate_b", [P, EXPERTS]),
            "passed": sem("passed"),
            "neg_mask": sb("neg_mask", [P, NSEQ, P], BF16), "neg_maskT": sb("neg_maskT", [P, NSEQ, P], BF16),
            "q_scale": sb("q_scale", [P, NSEQ, 1]), "d_mask": d["mask"],
            "d_wqkv": d["L0_ffn_wqkv"], "d_wo": d["L0_ffn_wo"], "d_qs": d["L0_ffn_q_scale"],
            "d_ks": d["L0_ffn_k_scale"], "d_w1": d["L0_ffn_w1"], "d_w2": d["L0_ffn_w2"], "d_b1": d["L0_ffn_b1"],
            "d_b2": d["L0_ffn_b2"], "d_ln_g": d["L0_ffn_ln_g"], "d_ln_b": d["L0_ffn_ln_b"],
        }
        wide = {n: sem(n) for n in WIDE_SEMS}
        glu = {n: sem("m_" + n) for n in GLU_SEMS}
        for name in ("first_quarter", "other_quarters", "tables_loaded", "rest_loaded", "set_up"):
            g[name] = sem(name)

        col = lambda name: d[name].rearrange("(p a) -> p a", a=1)
        row = lambda name: d[name].rearrange("(a p) -> a p", a=1)
        tables = [(g["cf"][:, :], d["consts_f32"]), (g["w_n1"][:, 0:3 * P], d["L0_xattn_WqkvT"]),
                  (g["cb"][:, :], d["consts_bf16"].bitcast(BF16)),
                  (g["w_n1"][:, 3 * P:4 * P], d["L0_xattn_WoutT"]),
                  (g["w_n1"][:, 4 * P:5 * P], d["L0_xattn_WgateT"]),
                  (g["row_n1"][:, 0:P], row("L0_xattn_b_out").broadcast_to([P, P])),
                  (g["row_n1"][:, P:2 * P], row("L0_xattn_b_gate").broadcast_to([P, P]))]
        tables += [(g["cols"][:, k:k + 1], col(name))
                   for k, name in enumerate(("L0_xattn_gamma", "L0_xattn_beta", "L0_xattn_b_out"))]
        g["tables_count"] = 16 * len(tables)
        rest = []
        for k, name in enumerate("qkvo"):
            rest += [(g["w_n2"][:, k * P:(k + 1) * P], d[f"L1_xattn_W{name}T"]),
                     (g["row_n2"][:, k * P:(k + 1) * P], row(f"L1_xattn_b{name}").broadcast_to([P, P]))]
        rest += [(g["e_w1"][:, 0:EXPERTS, :], d["L1_ffn_w1"].rearrange("e d f -> d e f")),
                 (g["e_w1"][:, EXPERTS, :], d["L1_ffn_sw1"]),
                 (g["e_w2"][:, 0:EXPERTS, :], d["L1_ffn_w2"].rearrange("e d f -> d e f")),
                 (g["e_w2"][:, EXPERTS, :], d["L1_ffn_sw2"]),
                 (g["e_b1"][:, 0:EXPERTS], d["L1_ffn_b1T"]), (g["e_b1"][:, EXPERTS:EXPERTS + 1], col("L1_ffn_sb1")),
                 (g["e_b2"][0:EXPERTS, :], d["L1_ffn_b2"]), (g["e_b2"][EXPERTS:EXPERTS + 1, :], row("L1_ffn_sb2")),
                 (g["e_gate_w"][:, :], d["L1_ffn_gate_w"]), (g["e_gate_b"][:, :], row("L1_ffn_gate_b").broadcast_to([P, EXPERTS]))]

        def load_all(sp):
            quarters = [slice(NSEQ // 4 * k, NSEQ // 4 * (k + 1)) for k in range(4)]

            def load_quarter(seqs, sem):
                for name, source in (("x", "x"), ("ctx", "ctx_1024")):
                    sp.dma_start(g[name][:, seqs, :], d[source][seqs, :, :].rearrange("b t d -> t b d")).then_inc(sem, 16)

            load_quarter(quarters[0], g["first_quarter"])
            for dst, src in tables:
                sp.dma_start(dst, src).then_inc(g["tables_loaded"], 16)
            for seqs in quarters[1:]:
                load_quarter(seqs, g["other_quarters"])
            for dst, src in rest:
                sp.dma_start(dst, src).then_inc(g["rest_loaded"], 16)
            sp.wait_ge(g["rest_loaded"], 16 * len(rest))

        g["load_all"] = load_all
        narrow_stage(nc, g, True)
        with nc.Fori(0, LAYERS) as layer:
            wide_stage(nc, g, layer, wide)
            glu_stage(nc, g, layer, glu)
        mask_stage(nc, g)
        narrow_stage(nc, g, False)
        expert_stage(nc, g, out)


def constants():
    f = np.float32
    cf = np.zeros((P, CF_COLS), f)
    cb = np.zeros((P, CB_COLS), f)
    cf[:, CF["ident"]] = np.eye(P)
    cb[:, CB["ident"]] = np.eye(P)
    t = np.arange(P, dtype=f)
    half = ND // 2
    freqs = t[:, None] * (f(1) / f(10000) ** (np.arange(0, ND, 2, dtype=f) / f(ND)))[None, :]
    c, s = np.cos(freqs).astype(f), np.sin(freqs).astype(f)
    c, s = np.tile(np.concatenate([c, c], 1), (1, NH)), np.tile(np.concatenate([-s, s], 1), (1, NH))
    cf[:, CF["rope_c"]] = np.concatenate([c * f(ND ** -0.5), c], 1)
    cf[:, CF["rope_s"]] = np.concatenate([s * f(ND ** -0.5), s], 1)
    idx = np.arange(0, WD, 2, dtype=f)
    freqs = t[:, None] * (f(1) / f(10000) ** (idx / f(WD)))[None, :]
    base = (idx + f(0.4 * WD)) / f(1.4 * WD)
    scale = base[None, :] ** ((t - P // 2) / f(32))[:, None]
    c, s = np.cos(freqs).astype(f), np.sin(freqs).astype(f)
    both = lambda a, b: np.concatenate([a, b], 1)
    cf[:, CF["xpos_c"]] = both(both(c * scale, c * scale) * f(8), both(c / scale, c / scale))
    cf[:, CF["xpos_s"]] = both(both(-s * scale, s * scale) * f(8), both(-s / scale, s / scale))
    cf[:, CF["iota"]] = np.arange(EXPERTS)
    dist = np.abs(t[None, :] - t[:, None])
    rest = (np.exp(-dist * f(0.1)) - dist * f(0.05)).astype(f)
    for n in range(3):
        term = (rest.view(np.uint32) & np.uint32(0xFFFF0000)).view(f)
        cb[:, CB["bias"].start + n * P:CB["bias"].start + (n + 1) * P] = term
        rest = rest - term
    i, j = np.arange(P)[:, None], np.arange(P)[None, :]
    band = np.where((i < j) | (i > j + 64), f(-2.0 ** 100), f(0))
    cb[:, CB["band"]] = band
    cb[:, CB["band_t"]] = band.T
    for name, heads in (("pick_n", NH), ("pick_w", WH)):
        pick = np.zeros((P, heads, P), f)
        for h in range(heads):
            pick[[h, heads + h], h, :] = 1
        cb[:, CB[name]] = pick.reshape(P, heads * P)
    return cf, (cb.view(np.uint32) >> 16).astype(np.uint16)


def kernel(**inputs):
    from concourse import bacc
    from concourse.bass_utils import run_bass_kernel_spmd

    arrays = {}
    for name, a in inputs.items():
        a = np.asarray(a)
        if name == "L0_xattn_Wqkv" or name in ("L0_xattn_Wout", "L0_xattn_Wgate") or \
                name.startswith("L1_xattn_W") or name == "L1_ffn_b1":
            name, a = name + "T", a.T
        if name.startswith("mask"):
            name = "mask"
        arrays[name] = np.ascontiguousarray(a)
    arrays["consts_f32"], arrays["consts_bf16"] = constants()

    nc = bacc.Bacc("TRN2", target_bir_lowering=False, num_devices=1)
    d = {name: nc.dram_tensor(f"in_{name}", a.shape, mybir.dt.from_np(a.dtype), kind="ExternalInput").ap()
         for name, a in arrays.items()}
    out = nc.dram_tensor("out", (NSEQ, P, P), F32, kind="ExternalOutput").ap()
    program(nc, d, out)
    result = run_bass_kernel_spmd(nc, [{f"in_{name}": a for name, a in arrays.items()}], core_ids=[0])
    return result.results[0]["out"]
```
